# Optimizing a Trainium2 kernel written in Bass

```python
import numpy as np
import jax
import jax.numpy as jnp

def _softmax(x, axis=-1):
    return jax.nn.softmax(x, axis=axis)

def _gelu(x):
    return jax.nn.gelu(x, approximate=True)

def _silu(x):
    return jax.nn.silu(x)

def _sigmoid(x):
    return jax.nn.sigmoid(x)

def _layernorm(x, axis=-1, eps=1e-05):
    m = jnp.mean(x, axis=axis, keepdims=True)
    v = jnp.var(x, axis=axis, keepdims=True)
    return (x - m) / jnp.sqrt(v + eps)

def _scatter_add(tgt, idx, src, axis=0):
    return tgt.at[idx].add(src)

def _segment_sum(src, seg, n):
    return jax.ops.segment_sum(src, seg, n)
kernel_name = 'mk_perceiver_d2_seqx_r4_8a4d59'

def setup_inputs(seed: int=0):
    np.random.seed(seed)
    _w = jnp.asarray

    def _rec_inputs():
        import jax
        import jax.numpy as jnp
        _rk = jax.random.key(seed)
        x = 7.22e-05 + 1 * jax.random.normal(jax.random.fold_in(_rk, 1), (64, 32, 256), jnp.float32)
        _lenS = 32 - jax.random.randint(jax.random.fold_in(_rk, 7), (64,), 0, max(1, 32 // 4) + 1, jnp.int32)
        _lenS2 = 257 - jax.random.randint(jax.random.fold_in(_rk, 8), (64,), 0, max(1, 257 // 4) + 1, jnp.int32)
        _ctx_1024P = jax.random.normal(jax.random.fold_in(_rk, 11), (64, 16, 256), jnp.float32)
        _ctx_1024c = jax.random.dirichlet(jax.random.fold_in(_rk, 511), 0.3 * jnp.ones((16,), jnp.float32), (64, 257))
        _ctx_1024t = jnp.einsum('bsk,bkd->bsd', _ctx_1024c, _ctx_1024P)
        _ctx_1024t = _ctx_1024t * jax.lax.rsqrt(jnp.mean(jnp.square(_ctx_1024t)) + 1e-12) * 0.953939
        ctx_1024 = 4.13588e-05 + 0.999923 * (_ctx_1024t + 0.3 * jax.random.normal(jax.random.fold_in(_rk, 611), (64, 257, 256), jnp.float32))
        return (x, ctx_1024)
    x, ctx_1024 = _rec_inputs()

    def _L0_xattn_setup():
        import jax, jax.numpy as jnp
        import numpy as np
        D = 256
        H = 16
        DH = D // H
        key = jax.random.key(seed)
        ks = jax.random.split(key, 11)
        B, T = (4, 512)
        s = 0.02
        return {'q': jax.random.normal(ks[0], (B, T, D), jnp.float32), 'k': jax.random.normal(ks[1], (B, T, D), jnp.float32), 'v': jax.random.normal(ks[2], (B, T, D), jnp.float32), 'Wq': jax.random.normal(ks[3], (D, D), jnp.float32) * s, 'b_q': jax.random.normal(ks[4], (D,), jnp.float32) * s, 'Wk': jax.random.normal(ks[5], (D, D), jnp.float32) * s, 'b_k': jax.random.normal(ks[6], (D,), jnp.float32) * s, 'Wv': jax.random.normal(ks[7], (D, D), jnp.float32) * s, 'b_v': jax.random.normal(ks[8], (D,), jnp.float32) * s, 'Wo': jax.random.normal(ks[9], (D, D), jnp.float32) * s, 'b_o': jax.random.normal(ks[10], (D,), jnp.float32) * s}
    _L0_xattn_all = _L0_xattn_setup()
    _L0_xattn_in = {k: v for k, v in _L0_xattn_all.items() if k in ('Wq', 'b_q', 'Wk', 'b_k', 'Wv', 'b_v', 'Wo', 'b_o')}
    del _L0_xattn_all

    def _L0_attn_setup():
        import jax, jax.numpy as jnp
        import numpy as np
        import math
        N_EMBD = 256
        NUM_HEADS = 16
        HEAD_DIM = N_EMBD // NUM_HEADS

        def alibi_slopes(num_heads):
            x = (2 ** 8) ** (1.0 / num_heads)
            return jnp.array([1.0 / x ** (i + 1) for i in range(num_heads)], dtype=jnp.float32)
        key = jax.random.key(seed)
        k1, k2 = jax.random.split(key)
        x = jax.random.normal(k1, (2, 512, N_EMBD), dtype=jnp.float32)
        W_kqv = jax.random.normal(k2, (3 * N_EMBD, N_EMBD), dtype=jnp.float32) * (1.0 / math.sqrt(N_EMBD))
        return {'x': x, 'W_kqv': W_kqv}
    _L0_attn_all = _L0_attn_setup()
    _L0_attn_in = {k: v for k, v in _L0_attn_all.items() if k in ('W_kqv',)}
    del _L0_attn_all

    def _L0_ffn_setup():
        import jax, jax.numpy as jnp
        import numpy as np
        TOP_K = 8
        key = jax.random.key(seed)
        k1, k2, k3, k4, k5 = jax.random.split(key, 5)
        B, S, D, F, E = (2, 512, 256, 192, 64)
        return {'hidden_states': jax.random.normal(k1, (B, S, D), dtype=jnp.float32), 'gate_w': jax.random.normal(k2, (E, D), dtype=jnp.float32) * 0.02, 'w_gate': jax.random.normal(k3, (E, F, D), dtype=jnp.float32) * 0.02, 'w_up': jax.random.normal(k4, (E, F, D), dtype=jnp.float32) * 0.02, 'w_down': jax.random.normal(k5, (E, D, F), dtype=jnp.float32) * 0.02}
    _L0_ffn_all = _L0_ffn_setup()
    _L0_ffn_in = {k: v for k, v in _L0_ffn_all.items() if k in ('gate_w', 'w_gate', 'w_up', 'w_down')}
    del _L0_ffn_all

    def _L1_xattn_setup():
        import jax, jax.numpy as jnp
        import numpy as np
        DIM = 256
        DIM_HEAD = 64
        HEADS = 16
        INNER = DIM_HEAD * HEADS
        EPS = 1e-05

        def layer_norm(x, g, b):
            m = jnp.mean(x, axis=-1, keepdims=True)
            v = jnp.mean(jnp.square(x - m), axis=-1, keepdims=True)
            return (x - m) * jax.lax.rsqrt(v + EPS) * g + b
        key = jax.random.key(seed)
        ks = jax.random.split(key, 8)
        B, N_IMG, N_LAT = (4, 1024, 128)
        std = 1.0 / np.sqrt(DIM)
        return {'image_embeds': jax.random.normal(ks[0], (B, N_IMG, DIM), dtype=jnp.float32), 'latents': jax.random.normal(ks[1], (B, N_LAT, DIM), dtype=jnp.float32), 'ln1_g': jnp.ones((DIM,), jnp.float32), 'ln1_b': jnp.zeros((DIM,), jnp.float32), 'ln2_g': jnp.ones((DIM,), jnp.float32), 'ln2_b': jnp.zeros((DIM,), jnp.float32), 'Wq': jax.random.normal(ks[2], (DIM, INNER), dtype=jnp.float32) * std, 'Wkv': jax.random.normal(ks[3], (DIM, 2 * INNER), dtype=jnp.float32) * std, 'Wo': jax.random.normal(ks[4], (INNER, DIM), dtype=jnp.float32) * std}
    _L1_xattn_all = _L1_xattn_setup()
    _L1_xattn_in = {k: v for k, v in _L1_xattn_all.items() if k in ('ln1_g', 'ln1_b', 'ln2_g', 'ln2_b', 'Wq', 'Wkv', 'Wo')}
    del _L1_xattn_all

    def _L1_attn_setup():
        import jax, jax.numpy as jnp
        import numpy as np
        B_SZ, SEQ = (2, 512)
        D_MODEL, D_STATE, D_CONV = (256, 16, 4)
        D_INPUT, D_OUTPUT = (256, 256)
        D_INNER = 2 * D_MODEL
        DT_RANK = D_MODEL // 16
        key = jax.random.key(seed)
        ks = jax.random.split(key, 8)

        def rn(k, shape, scale):
            return (jax.random.normal(k, shape) * scale).astype(jnp.float32)
        return {'x': rn(ks[0], (B_SZ, SEQ, D_INPUT), 1.0), 'fc1_w': rn(ks[1], (D_MODEL, D_INPUT), D_INPUT ** (-0.5)), 'fc1_b': jnp.zeros((D_MODEL,), jnp.float32), 'in_proj_w': rn(ks[2], (2 * D_INNER, D_MODEL), D_MODEL ** (-0.5)), 'conv_w': rn(ks[3], (D_INNER, D_CONV), D_CONV ** (-0.5)), 'conv_b': jnp.zeros((D_INNER,), jnp.float32), 'x_proj_w': rn(ks[4], (DT_RANK + 2 * D_STATE, D_INNER), D_INNER ** (-0.5)), 'dt_proj_w': rn(ks[5], (D_INNER, DT_RANK), DT_RANK ** (-0.5)), 'dt_proj_b': jnp.full((D_INNER,), -4.6, jnp.float32), 'A_log': jnp.log(jnp.broadcast_to(jnp.arange(1, D_STATE + 1, dtype=jnp.float32), (D_INNER, D_STATE))), 'D': jnp.ones((D_INNER,), jnp.float32), 'out_proj_w': rn(ks[6], (D_MODEL, D_INNER), D_INNER ** (-0.5)), 'fc2_w': rn(ks[7], (D_OUTPUT, D_MODEL), D_MODEL ** (-0.5)), 'fc2_b': jnp.zeros((D_OUTPUT,), jnp.float32)}
    _L1_attn_all = _L1_attn_setup()
    _L1_attn_in = {k: v for k, v in _L1_attn_all.items() if k in ('fc1_w', 'fc1_b', 'in_proj_w', 'conv_w', 'conv_b', 'x_proj_w', 'dt_proj_w', 'dt_proj_b', 'A_log', 'D', 'out_proj_w', 'fc2_w', 'fc2_b')}
    del _L1_attn_all

    def _L1_ffn_setup():
        import jax, jax.numpy as jnp
        import numpy as np
        DIM = 256
        HID = 128
        N_EXPERTS = 16
        TOP_K = 4
        key = jax.random.key(seed)
        ks = jax.random.split(key, 8)
        s = 0.02
        x = jax.random.normal(ks[0], (2, 256, DIM), dtype=jnp.float32)
        gate_w = jax.random.normal(ks[1], (N_EXPERTS, DIM), dtype=jnp.float32) * s
        w1 = jax.random.normal(ks[2], (N_EXPERTS, HID, DIM), dtype=jnp.float32) * s
        w3 = jax.random.normal(ks[3], (N_EXPERTS, HID, DIM), dtype=jnp.float32) * s
        w2 = jax.random.normal(ks[4], (N_EXPERTS, DIM, HID), dtype=jnp.float32) * s
        sw1 = jax.random.normal(ks[5], (HID, DIM), dtype=jnp.float32) * s
        sw3 = jax.random.normal(ks[6], (HID, DIM), dtype=jnp.float32) * s
        sw2 = jax.random.normal(ks[7], (DIM, HID), dtype=jnp.float32) * s
        return {'x': x, 'gate_w': gate_w, 'w1': w1, 'w3': w3, 'w2': w2, 'sw1': sw1, 'sw3': sw3, 'sw2': sw2}
    _L1_ffn_all = _L1_ffn_setup()
    _L1_ffn_in = {k: v for k, v in _L1_ffn_all.items() if k in ('gate_w', 'w1', 'w3', 'w2', 'sw1', 'sw3', 'sw2')}
    del _L1_ffn_all
    return {'x': x, 'ctx_1024': ctx_1024, 'L0_xattn_Wq': _L0_xattn_in['Wq'], 'L0_xattn_b_q': _L0_xattn_in['b_q'], 'L0_xattn_Wk': _L0_xattn_in['Wk'], 'L0_xattn_b_k': _L0_xattn_in['b_k'], 'L0_xattn_Wv': _L0_xattn_in['Wv'], 'L0_xattn_b_v': _L0_xattn_in['b_v'], 'L0_xattn_Wo': _L0_xattn_in['Wo'], 'L0_xattn_b_o': _L0_xattn_in['b_o'], 'L0_attn_W_kqv': _L0_attn_in['W_kqv'], 'L0_ffn_gate_w': _L0_ffn_in['gate_w'], 'L0_ffn_w_gate': _L0_ffn_in['w_gate'], 'L0_ffn_w_up': _L0_ffn_in['w_up'], 'L0_ffn_w_down': _L0_ffn_in['w_down'], 'L1_xattn_ln1_g': _L1_xattn_in['ln1_g'], 'L1_xattn_ln1_b': _L1_xattn_in['ln1_b'], 'L1_xattn_ln2_g': _L1_xattn_in['ln2_g'], 'L1_xattn_ln2_b': _L1_xattn_in['ln2_b'], 'L1_xattn_Wq': _L1_xattn_in['Wq'], 'L1_xattn_Wkv': _L1_xattn_in['Wkv'], 'L1_xattn_Wo': _L1_xattn_in['Wo'], 'L1_attn_fc1_w': _L1_attn_in['fc1_w'], 'L1_attn_fc1_b': _L1_attn_in['fc1_b'], 'L1_attn_in_proj_w': _L1_attn_in['in_proj_w'], 'L1_attn_conv_w': _L1_attn_in['conv_w'], 'L1_attn_conv_b': _L1_attn_in['conv_b'], 'L1_attn_x_proj_w': _L1_attn_in['x_proj_w'], 'L1_attn_dt_proj_w': _L1_attn_in['dt_proj_w'], 'L1_attn_dt_proj_b': _L1_attn_in['dt_proj_b'], 'L1_attn_A_log': _L1_attn_in['A_log'], 'L1_attn_D': _L1_attn_in['D'], 'L1_attn_out_proj_w': _L1_attn_in['out_proj_w'], 'L1_attn_fc2_w': _L1_attn_in['fc2_w'], 'L1_attn_fc2_b': _L1_attn_in['fc2_b'], 'L1_ffn_gate_w': _L1_ffn_in['gate_w'], 'L1_ffn_w1': _L1_ffn_in['w1'], 'L1_ffn_w3': _L1_ffn_in['w3'], 'L1_ffn_w2': _L1_ffn_in['w2'], 'L1_ffn_sw1': _L1_ffn_in['sw1'], 'L1_ffn_sw3': _L1_ffn_in['sw3'], 'L1_ffn_sw2': _L1_ffn_in['sw2']}

def reference(x, ctx_1024, L0_xattn_Wq, L0_xattn_b_q, L0_xattn_Wk, L0_xattn_b_k, L0_xattn_Wv, L0_xattn_b_v, L0_xattn_Wo, L0_xattn_b_o, L0_attn_W_kqv, L0_ffn_gate_w, L0_ffn_w_gate, L0_ffn_w_up, L0_ffn_w_down, L1_xattn_ln1_g, L1_xattn_ln1_b, L1_xattn_ln2_g, L1_xattn_ln2_b, L1_xattn_Wq, L1_xattn_Wkv, L1_xattn_Wo, L1_attn_fc1_w, L1_attn_fc1_b, L1_attn_in_proj_w, L1_attn_conv_w, L1_attn_conv_b, L1_attn_x_proj_w, L1_attn_dt_proj_w, L1_attn_dt_proj_b, L1_attn_A_log, L1_attn_D, L1_attn_out_proj_w, L1_attn_fc2_w, L1_attn_fc2_b, L1_ffn_gate_w, L1_ffn_w1, L1_ffn_w3, L1_ffn_w2, L1_ffn_sw1, L1_ffn_sw3, L1_ffn_sw2):
    import jax
    import jax.numpy as jnp

    def _L0_xattn_ref(q, k, v, Wq, b_q, Wk, b_k, Wv, b_v, Wo, b_o):
        import jax, jax.numpy as jnp
        import numpy as np
        D = 256
        H = 16
        DH = D // H
        B, Tq, _ = q.shape
        Tk = k.shape[1]
        Q = (q @ Wq + b_q).reshape(B, Tq, H, DH)
        K = (k @ Wk + b_k).reshape(B, Tk, H, DH)
        V = (v @ Wv + b_v).reshape(B, Tk, H, DH)
        scores = jnp.einsum('bthd,bshd->bhts', Q, K) / jnp.sqrt(jnp.float32(DH))
        P = jax.nn.softmax(scores, axis=-1)
        out = jnp.einsum('bhts,bshd->bthd', P, V).reshape(B, Tq, D)
        return out @ Wo + b_o

    def _L0_attn_ref(x, W_kqv):
        import jax, jax.numpy as jnp
        import numpy as np
        import math
        N_EMBD = 256
        NUM_HEADS = 16
        HEAD_DIM = N_EMBD // NUM_HEADS

        def alibi_slopes(num_heads):
            x = (2 ** 8) ** (1.0 / num_heads)
            return jnp.array([1.0 / x ** (i + 1) for i in range(num_heads)], dtype=jnp.float32)
        B, S, E = x.shape
        H, D = (NUM_HEADS, HEAD_DIM)
        kqv = jnp.einsum('bse,fe->bsf', x, W_kqv)
        k, q, v = jnp.split(kqv, 3, axis=-1)
        q = q.reshape(B, S, H, D).transpose(0, 2, 1, 3)
        k = k.reshape(B, S, H, D).transpose(0, 2, 1, 3)
        v = v.reshape(B, S, H, D).transpose(0, 2, 1, 3)
        rel = jnp.arange(S)[None, :] - jnp.arange(S)[:, None]
        bias = alibi_slopes(H)[:, None, None] * rel.astype(jnp.float32)
        scale = math.sqrt(E)
        score = jnp.einsum('bhqd,bhkd->bhqk', q, k) / scale + bias[None]
        causal = jnp.tril(jnp.ones((S, S), dtype=bool))
        score = jnp.where(causal[None, None], score, -jnp.inf)
        attn = jax.nn.softmax(score, axis=-1)
        out = jnp.einsum('bhqk,bhkd->bhqd', attn, v)
        return out.transpose(0, 2, 1, 3).reshape(B, S, E)

    def _L0_ffn_ref(hidden_states, gate_w, w_gate, w_up, w_down):
        import jax, jax.numpy as jnp
        import numpy as np
        TOP_K = 8
        B, S, D = hidden_states.shape
        E = gate_w.shape[0]
        x = hidden_states.reshape(-1, D)
        logits = x.astype(jnp.float32) @ gate_w.astype(jnp.float32).T
        scores = jax.nn.softmax(logits, axis=-1)
        topk_w, topk_ids = jax.lax.top_k(scores, TOP_K)
        topk_w = topk_w / (topk_w.sum(axis=-1, keepdims=True) + 1e-20)
        flat_ids = topk_ids.reshape(-1)
        sort_idx = jnp.argsort(flat_ids)
        sorted_tokens = x[sort_idx // TOP_K]
        group_sizes = jnp.zeros((E,), jnp.int32).at[flat_ids].add(1)
        g = jax.lax.ragged_dot(sorted_tokens, jnp.swapaxes(w_gate, 1, 2), group_sizes)
        u = jax.lax.ragged_dot(sorted_tokens, jnp.swapaxes(w_up, 1, 2), group_sizes)
        h = jax.nn.silu(g) * u
        out = jax.lax.ragged_dot(h, jnp.swapaxes(w_down, 1, 2), group_sizes)
        unsorted = jnp.zeros_like(out).at[sort_idx].set(out)
        y = (unsorted.reshape(B * S, TOP_K, D) * topk_w[..., None]).sum(axis=1)
        return y.reshape(B, S, D)

    def _L1_xattn_ref(image_embeds, latents, ln1_g, ln1_b, ln2_g, ln2_b, Wq, Wkv, Wo):
        import jax, jax.numpy as jnp
        import numpy as np
        DIM = 256
        DIM_HEAD = 64
        HEADS = 16
        INNER = DIM_HEAD * HEADS
        EPS = 1e-05

        def layer_norm(x, g, b):
            m = jnp.mean(x, axis=-1, keepdims=True)
            v = jnp.mean(jnp.square(x - m), axis=-1, keepdims=True)
            return (x - m) * jax.lax.rsqrt(v + EPS) * g + b
        B, S_lat, _ = latents.shape
        x = layer_norm(image_embeds, ln1_g, ln1_b)
        l = layer_norm(latents, ln2_g, ln2_b)
        q = l @ Wq
        kv_in = jnp.concatenate([x, l], axis=1)
        kv = kv_in @ Wkv
        k, v = jnp.split(kv, 2, axis=-1)

        def to_heads(t):
            return t.reshape(t.shape[0], t.shape[1], HEADS, DIM_HEAD).transpose(0, 2, 1, 3)
        q, k, v = (to_heads(q), to_heads(k), to_heads(v))
        scale = 1.0 / np.sqrt(np.sqrt(DIM_HEAD))
        w = jnp.einsum('bhqd,bhkd->bhqk', q * scale, k * scale)
        w = jax.nn.softmax(w.astype(jnp.float32), axis=-1).astype(q.dtype)
        out = jnp.einsum('bhqk,bhkd->bhqd', w, v)
        out = out.transpose(0, 2, 1, 3).reshape(B, S_lat, INNER)
        return out @ Wo

    def _L1_attn_ref(x, fc1_w, fc1_b, in_proj_w, conv_w, conv_b, x_proj_w, dt_proj_w, dt_proj_b, A_log, D, out_proj_w, fc2_w, fc2_b):
        import jax, jax.numpy as jnp
        import numpy as np
        B_SZ, SEQ = (2, 512)
        D_MODEL, D_STATE, D_CONV = (256, 16, 4)
        D_INPUT, D_OUTPUT = (256, 256)
        D_INNER = 2 * D_MODEL
        DT_RANK = D_MODEL // 16
        B, L, _ = x.shape
        d_inner, d_conv = conv_w.shape
        d_state = A_log.shape[1]
        dt_rank = dt_proj_w.shape[1]
        h = x @ fc1_w.T + fc1_b
        xz = h @ in_proj_w.T
        xc, z = jnp.split(xz, 2, axis=-1)
        xp = jnp.pad(xc, ((0, 0), (d_conv - 1, 0), (0, 0)))
        u = sum((xp[:, w:w + L, :] * conv_w[:, w] for w in range(d_conv))) + conv_b
        u = jax.nn.silu(u)
        x_dbl = u @ x_proj_w.T
        dt_low, Bm, Cm = jnp.split(x_dbl, [dt_rank, dt_rank + d_state], axis=-1)
        dt = jax.nn.softplus(dt_low @ dt_proj_w.T + dt_proj_b)
        A = -jnp.exp(A_log)

        def step(hstate, t):
            dt_t, B_t, C_t, u_t = t
            dA = jnp.exp(dt_t[..., None] * A)
            hstate = dA * hstate + (dt_t * u_t)[..., None] * B_t[:, None, :]
            y_t = jnp.einsum('bdn,bn->bd', hstate, C_t)
            return (hstate, y_t)
        h0 = jnp.zeros((B, d_inner, d_state), x.dtype)
        xs = (jnp.swapaxes(dt, 0, 1), jnp.swapaxes(Bm, 0, 1), jnp.swapaxes(Cm, 0, 1), jnp.swapaxes(u, 0, 1))
        _, ys = jax.lax.scan(step, h0, xs)
        y = jnp.swapaxes(ys, 0, 1) + u * D
        y = y * jax.nn.silu(z)
        out = y @ out_proj_w.T
        return out @ fc2_w.T + fc2_b

    def _L1_ffn_ref(x, gate_w, w1, w3, w2, sw1, sw3, sw2):
        import jax, jax.numpy as jnp
        import numpy as np
        DIM = 256
        HID = 128
        N_EXPERTS = 16
        TOP_K = 4
        bsz, seq_len, dim = x.shape
        xf = x.reshape(-1, dim)
        T = xf.shape[0]
        probs = jax.nn.softmax(xf @ gate_w.T, axis=-1)
        top_w, top_idx = jax.lax.top_k(probs, TOP_K)
        top_w = top_w / jnp.sum(top_w, axis=-1, keepdims=True)
        rows = jnp.arange(T)[:, None]
        combine = jnp.zeros((T, N_EXPERTS), dtype=xf.dtype).at[rows, top_idx].set(top_w)
        h1 = jnp.einsum('td,ehd->teh', xf, w1)
        h3 = jnp.einsum('td,ehd->teh', xf, w3)
        act = jax.nn.silu(h1) * h3
        eout = jnp.einsum('teh,edh->ted', act, w2)
        moe_out = jnp.einsum('ted,te->td', eout, combine)
        shared = jax.nn.silu(xf @ sw1.T) * (xf @ sw3.T) @ sw2.T
        return (moe_out + shared).reshape(bsz, seq_len, dim)
    x = x + _L0_xattn_ref(_layernorm(x, axis=-1), ctx_1024, ctx_1024, L0_xattn_Wq, L0_xattn_b_q, L0_xattn_Wk, L0_xattn_b_k, L0_xattn_Wv, L0_xattn_b_v, L0_xattn_Wo, L0_xattn_b_o)
    x = x + _L0_attn_ref(_layernorm(x, axis=-1), L0_attn_W_kqv)
    x = x + _L0_ffn_ref(_layernorm(x, axis=-1), L0_ffn_gate_w, L0_ffn_w_gate, L0_ffn_w_up, L0_ffn_w_down)
    x = x + _L1_xattn_ref(ctx_1024, _layernorm(x, axis=-1), L1_xattn_ln1_g, L1_xattn_ln1_b, L1_xattn_ln2_g, L1_xattn_ln2_b, L1_xattn_Wq, L1_xattn_Wkv, L1_xattn_Wo)
    x = x + _L1_attn_ref(_layernorm(x, axis=-1), L1_attn_fc1_w, L1_attn_fc1_b, L1_attn_in_proj_w, L1_attn_conv_w, L1_attn_conv_b, L1_attn_x_proj_w, L1_attn_dt_proj_w, L1_attn_dt_proj_b, L1_attn_A_log, L1_attn_D, L1_attn_out_proj_w, L1_attn_fc2_w, L1_attn_fc2_b)
    x = x + _L1_ffn_ref(_layernorm(x, axis=-1), L1_ffn_gate_w, L1_ffn_w1, L1_ffn_w3, L1_ffn_w2, L1_ffn_sw1, L1_ffn_sw3, L1_ffn_sw2)
    return x

_drawn_inputs = setup_inputs


def setup_inputs(seed=0):
    import zlib

    import numpy as np

    out = dict(_drawn_inputs(seed))
    spreads = {'L1_xattn_ln1_g': (1.0, 0.2),
     'L1_xattn_ln1_b': (0.0, 0.1),
     'L1_xattn_ln2_g': (1.0, 0.2),
     'L1_xattn_ln2_b': (0.0, 0.404),
     'L1_attn_fc1_b': (0.0, 0.1),
     'L1_attn_conv_b': (0.0, 0.324),
     'L1_attn_dt_proj_b': (-4.599999904632568, 0.6),
     'L1_attn_D': (1.0, 0.6),
     'L1_attn_fc2_b': (0.0, 0.1)}
    factors = {'L0_xattn_Wq': 8.0,
     'L0_xattn_b_q': 8.0,
     'L0_xattn_Wk': 8.0,
     'L0_xattn_b_k': 64.0,
     'L0_xattn_b_v': 8.0,
     'L0_ffn_gate_w': 8.0,
     'L0_ffn_w_gate': 8.0,
     'L0_ffn_w_up': 8.0,
     'L0_ffn_w_down': 8.0,
     'L1_attn_dt_proj_w': 4.007,
     'L1_attn_A_log': 3.374,
     'L1_ffn_gate_w': 8.0,
     'L1_ffn_w1': 8.0,
     'L1_ffn_w3': 8.0,
     'L1_ffn_w2': 8.0,
     'L1_ffn_sw1': 7.448,
     'L1_ffn_sw3': 7.276,
     'L1_ffn_sw2': 7.272}
    for name, (base, spread) in spreads.items():
        noise = np.random.default_rng([zlib.crc32(name.encode()), seed]).standard_normal(out[name].shape)
        drawn = base * np.exp(spread * noise) if base else spread * noise
        out[name] = jnp.asarray(drawn.astype(out[name].dtype))
    for name, factor in factors.items():
        out[name] = (out[name] * factor).astype(out[name].dtype)
    return out
```

```python
import numpy as np
import concourse.bass as bass
from concourse import mybir
from contextlib import ExitStack

F32 = mybir.dt.float32
ALU = mybir.AluOpType
ACT = mybir.ActivationFunctionType
AX = mybir.AxisListType

BATCH, SEQ, D = 64, 32, 256
CTX = 257
TOKENS = BATCH * SEQ
P = 128
TILES = TOKENS // P
BPT = P // SEQ
KT = D // P
BANK = 512
HEADS = 16
HPG = P // SEQ
GROUPS = HEADS // HPG
EPS = 1e-5
NEG = -1e30


class Chain:

    def __init__(self, engine, sem, base=0):
        self.engine, self.sem, self.base, self.n = engine, sem, base, 0

    def link(self, instruction):
        self.n += 1
        instruction.then_inc(self.sem, 1)
        self.engine.wait_ge(self.sem, self.base + self.n)


class Space:

    used = []

    def __init__(self, nc, stage):
        self.nc, self.stage, self.ctx = nc, stage, ExitStack()

    @classmethod
    def clear_used(cls, nc):
        nc.clear_and_free_semaphores(cls.used)
        cls.used = []
        nc.all_engine_barrier()

    def __enter__(self):
        return self

    def __exit__(self, *error):
        return self.ctx.__exit__(*error)

    def sb(self, name, shape, dt=F32):
        return self.ctx.enter_context(self.nc.sbuf_tensor(f"{self.stage}_{name}", shape, dt))

    def ps(self, name, shape, dt=F32):
        return self.ctx.enter_context(self.nc.psum_tensor(f"{self.stage}_{name}", shape, dt))

    def sem(self, name):
        self.used.append(self.nc.alloc_semaphore(f"{self.stage}_{name}"))
        return self.used[-1]

    def block(self):
        return self.nc.Block()


def load_state(nc, x, X, ident):
    with Space(nc, "load") as sp, sp.block() as block:
        loaded, zeroed = sp.sem("loaded"), sp.sem("zeroed")

        @block.sync
        def _(sync):
            rows = x.rearrange("b s d -> (b s) d").rearrange("(t p) d -> p t d", p=P)
            sync.dma_start(X[:, 0:TILES // 2, :], rows[:, 0:TILES // 2, :]).then_inc(loaded, 16)
            sync.wait_ge(loaded, 32)

        @block.scalar
        def _(act):
            rows = x.rearrange("b s d -> (b s) d").rearrange("(t p) d -> p t d", p=P)
            act.dma_start(X[:, TILES // 2:, :], rows[:, TILES // 2:, :]).then_inc(loaded, 16)

        @block.gpsimd
        def _(pool):
            nc.gpsimd.memset(ident[:, :], 0.0).then_inc(zeroed, 1)
            pool.wait_ge(zeroed, 1)
            nc.gpsimd.affine_select(out=ident[:, :], in_=ident[:, :], compare_op=ALU.not_equal, fill=1.0,
                                    base=0, pattern=[[-1, P]], channel_multiplier=1).then_inc(zeroed, 1)


def store_state(nc, out, X):
    with Space(nc, "store") as sp, sp.block() as block:
        stored = sp.sem("stored")
        rows = out.rearrange("b s d -> (b s) d").rearrange("(t p) d -> p t d", p=P)

        @block.sync
        def _(sync):
            sync.dma_start(rows[:, 0:TILES // 2, :], X[:, 0:TILES // 2, :]).then_inc(stored, 16)
            sync.wait_ge(stored, 32)

        @block.scalar
        def _(act):
            act.dma_start(rows[:, TILES // 2:, :], X[:, TILES // 2:, :]).then_inc(stored, 16)
            act.wait_ge(stored, 32)


def norm_moments(dve, stats, tmp, mean, chain, var_ready):
    mean_even, sum_even, mean_odd, sum_odd = (stats[:, :, k] for k in (1, 2, 4, 5))
    chain.link(dve.tensor_tensor(tmp[:, 0, :], mean_even, mean_odd, ALU.add))
    chain.link(dve.tensor_tensor(tmp[:, 1, :], mean_even, mean_odd, ALU.subtract))
    chain.link(dve.tensor_tensor(tmp[:, 2, :], sum_even, sum_odd, ALU.add))
    chain.link(dve.tensor_scalar(mean, tmp[:, 0, :], 0.5, None, ALU.mult))
    chain.link(dve.scalar_tensor_tensor(tmp[:, 3, :], tmp[:, 1, :], 0.25, tmp[:, 1, :], ALU.mult, ALU.mult))
    chain.link(dve.scalar_tensor_tensor(tmp[:, 4, :], tmp[:, 2, :], 1.0 / D, tmp[:, 3, :], ALU.mult, ALU.add))
    dve.tensor_scalar(tmp[:, 5, :], tmp[:, 4, :], EPS, None, ALU.add).then_inc(var_ready, 1)


MOMENT_LINKS = 6


def norm_transposed(nc, stage, X, XT, ident, table=None):
    with Space(nc, stage + "_norm") as sp:
        stats = sp.sb("stats", [P, TILES, 6])
        tmp = sp.sb("tmp", [P, 7, TILES])
        mean = sp.sb("mean", [P, TILES])
        rstd = sp.sb("rstd", [P, TILES])
        xn = sp.sb("xn", [P, 4, D])
        turned = [sp.ps(f"turned{k}", [P, BANK]) for k in range(2)]
        step, stats_ready, var_ready, root_ready = (sp.sem(n) for n in ("step", "stats_ready", "var_ready", "root_ready"))
        rows_ready, turned_pairs, copied_pairs = (sp.sem(n) for n in ("rows_ready", "turned_pairs", "copied_pairs"))
        stored = sp.sem("stored")
        with sp.block() as block:

            if table is not None:
                @block.sync
                def _(sync):
                    rows = table[0:TOKENS, 0:D].rearrange("(t p) d -> p t d", p=P)
                    sync.sem_inc(stored, 16)
                    with sync.Fori(0, TILES // 4) as i:
                        sync.wait_ge(rows_ready, i * 4 + 4)
                        sync.dma_start(rows[:, bass.ds(i * 4, 4), :], xn[:, :, :]).then_inc(stored, 16)
                    sync.wait_ge(stored, 16 * (TILES // 4) + 16)

            @block.vector
            def _(dve):
                with dve.Fori(0, TILES) as t:
                    nc.vector.bn_stats(stats[:, t, :], X[:, t, :]).then_inc(stats_ready, 1)
                dve.wait_ge(stats_ready, TILES)
                chain = Chain(dve, step)
                norm_moments(dve, stats, tmp, mean[:, :], chain, var_ready)
                dve.wait_ge(root_ready, 1)
                chain.link(nc.vector.reciprocal(rstd[:, :], tmp[:, 6, :]))
                with dve.Fori(0, TILES // 4) as i:
                    for k in range(4):
                        if k % 2 == 0:
                            dve.wait_ge(turned_pairs, i * 2 + (k // 2 + 1))
                        if k == 0 and table is not None:
                            dve.wait_ge(stored, i * 16 + 16)
                        t = i * 4 + k
                        nc.vector.tensor_scalar(xn[:, k, :], X[:, t, :], mean[:, bass.ds(t, 1)], rstd[:, bass.ds(t, 1)],
                                                ALU.subtract, ALU.mult).then_inc(rows_ready, 1)

            @block.scalar
            def _(act):
                act.sem_inc(copied_pairs, 2)
                act.wait_ge(var_ready, 1)
                nc.scalar.activation(tmp[:, 6, :], tmp[:, 5, :], ACT.Sqrt).then_inc(root_ready, 1)
                with act.Fori(0, TILES // 4) as i:
                    for k in range(2):
                        act.wait_ge(turned_pairs, i * 2 + (k + 3))
                        nc.scalar.copy(XT[:, :, bass.ds(i * (4 * P) + k * 2 * P, 2 * P)],
                                       turned[k][:, :].rearrange("p (c n) -> p c n", c=KT)).then_inc(copied_pairs, 1)

            @block.tensor
            def _(pe):
                pe.sem_inc(turned_pairs, 2)
                with pe.Fori(0, TILES // 4) as i:
                    for k in range(2):
                        pe.wait_ge(copied_pairs, i * 2 + (k + 1))
                        for n in range(2):
                            pe.wait_ge(rows_ready, i * 4 + (2 * k + n + 1))
                            for c in range(KT):
                                last = nc.tensor.transpose(turned[k][:, (2 * c + n) * P:(2 * c + n + 1) * P],
                                                           xn[:, 2 * k + n, c * P:(c + 1) * P], ident[:, :])
                        last.then_inc(turned_pairs, 1)


def route(nc, stage, XT, gate, experts, top_k, eps, W):
    with Space(nc, stage + "_route") as sp:
        gate_w = sp.sb("gate_w", [P, KT, experts])
        shifted = sp.sb("shifted", [P, TILES, experts])
        probs = sp.sb("probs", [P, TILES, experts])
        rest = sp.sb("rest", [P, TILES, experts])
        best = sp.sb("best", [P, TILES, 8])
        row = sp.sb("row", [P, 4, TILES])
        logits = sp.ps("logits", [P, TILES, experts])
        loaded, logits_ready, shifted_ready, exp_ready, step = (
            sp.sem(n) for n in ("loaded", "logits_ready", "shifted_ready", "exp_ready", "step"))

        def wide(column):
            return column.rearrange("p (t o) -> p t o", o=1).to_broadcast([P, TILES, experts])

        with sp.block() as block:

            @block.sync
            def _(sync):
                sync.dma_start(gate_w[:, :, :], gate).then_inc(loaded, 16)

            @block.tensor
            def _(pe):
                pe.wait_ge(loaded, 16)
                for t in range(TILES):
                    for c in range(KT):
                        last = nc.tensor.matmul(logits[:, t, :], XT[:, c, t * P:(t + 1) * P], gate_w[:, c, :],
                                                start=(c == 0), stop=(c == KT - 1))
                last.then_inc(logits_ready, 1)

            @block.scalar
            def _(act):
                act.wait_ge(shifted_ready, 1)
                nc.scalar.activation(probs[:, :, :], shifted[:, :, :], ACT.Exp).then_inc(exp_ready, 1)

            @block.vector
            def _(dve):
                chain = Chain(dve, step)
                link = chain.link
                dve.wait_ge(logits_ready, 1)
                link(nc.vector.tensor_reduce(row[:, 0, :], logits[:, :, :], AX.X, ALU.max))
                nc.vector.tensor_tensor(shifted[:, :, :], logits[:, :, :], wide(row[:, 0, :]),
                                        ALU.subtract).then_inc(shifted_ready, 1)
                dve.wait_ge(exp_ready, 1)
                link(nc.vector.tensor_reduce(row[:, 1, :], probs[:, :, :], AX.X, ALU.add))
                link(nc.vector.reciprocal(row[:, 2, :], row[:, 1, :]))
                link(nc.vector.tensor_tensor(probs[:, :, :], probs[:, :, :], wide(row[:, 2, :]), ALU.mult))
                for t in range(TILES):
                    last = nc.vector.max(best[:, t, :], probs[:, t, :])
                link(last)
                if top_k < 8:
                    link(nc.vector.memset(best[:, :, top_k:8], -1.0))
                for t in range(TILES):
                    last = nc.vector.match_replace(rest[:, t, :], best[:, t, :], probs[:, t, :], 0.0)
                link(last)
                link(nc.vector.tensor_tensor(probs[:, :, :], probs[:, :, :], rest[:, :, :], ALU.subtract))
                link(nc.vector.tensor_reduce(row[:, 1, :], probs[:, :, :], AX.X, ALU.add))
                if eps:
                    link(nc.vector.tensor_scalar(row[:, 1, :], row[:, 1, :], eps, None, ALU.add))
                link(nc.vector.reciprocal(row[:, 3, :], row[:, 1, :]))
                link(nc.vector.tensor_tensor(W[:, :, 0:experts], probs[:, :, :], wide(row[:, 3, :]), ALU.mult))
                if W.shape[2] > experts:
                    link(nc.vector.memset(W[:, :, experts:], 1.0))


def experts_sum(nc, stage, X, XT, W, w_up, w_down, n_experts, FP, FT):
    NB = 512
    CHUNKS = TOKENS // NB
    TPC = NB // P
    with Space(nc, stage + "_experts") as sp:
        wgu = [sp.sb(f"wgu{s}", [P, KT, 2 * FT * FP]) for s in range(2)]
        wd = [sp.sb(f"wd{s}", [FP, FT, D]) for s in range(2)]
        gated = sp.sb("gated", [FP, 2, NB])
        hidden = [sp.sb(f"hidden{s}", [FP, FT, NB]) for s in range(2)]
        pair = [sp.ps(f"pair{s}", [FP, 2, NB]) for s in range(2)]
        y = [sp.ps(f"y{s}", [P, TPC, D]) for s in range(2)]
        w_loaded = [sp.sem(f"w_loaded{s}") for s in range(2)]
        pair_made, gate_made, hidden_made, y_made, combined = (
            sp.sem(n) for n in ("pair_made", "gate_made", "hidden_made", "y_made", "combined"))
        acc = sp.sem("acc")

        def run(engine, body):
            with engine.Fori(0, n_experts // 2) as i:
                body(i, 2)
            if n_experts % 2:
                body(n_experts // 2, 1)

        with sp.block() as block:

            @block.sync
            def _(sync):
                def load(e, s):
                    sync.dma_start(wgu[s][:, :, :], w_up[e]).then_inc(w_loaded[s], 16)
                    sync.dma_start(wd[s][:, :, :], w_down[e]).then_inc(w_loaded[s], 16)

                for s in range(2):
                    load(s, s)
                with sync.Fori(0, n_experts // 2 - 1) as i:
                    for s in range(2):
                        sync.wait_ge(y_made, i * (2 * CHUNKS) + (2 + (s + 1) * CHUNKS))
                        load(i * 2 + (2 + s), s)
                if n_experts % 2:
                    sync.wait_ge(y_made, 2 + (n_experts - 2) * CHUNKS)
                    load(n_experts - 1, 0)

            @block.tensor
            def _(pe):
                pe.sem_inc(y_made, 2)

                def up(i, c):
                    s, q = c // CHUNKS, c % CHUNKS
                    for j in range(FT):
                        n = c * FT + j
                        pe.wait_ge(hidden_made, i * (2 * CHUNKS * FT) + (n + 1))
                        for half in range(2):
                            for k in range(KT):
                                col = (half * FT + j) * FP
                                last = nc.tensor.matmul(pair[n % 2][:, half, :], wgu[s][:, k, col:col + FP],
                                                        XT[:, k, q * NB:(q + 1) * NB], start=(k == 0), stop=(k == KT - 1))
                        last.then_inc(pair_made, 1)

                def down(i, c):
                    s = c // CHUNKS
                    pe.wait_ge(hidden_made, i * (2 * CHUNKS * FT) + ((c + 1) * FT + 2))
                    pe.wait_ge(combined, i * (2 * CHUNKS) + (c + 1))
                    for t in range(TPC):
                        for j in range(FT):
                            last = nc.tensor.matmul(y[c % 2][:, t, :], hidden[c % 2][:, j, t * P:(t + 1) * P],
                                                    wd[s][:, j, :], start=(j == 0), stop=(j == FT - 1))
                    last.then_inc(y_made, 1)

                def body(i, parts):
                    for s in range(parts):
                        pe.wait_ge(w_loaded[s], i * 32 + 32)
                        for c in range(s * CHUNKS, (s + 1) * CHUNKS):
                            up(i, c)
                            if c:
                                down(i, c - 1)
                    down(i, parts * CHUNKS - 1)

                run(pe, body)

            @block.scalar
            def _(act):
                def body(i, parts):
                    for n in range(parts * CHUNKS * FT):
                        at = i * (2 * CHUNKS * FT)
                        act.wait_ge(pair_made, at + (n + 1))
                        act.wait_ge(hidden_made, at + (n + 1))
                        nc.scalar.activation(gated[:, n % 2, :], pair[n % 2][:, 0, :], ACT.Silu).then_inc(gate_made, 1)

                run(act, body)

            @block.vector
            def _(dve):
                dve.sem_inc(hidden_made, 2)
                dve.sem_inc(combined, 2)

                def product(i, c):
                    dve.wait_ge(y_made, i * (2 * CHUNKS) + (c + 1))
                    for j in range(FT):
                        n = c * FT + j
                        dve.wait_ge(gate_made, i * (2 * CHUNKS * FT) + (n + 1))
                        nc.vector.tensor_tensor(hidden[c % 2][:, j, :], gated[:, n % 2, :], pair[n % 2][:, 1, :],
                                                ALU.mult).then_inc(hidden_made, 1)

                def combine(i, c):
                    s, q = c // CHUNKS, c % CHUNKS
                    dve.wait_ge(y_made, i * (2 * CHUNKS) + (c + 3))
                    for t in range(TPC):
                        tile = q * TPC + t
                        nc.vector.scalar_tensor_tensor(X[:, tile, :], y[c % 2][:, t, :],
                                                              W[:, tile, bass.ds(i * 2 + s, 1)],
                                                              X[:, tile, :], ALU.mult, ALU.add).then_inc(combined if t == TPC - 1 else acc, 1)

                def body(i, parts):
                    for c in range(parts * CHUNKS):
                        product(i, c)
                        if c:
                            combine(i, c - 1)
                    combine(i, parts * CHUNKS - 1)

                run(dve, body)


def build_program(nc, A, out, stages=(0, 1, 2, 3, 4, 5)):
    Space.used = []
    with ExitStack() as ctx:
        X = ctx.enter_context(nc.sbuf_tensor("X", [P, TILES, D], F32))
        ident = ctx.enter_context(nc.sbuf_tensor("ident", [P, P], F32))
        load_state(nc, A["x"], X, ident)
        for n in stages:
            with ExitStack() as layer:
                XT = layer.enter_context(nc.sbuf_tensor(f"XT{n}", [P, KT, TOKENS], F32))
                if n not in (2, 3):
                    norm_transposed(nc, f"s{n}", X, XT, ident)
                SUBLAYERS[n](nc, A, X, XT, ident)
            Space.clear_used(nc)
        store_state(nc, out, X)


def sub_moe1(nc, A, X, XT, ident):
    with nc.sbuf_tensor("moe1_W", [P, TILES, 17], F32) as W:
        route(nc, "moe1", XT, A["L1_ffn_gate_w"], 16, 4, 0.0, W)
        experts_sum(nc, "moe1", X, XT, W, A["L1_ffn_up"], A["L1_ffn_down"], 17, 128, 1)


SUBLAYERS = {5: sub_moe1}


E0, TOP0, F0, FT0 = 64, 8, 96, 2
HALVES = P // E0
HALF = TOKENS // HALVES
CAP = 192
REST = CAP - P
SLOT_TILES = HALVES * CAP // P
ROW = D + E0


def expert_lists(nc, A, W, ident, table, sums, slots, flag, left):
    J = HALF // P
    with Space(nc, "lists") as sp:
        mask = sp.sb("mask", [P, J, HALVES, E0])
        codes = sp.sb("codes", [P, HALF])
        values = [sp.sb("values", [P, HALF]), left]
        lists = sp.sb("lists", [P, CAP])
        rests = sp.sb("rests", [E0, HALVES, REST])
        base = sp.sb("base", [P, SLOT_TILES + 1])
        slot_f = sp.sb("slot_f", [P, 3, SLOT_TILES, E0])
        zeros = sp.sb("zeros", [P, (TOKENS // P + 1) * D])
        top = sp.sb("top", [P, 1])
        top_row = sp.sb("top_row", [1, P])
        most = sp.sb("most", [1, 1])
        ps_v = sp.ps("ps_v", [P, HALF])
        ps_l = sp.ps("ps_l", [P, HALVES, E0])
        ps_r = sp.ps("ps_r", [P, BANK])
        ps_m = sp.ps("ps_m", [P, BANK])
        loaded, mask_made, turned, step, moved, lists_turned, stored, zeroed, top_made, top_turned = (
            sp.sem(n) for n in ("loaded", "mask_made", "turned", "step", "moved", "lists_turned", "stored", "zeroed",
                                "top_made", "top_turned"))
        with sp.block() as block:

            @block.sync
            def _(sync):
                sync.dma_start(codes[:, :], A["codes"]).then_inc(loaded, 16)
                sync.dma_start(base[:, :], A["slot_base"]).then_inc(loaded, 16)
                sync.dma_start(table[0:TOKENS, D:].rearrange("(t p) e -> p t e", p=P), W[:, :, :]).then_inc(stored, 16)
                sync.wait_ge(zeroed, 1)
                sync.dma_start(table[TOKENS:, :], zeros[:, 0:ROW]).then_inc(stored, 16)
                for s in sums:
                    sync.dma_start(s.rearrange("(p t) d -> p (t d)", p=P), zeros[:, :]).then_inc(stored, 16)
                sync.wait_ge(stored, 16 * (2 + len(sums)))

            @block.gpsimd
            def _(pool):
                nc.gpsimd.memset(zeros[:, :], 0.0).then_inc(zeroed, 1)

            @block.tensor
            def _(pe):
                pe.wait_ge(mask_made, 1)
                for j in range(J):
                    last = nc.tensor.transpose(ps_v[:, j * P:(j + 1) * P], mask[:, j, :, :].rearrange("p h e -> p (h e)"), ident[:, :])
                last.then_inc(turned, 1)
                pe.wait_ge(moved, HALVES)
                nc.tensor.transpose(ps_l[:, :, :].rearrange("p h e -> p (h e)"), lists[:, 0:P], ident[:, :]).then_inc(lists_turned, 1)
                nc.tensor.transpose(ps_r[:, 0:E0], rests[:, :, :].rearrange("e h s -> e (h s)"), ident[0:E0, 0:E0]
                                    ).then_inc(lists_turned, 1)
                pe.wait_ge(top_made, 1)
                nc.tensor.transpose(ps_m[0:1, 0:P], top[:, 0:1], ident[:, :]).then_inc(top_turned, 1)

            @block.vector
            def _(dve):
                link = Chain(dve, step).link
                v = nc.vector
                v.tensor_scalar(mask[:, :, :, :], W[:, :, :].rearrange("p (h j) e -> p j h e", h=HALVES), 0.0, None,
                                ALU.is_gt).then_inc(mask_made, 1)
                dve.wait_ge(loaded, 32)
                dve.wait_ge(turned, 1)
                link(v.tensor_tensor(values[0][:, :], ps_v[:, :], codes[:, :], ALU.mult))
                for r in range(CAP // 8):
                    best = lists[:, 8 * r:8 * r + 8]
                    link(v.max(best, values[r % 2][:, :]))
                    link(v.match_replace(values[(r + 1) % 2][:, :], best, values[r % 2][:, :], 0.0))
                assert CAP // 8 % 2 == 0
                link(v.tensor_copy(left[:, :], values[0][:, :]))
                v.tensor_reduce(top[:, 0:1], left[:, :], AX.X, ALU.max).then_inc(top_made, 1)
                for h in range(HALVES):
                    v.tensor_copy(rests[:, h, :], lists[h * E0:(h + 1) * E0, P:]).then_inc(moved, 1)
                dve.wait_ge(lists_turned, 2)
                tiles = [ps_l[:, 0, :], ps_l[:, 1, :], ps_r[:, 0:E0]]
                for r, code in enumerate(tiles):
                    link(v.tensor_scalar(slot_f[:, 0, r, :], code, -1.0, base[:, r:r + 1], ALU.mult, ALU.add))
                    link(v.tensor_scalar(slot_f[:, 1, r, :], code, 0.0, None, ALU.is_gt))
                link(v.tensor_tensor(slot_f[:, 2, :, :], slot_f[:, 0, :, :], slot_f[:, 1, :, :], ALU.mult))
                link(v.tensor_scalar(slots[:, :, :].rearrange("p e r -> p r e"), slot_f[:, 2, :, :], base[:, SLOT_TILES:], None, ALU.add))
                dve.wait_ge(top_turned, 1)
                link(v.tensor_reduce(most[:, :], ps_m[0:1, 0:P], AX.X, ALU.max))
                link(v.tensor_scalar(flag[:, :], most[:, :], 0.0, None, ALU.is_gt))


def chosen_experts(nc, A, table, sums, slots, ident):
    N = SLOT_TILES * P
    with Space(nc, "chosen") as sp:
        wgu = [sp.sb(f"wgu{s}", [P, KT, 2 * FT0 * F0]) for s in range(2)]
        wd = [sp.sb(f"wd{s}", [F0, FT0, D]) for s in range(2)]
        index = [sp.sb(f"index{s}", [P, SLOT_TILES], mybir.dt.int32) for s in range(4)]
        rows = [sp.sb(f"rows{s}", [P, SLOT_TILES, ROW]) for s in range(4)]
        x_t = [sp.sb(f"x_t{s}", [P, KT, N]) for s in range(2)]
        gated = sp.sb("gated", [F0, FT0, N])
        hidden = [sp.sb(f"hidden{s}", [F0, FT0, N]) for s in range(2)]
        y = [sp.sb(f"y{s}", [P, SLOT_TILES, D]) for s in range(2)]
        ps_x = sp.ps("ps_x", [P, KT, BANK])
        pair = [sp.ps(f"pair{j}", [F0, 2, BANK]) for j in range(FT0)]
        ps_y = sp.ps("ps_y", [P, 4, D])
        w_loaded = [sp.sem(f"w_loaded{s}") for s in range(2)]
        gathered = [sp.sem(f"gathered{s}") for s in range(4)]
        scattered = [sp.sem(f"scattered{s}") for s in range(4)]
        index_made, x_turned, x_copied, y_made, y_scaled, pair_made, gate_made, hidden_made, y_acc = (
            sp.sem(n) for n in ("index_made", "x_turned", "x_copied", "y_made", "y_scaled", "pair_made", "gate_made",
                                "hidden_made", "y_acc"))
        issued = sp.sem("issued")

        def turns(engine, step):
            for s in range(4):
                step(s, 0, s, s == 0, False)
            with engine.Fori(1, E0 // 4 - 1) as i:
                for s in range(4):
                    step(i * 4 + s, i, s, False, False)
            for s in range(4):
                step(E0 - 4 + s, E0 // 4 - 1, s, False, s == 3)

        with sp.block() as block:

            @block.sync
            def _(sync):
                def load(e, s):
                    sync.dma_start(wgu[s][:, :, :], A["L0_ffn_up"][e]).then_inc(w_loaded[s], 16)
                    sync.dma_start(wd[s][:, :, :], A["L0_ffn_down"][e]).then_inc(w_loaded[s], 16)

                for s in range(2):
                    load(s, s)
                with sync.Fori(0, E0 // 2 - 1) as i:
                    for s in range(2):
                        sync.wait_ge(y_made, i * 2 + (s + 1))
                        load(i * 2 + (s + 2), s)

            @block.gpsimd
            def _(pool):
                def gather(e, s):
                    nc.gpsimd.tensor_copy(index[s][:, :], slots[:, bass.ds(e, 1), :].rearrange("p o r -> p (o r)")
                                          ).then_inc(index_made, 1)
                    pool.wait_ge(index_made, e + 1)
                    pool.sem_inc(issued, 1)
                    for r in range(SLOT_TILES):
                        nc.gpsimd.indirect_dma_start(rows[s][:, r, :], None, table[:, :],
                                                     bass.IndirectOffsetOnAxis(ap=index[s][:, r:r + 1], axis=0)
                                                     ).then_inc(gathered[s], 16)

                def step(e, i, s, first, last):
                    p, ip = (s - 1) % 4, i - (1 if s == 0 else 0)
                    if not first:
                        pool.wait_ge(scattered[p], (ip * 16 + 16) * SLOT_TILES)
                    if not (isinstance(e, int) and e + 3 >= E0):
                        gather(i * 4 + (s + 3), p)
                    pool.wait_ge(y_scaled, e + 1)
                    pool.sem_inc(issued, 1)
                    for r in range(SLOT_TILES):
                        nc.gpsimd.indirect_dma_start(sums[r], bass.IndirectOffsetOnAxis(ap=index[s][:, r:r + 1], axis=0),
                                                     y[s % 2][:, r, :], None, compute_op=ALU.add).then_inc(scattered[s], 16)

                for s in range(3):
                    gather(s, s)
                turns(pool, step)
                pool.wait_ge(scattered[3], E0 // 4 * 16 * SLOT_TILES)

            @block.tensor
            def _(pe):
                def turn_x(e, i, s):
                    pe.wait_ge(gathered[s], (i * 16 + 16) * SLOT_TILES)
                    if not (isinstance(e, int) and e == 0):
                        pe.wait_ge(x_copied, e)
                    for c in range(KT):
                        for r in range(SLOT_TILES):
                            last = nc.tensor.transpose(ps_x[:, c, r * P:(r + 1) * P], rows[s][:, r, c * P:(c + 1) * P], ident[:, :])
                    last.then_inc(x_turned, 1)

                def up(e, i, s, j, first):
                    s, turn = s % 2, s // 2
                    if j == 0:
                        pe.wait_ge(x_copied, e + 1)
                        pe.wait_ge(w_loaded[s], i * 64 + (turn * 32 + 32))
                    if not first:
                        pe.wait_ge(hidden_made, (e - 1) * FT0 + (j + 1))
                    for side in range(2):
                        for c in range(KT):
                            col = (side * FT0 + j) * F0
                            last = nc.tensor.matmul(pair[j][:, side, 0:N], wgu[s][:, c, col:col + F0], x_t[s][:, c, :],
                                                    start=(c == 0), stop=(c == KT - 1))
                    last.then_inc(pair_made, 1)

                def down(e, s, very_first):
                    pe.wait_ge(hidden_made, e * FT0 + FT0)
                    if not very_first:
                        pe.wait_ge(y_scaled, e)
                    for r in range(SLOT_TILES):
                        for j in range(FT0):
                            last = nc.tensor.matmul(ps_y[:, r, :], hidden[s][:, j, r * P:(r + 1) * P], wd[s][:, j, :],
                                                    start=(j == 0), stop=(j == FT0 - 1))
                    last.then_inc(y_made, 1)

                turn_x(0, 0, 0)

                def step(e, i, s, first, last):
                    up(e, i, s, 0, first)
                    if not first:
                        down(i * 4 + (s - 1), (s - 1) % 2, isinstance(e, int) and e == 1)
                    up(e, i, s, 1, first)
                    if not last:
                        turn_x(i * 4 + (s + 1), i + (s + 1) // 4, (s + 1) % 4)

                turns(pe, step)
                down(E0 - 1, 1, False)

            @block.scalar
            def _(act):
                def take_x(e, s, early):
                    act.wait_ge(x_turned, e + 1)
                    if not early:
                        act.wait_ge(pair_made, (e - 1) * FT0)
                    nc.scalar.copy(x_t[s][:, :, :], ps_x[:, :, 0:N]).then_inc(x_copied, 1)

                take_x(0, 0, True)

                def step(e, i, s, first, last):
                    for j in range(FT0):
                        act.wait_ge(pair_made, e * FT0 + (j + 1))
                        if not first:
                            act.wait_ge(hidden_made, (e - 1) * FT0 + (j + 1))
                        nc.scalar.activation(gated[:, j, :], pair[j][:, 0, 0:N], ACT.Silu).then_inc(gate_made, 1)
                    if not last:
                        take_x(i * 4 + (s + 1), (s + 1) % 2, isinstance(e, int) and e == 0)

                turns(act, step)

            @block.vector
            def _(dve):
                def scale(e, i, s):
                    dve.wait_ge(y_made, e + 1)
                    if not (isinstance(e, int) and e < 2):
                        dve.wait_ge(scattered[(s - 2) % 4], (i * 16 + (16 if s >= 2 else 0)) * SLOT_TILES)
                    for r in range(SLOT_TILES):
                        nc.vector.tensor_scalar(y[s % 2][:, r, :], ps_y[:, r, :], rows[s][:, r, bass.ds(e + D, 1)], None,
                                                ALU.mult).then_inc(y_scaled if r == SLOT_TILES - 1 else y_acc, 1)

                def step(e, i, s, first, last):
                    for j in range(FT0):
                        dve.wait_ge(gate_made, e * FT0 + (j + 1))
                        if not (isinstance(e, int) and e < 2):
                            dve.wait_ge(y_made, e - 1)
                        nc.vector.tensor_tensor(hidden[s % 2][:, j, :], gated[:, j, :], pair[j][:, 1, 0:N], ALU.mult
                                                ).then_inc(hidden_made, 1)
                        if j == 0 and not first:
                            scale(i * 4 + (s - 1), i - (1 if s == 0 else 0), (s - 1) % 4)

                turns(dve, step)
                scale(E0 - 1, E0 // 4 - 1, 3)


def add_sums(nc, X, sums):
    with Space(nc, "add_sums") as sp:
        part = [sp.sb(f"part{r}", [P, TILES, D]) for r in range(len(sums))]
        loaded = [sp.sem(f"loaded{r}") for r in range(len(sums))]
        added = sp.sem("added")
        with sp.block() as block:

            @block.sync
            def _(sync):
                for r, s in enumerate(sums):
                    sync.dma_start(part[r][:, :, :], s[0:TOKENS, :].rearrange("(t p) d -> p t d", p=P)).then_inc(loaded[r], 16)

            @block.vector
            def _(dve):
                link = Chain(dve, added).link
                for r in range(len(sums)):
                    dve.wait_ge(loaded[r], 16)
                    link(nc.vector.tensor_tensor(X[:, :, :], X[:, :, :], part[r][:, :, :], ALU.add))


def keep_left(nc, W, left, ident):
    J = HALF // P
    with Space(nc, "keep_left") as sp:
        over = sp.sb("over", [P, HALF])
        ps = sp.ps("ps", [P, J, HALVES, E0])
        marked, turned, done = (sp.sem(n) for n in ("marked", "turned", "done"))
        with sp.block() as block:

            @block.vector
            def _(dve):
                nc.vector.tensor_scalar(over[:, :], left[:, :], 0.0, None, ALU.is_gt).then_inc(marked, 1)
                dve.wait_ge(turned, 1)
                for h in range(HALVES):
                    part = W[:, h * J:(h + 1) * J, :]
                    nc.vector.tensor_tensor(part, part, ps[:, :, h, :], ALU.mult).then_inc(done, 1)

            @block.tensor
            def _(pe):
                pe.wait_ge(marked, 1)
                for j in range(J):
                    last = nc.tensor.transpose(ps[:, j, :, :].rearrange("p h e -> p (h e)"), over[:, j * P:(j + 1) * P], ident[:, :])
                last.then_inc(turned, 1)


def top8_experts(nc, A, X, XT, ident):
    table = nc.dram_tensor("table", (TOKENS + P, ROW), F32, kind="Internal").ap()
    sums = [nc.dram_tensor(f"sums{r}", (TOKENS + P, D), F32, kind="Internal").ap() for r in range(SLOT_TILES)]
    norm_transposed(nc, "s2", X, XT, ident, table)
    with Space(nc, "top8") as sp:
        W = sp.sb("W", [P, TILES, E0])
        left = sp.sb("left", [P, HALF])
        slots = sp.sb("slots", [P, E0, SLOT_TILES], mybir.dt.int32)
        flag = sp.sb("flag", [1, 1], mybir.dt.int32)
        route(nc, "moe0", XT, A["L0_ffn_gate_w"], E0, TOP0, 1e-20, W)
        expert_lists(nc, A, W, ident, table, sums, slots, flag, left)
        chosen_experts(nc, A, table, sums, slots, ident)
        add_sums(nc, X, sums)
        overflow = nc.values_load(flag[0:1, 0:1], min_val=0, max_val=1)
        with nc.If(overflow > 0):
            nc.all_engine_barrier()
            keep_left(nc, W, left, ident)
            experts_sum(nc, "moe0", X, XT, W, A["L0_ffn_up"], A["L0_ffn_down"], E0, F0, FT0)
        nc.end_all_ifs()


SUBLAYERS[2] = top8_experts


def pipelined(engine, n, front, back, unroll=2):
    front(0, 0, 0)

    def turn(i, steps):
        for k in range(unroll):
            if k < steps:
                front(i * unroll + (k + 1), i + (k + 1) // unroll, (k + 1) % unroll)
            back(i * unroll + k, i, k)

    with engine.Fori(0, n // unroll - 1) as i:
        turn(i, unroll)
    turn(n // unroll - 1, unroll - 1)


def nothing(t, i, s):
    pass


def self_attention(nc, A, X, XT, ident):
    HD = D // HEADS
    HPC = P // HD
    with Space(nc, "self") as sp:
        w = sp.sb("w", [P, KT, 3 * D])
        bias = sp.sb("bias", [P, GROUPS, SEQ])
        own = sp.sb("own", [P, HPC])
        xt = [sp.sb(f"xt{s}", [P, KT, P]) for s in range(2)]
        k_t = [sp.sb(f"k_t{s}", [P, KT, P]) for s in range(2)]
        v = [sp.sb(f"v{s}", [P, D]) for s in range(2)]
        q_own = [sp.sb(f"q_own{s}", [P, KT, BPT, HPC * SEQ]) for s in range(2)]
        soft = sp.sb("soft", [P, GROUPS, P])
        shifted = [sp.sb(f"shifted{s}", [P, GROUPS, P]) for s in range(2)]
        probs = [sp.sb(f"probs{s}", [P, GROUPS, P]) for s in range(2)]
        probs_t = sp.sb("probs_t", [P, GROUPS, P])
        row = sp.sb("row", [P, 3, GROUPS * BPT])
        ps_q = sp.ps("ps_q", [P, BANK])
        ps_kv = sp.ps("ps_kv", [P, 2, D])
        ps_s = sp.ps("ps_s", [P, GROUPS, P])
        ps_t = sp.ps("ps_t", [P, GROUPS, P])
        ps_o = sp.ps("ps_o", [P, BPT, 2 * GROUPS, HPG * HD])
        loaded = sp.sem("loaded")
        names = ("xt_copied", "projected", "scored", "turned", "attended", "kv_copied", "exps", "t_copied",
                 "q_masked", "shifts", "normed", "added")
        xt_copied, projected, scored, turned, attended, kv_copied, exps, t_copied, q_masked, shifts, normed, added = (
            sp.sem(n) for n in names)
        step, acc = sp.sem("step"), sp.sem("acc")

        with sp.block() as block:

            @block.sync
            def _(sync):
                sync.dma_start(w[:, :, :], A["L0_attn_w"]).then_inc(loaded, 16)
                sync.dma_start(bias[:, :, :], A["alibi"]).then_inc(loaded, 16)
                sync.dma_start(own[:, :], A["own16"]).then_inc(loaded, 16)

            @block.gpsimd
            def _(pool):
                pool.sem_inc(xt_copied, 2)

                def front(t, i, s):
                    pool.wait_ge(projected, t + 1)
                    nc.gpsimd.tensor_copy(xt[s][:, :, :], XT[:, :, bass.ds(t * P, P)]).then_inc(xt_copied, 1)

                pipelined(pool, TILES, front, nothing)

            @block.tensor
            def _(pe):
                pe.wait_ge(loaded, 48)
                pe.sem_inc(projected, 2)
                pe.sem_inc(attended, 2)
                pe.sem_inc(turned, 2)

                def front(t, i, s):
                    pe.wait_ge(xt_copied, t + 3)
                    pe.wait_ge(kv_copied, t + 1)
                    pe.wait_ge(q_masked, t * KT + KT)
                    for m in range(2 * KT):
                        col = (D if m < KT else 0) + (m % KT) * P
                        for c in range(KT):
                            out = ps_q[:, m * P:(m + 1) * P] if m < KT else ps_kv[:, 0, (m - KT) * P:(m - KT + 1) * P]
                            nc.tensor.matmul(out, w[:, c, col:col + P], xt[s][:, c, :],
                                             start=(c == 0), stop=(c == KT - 1))
                    for c in range(KT):
                        last = nc.tensor.matmul(ps_kv[:, 1, :], xt[s][:, c, :], w[:, c, 2 * D:3 * D],
                                                start=(c == 0), stop=(c == KT - 1))
                    last.then_inc(projected, 1)
                    pe.wait_ge(q_masked, t * KT + 2 * KT)
                    pe.wait_ge(kv_copied, t + 2)
                    pe.wait_ge(shifts, t + 2)
                    for b in range(BPT):
                        at = slice(b * SEQ, (b + 1) * SEQ)
                        for g in range(GROUPS):
                            last = nc.tensor.matmul(ps_s[:, g, at], q_own[s][:, g * HPG // HPC, b, (g * P) % (HPC * SEQ):(g * P) % (HPC * SEQ) + P],
                                                    k_t[s][:, g * HPG // HPC, at], start=True, stop=True)
                    last.then_inc(scored, 1)

                def back(t, i, s):
                    pe.wait_ge(normed, t + 1)
                    pe.wait_ge(t_copied, t + 1)
                    for g in range(GROUPS):
                        last = nc.tensor.transpose(ps_t[:, g, :], probs[s][:, g, :], ident[:, :])
                    last.then_inc(turned, 1)
                    pe.wait_ge(t_copied, t + 2)
                    pe.wait_ge(added, t + 1)
                    for g in range(GROUPS):
                        for b in range(BPT):
                            at = slice(b * SEQ, (b + 1) * SEQ)
                            last = nc.tensor.matmul(ps_o[:, b, g, :], probs_t[at, g, :],
                                                    v[s][at, g * HPG * HD:(g + 1) * HPG * HD], start=True, stop=True)
                    last.then_inc(attended, 1)

                pipelined(pe, TILES, front, back)

            @block.scalar
            def _(act):
                act.sem_inc(kv_copied, 1)
                act.sem_inc(t_copied, 1)

                def front(t, i, s):
                    act.wait_ge(projected, t + 3)
                    act.wait_ge(attended, t + 1)
                    nc.scalar.copy(v[s][:, :], ps_kv[:, 1, :]).then_inc(acc, 1)
                    nc.scalar.copy(k_t[s][:, :, :], ps_kv[:, 0, :].rearrange("p (c n) -> p c n", c=KT)).then_inc(kv_copied, 1)
                    act.wait_ge(shifts, t + 3)
                    nc.scalar.activation(shifted[s][:, :, :], shifted[s][:, :, :], ACT.Exp).then_inc(exps, 1)

                def back(t, i, s):
                    act.wait_ge(turned, t + 3)
                    act.wait_ge(attended, t + 2)
                    nc.scalar.copy(probs_t[:, :, :], ps_t[:, :, :]).then_inc(t_copied, 1)

                pipelined(act, TILES, front, back)

            @block.vector
            def _(dve):
                STEPS = 4
                dve.wait_ge(loaded, 48)
                dve.sem_inc(q_masked, KT)
                dve.sem_inc(shifts, 2)
                dve.sem_inc(added, 1)

                def wide(k):
                    return row[:, k, :].rearrange("p (n o) -> p n o", o=1).to_broadcast([P, GROUPS * BPT, SEQ])

                def by_row(a):
                    return a[:, :, :].rearrange("p g (b k) -> p (g b) k", k=SEQ)

                def front(t, i, s):
                    chain = Chain(dve, step, t * STEPS)
                    dve.wait_ge(projected, t + 3)
                    for c in range(KT):
                        nc.vector.tensor_tensor(
                            q_own[s][:, c, :, :].rearrange("p b (h q) -> p b h q", q=SEQ),
                            ps_q[:, c * P:(c + 1) * P].rearrange("p (b o q) -> p b o q", o=1, q=SEQ).to_broadcast([P, BPT, HPC, SEQ]),
                            own[:, :].rearrange("p (b h o) -> p b h o", b=1, o=1).to_broadcast([P, BPT, HPC, SEQ]),
                            ALU.mult).then_inc(q_masked, 1)
                    dve.wait_ge(scored, t + 1)
                    chain.link(nc.vector.tensor_tensor(
                        soft[:, :, :].rearrange("p g (b k) -> p g b k", k=SEQ),
                        ps_s[:, :, :].rearrange("p g (b k) -> p g b k", k=SEQ),
                        bias[:, :, :].rearrange("p g (o k) -> p g o k", o=1).to_broadcast([P, GROUPS, BPT, SEQ]), ALU.add))
                    chain.link(nc.vector.tensor_reduce(row[:, 0, :], by_row(soft), AX.X, ALU.max))
                    nc.vector.tensor_tensor(by_row(shifted[s]), by_row(soft), wide(0), ALU.subtract).then_inc(shifts, 1)
                    dve.wait_ge(exps, t + 1)
                    chain.link(nc.vector.tensor_reduce(row[:, 1, :], by_row(shifted[s]), AX.X, ALU.add))
                    chain.link(nc.vector.reciprocal(row[:, 2, :], row[:, 1, :]))
                    dve.wait_ge(turned, t + 1)
                    nc.vector.tensor_tensor(by_row(probs[s]), by_row(shifted[s]), wide(2), ALU.mult).then_inc(normed, 1)

                def back(t, i, s):
                    dve.wait_ge(attended, t + 3)
                    for b in range(BPT):
                        rows = slice(b * SEQ, (b + 1) * SEQ)
                        for h in range(HPG):
                            out = X[rows, bass.ds(t, 1), :].rearrange("p o (g h d) -> p (o g) h d", g=GROUPS, h=HPG)[:, :, h, :]
                            last = nc.vector.tensor_tensor(out, ps_o[h * SEQ:(h + 1) * SEQ, b, 0:GROUPS, h * HD:(h + 1) * HD],
                                                           out, ALU.add)
                            last.then_inc(added if (b, h) == (BPT - 1, HPG - 1) else acc, 1)

                pipelined(dve, TILES, front, back)


SUBLAYERS[1] = self_attention


def project_queries(nc, A, XT, Q, stage, weights, bias):
    NB = 512
    with Space(nc, stage) as sp:
        w = sp.sb("w", [P, KT, D])
        b = sp.sb("b", [P, KT])
        ps = [sp.ps(f"ps{s}", [P, KT, NB]) for s in range(2)]
        loaded, made, copied = (sp.sem(n) for n in ("loaded", "made", "copied"))
        with sp.block() as block:

            @block.sync
            def _(sync):
                sync.dma_start(w[:, :, :], weights).then_inc(loaded, 16)
                sync.dma_start(b[:, :], bias).then_inc(loaded, 16)

            @block.tensor
            def _(pe):
                pe.wait_ge(loaded, 32)
                for q in range(TOKENS // NB):
                    if q >= 2:
                        pe.wait_ge(copied, KT * (q - 1))
                    for m in range(KT):
                        for c in range(KT):
                            last = nc.tensor.matmul(ps[q % 2][:, m, :], w[:, c, m * P:(m + 1) * P],
                                                    XT[:, c, q * NB:(q + 1) * NB], start=(c == 0), stop=(c == KT - 1))
                    last.then_inc(made, 1)

            @block.scalar
            def _(act):
                act.wait_ge(loaded, 32)
                for q in range(TOKENS // NB):
                    act.wait_ge(made, q + 1)
                    for m in range(KT):
                        nc.scalar.activation(Q[:, m, q * NB:(q + 1) * NB], ps[q % 2][:, m, :], ACT.Identity,
                                             bias=b[:, m:m + 1]).then_inc(copied, 1)


def project_rows(nc, stage, X, rows, ident, weights, bias_in, bias_out):
    with Space(nc, stage) as sp:
        w = sp.sb("w", [P, KT, D])
        b_in = sp.sb("b_in", [P, KT])
        b_out = sp.sb("b_out", [1, D])
        ones = sp.sb("ones", [1, P])
        rows_t = [sp.sb(f"rows_t{s}", [P, KT, P]) for s in range(2)]
        ps_t = [sp.ps(f"ps_t{s}", [P, BANK]) for s in range(2)]
        ps_y = [sp.ps(f"ps_y{s}", [P, BANK]) for s in range(2)]
        loaded, ones_ready, turned, copied, made, added = (
            sp.sem(n) for n in ("loaded", "ones_ready", "turned", "copied", "made", "added"))
        with sp.block() as block:

            @block.sync
            def _(sync):
                sync.dma_start(w[:, :, :], weights).then_inc(loaded, 16)
                sync.dma_start(b_in[:, :], bias_in).then_inc(loaded, 16)
                sync.dma_start(b_out[:, :], bias_out).then_inc(loaded, 16)

            @block.gpsimd
            def _(pool):
                nc.gpsimd.memset(ones[:, :], 1.0).then_inc(ones_ready, 1)

            @block.tensor
            def _(pe):
                pe.wait_ge(loaded, 48)
                pe.wait_ge(ones_ready, 1)

                def turn(t):
                    if t >= 2:
                        pe.wait_ge(copied, KT * (t - 1))
                    for c in range(KT):
                        last = nc.tensor.transpose(ps_t[t % 2][:, c * P:(c + 1) * P], rows[:, t, c * P:(c + 1) * P], ident[:, :])
                    last.then_inc(turned, 1)

                turn(0)
                for t in range(TILES):
                    if t + 1 < TILES:
                        turn(t + 1)
                    pe.wait_ge(copied, KT * (t + 1))
                    if t >= 2:
                        pe.wait_ge(added, t - 1)
                    nc.tensor.matmul(ps_y[t % 2][:, 0:D], ones[:, :], b_out[:, :], start=True, stop=False)
                    for c in range(KT):
                        last = nc.tensor.matmul(ps_y[t % 2][:, 0:D], rows_t[t % 2][:, c, :], w[:, c, :],
                                                start=False, stop=(c == KT - 1))
                    last.then_inc(made, 1)

            @block.scalar
            def _(act):
                act.wait_ge(loaded, 48)
                for t in range(TILES):
                    act.wait_ge(turned, t + 1)
                    if t >= 2:
                        act.wait_ge(made, t - 1)
                    for c in range(KT):
                        nc.scalar.activation(rows_t[t % 2][:, c, :], ps_t[t % 2][:, c * P:(c + 1) * P], ACT.Identity,
                                             bias=b_in[:, c:c + 1]).then_inc(copied, 1)

            @block.vector
            def _(dve):
                for t in range(TILES):
                    dve.wait_ge(made, t + 1)
                    nc.vector.tensor_tensor(X[:, t, :], X[:, t, :], ps_y[t % 2][:, 0:D], ALU.add).then_inc(added, 1)


def cross_attention_0(nc, A, X, XT, ident):
    HD = D // HEADS
    HPC = P // HD
    W = HPG * HD
    FULL = CTX // P
    with Space(nc, "cross0") as outer:
        Q = outer.sb("Q", [P, KT, TOKENS])
        attended_rows = outer.sb("attended_rows", [P, TILES, D])
        project_queries(nc, A, XT, Q, "cross0_q", A["L0_xattn_Wq"], A["L0_xattn_b_q"])
        with Space(nc, "cross0_in") as sp:
            w = sp.sb("w", [P, KT, 2 * D])
            b_k = sp.sb("b_k", [P, KT])
            own = sp.sb("own", [P, HPC])
            ends = sp.sb("ends", [P, KT, BATCH])
            v_end_rows = sp.sb("v_end_rows", [BATCH, D])
            v_end = sp.sb("v_end", [GROUPS, BATCH, D])
            ctx_t = [sp.sb(f"ctx_t{s}", [P, KT, CTX]) for s in range(2)]
            q_own = [sp.sb(f"q_own{s}", [P, KT, HPC * SEQ]) for s in range(2)]
            k_t = [sp.sb(f"k_t{s}", [P, KT, CTX]) for s in range(2)]
            v = [sp.sb(f"v{s}", [P, FULL, D]) for s in range(2)]
            probs = [sp.sb(f"probs{s}", [P, GROUPS, CTX]) for s in range(2)]
            probs_t = sp.sb("probs_t", [P, FULL, GROUPS * P])
            end_t = sp.sb("end_t", [GROUPS, P])
            row = [sp.sb(f"row{s}", [P, 4, GROUPS]) for s in range(2)]
            ps_k = sp.ps("ps_k", [P, KT, BANK])
            ps_v = sp.ps("ps_v", [P, FULL, D])
            ps_s = [sp.ps(f"ps_s{s}", [P, BANK]) for s in range(2)]
            ps_t = [sp.ps(f"ps_t{s}", [P, GROUPS * P]) for s in range(2)]
            ps_o = sp.ps("ps_o", [P, BANK])
            names = ("loaded", "ctx_loaded0", "ctx_loaded1", "zeroed", "end_made", "end_copied", "end_placed", "q_masked",
                     "k_made", "v_made", "k_copied", "v_copied", "scored", "maxed", "negated", "exps", "turned", "t_copied",
                     "summed", "attended", "extracted", "act_acc", "dve_acc")
            sems = {n: sp.sem(n) for n in names}
            (loaded, ctx_loaded0, ctx_loaded1, zeroed, end_made, end_copied, end_placed, q_masked,
             k_made, v_made, k_copied, v_copied, scored, maxed, negated, exps, turned, t_copied,
             summed, attended, extracted, act_acc, dve_acc) = (sems[n] for n in names)
            ctx_loaded = (ctx_loaded0, ctx_loaded1)
            with sp.block() as block:

                @block.sync
                def _(sync):
                    sync.dma_start(ends[:, :, :], A["ctx_ends"]).then_inc(loaded, 16)
                    sync.dma_start(w[:, :, :], A["L0_xattn_Wkv"]).then_inc(loaded, 16)
                    sync.dma_start(b_k[:, :], A["L0_xattn_b_k"]).then_inc(loaded, 16)
                    sync.dma_start(own[:, :], A["own4"]).then_inc(loaded, 16)
                    for s in range(2):
                        sync.dma_start(ctx_t[s][:, :, :], A["ctx_t"][s]).then_inc(ctx_loaded[s], 16)
                    sync.wait_ge(end_copied, 1)
                    sync.wait_ge(zeroed, 1)
                    for g in range(GROUPS):
                        sync.dma_start(v_end[g:g + 1, :, g * W:(g + 1) * W],
                                       v_end_rows[:, g * W:(g + 1) * W]).then_inc(end_placed, 16)
                    with sync.Fori(0, BATCH // 2 - 1) as i:
                        for s in range(2):
                            sync.wait_ge(v_made, i * 2 + (s + 1))
                            sync.dma_start(ctx_t[s][:, :, :], A["ctx_t"][i * 2 + (s + 2)]).then_inc(ctx_loaded[s], 16)

                @block.gpsimd
                def _(pool):
                    nc.gpsimd.memset(v_end[:, :, :], 0.0).then_inc(zeroed, 1)
                    pool.wait_ge(loaded, 64)

                    def front(t, i, s):
                        s = s % 2
                        pool.wait_ge(scored, t * GROUPS + GROUPS)
                        nc.gpsimd.tensor_tensor(
                            q_own[s][:, :, :].rearrange("p c (h q) -> p c h q", q=SEQ),
                            Q[:, :, bass.ds(t * SEQ, SEQ)].rearrange("p c (o q) -> p c o q", o=1).to_broadcast([P, KT, HPC, SEQ]),
                            own[:, :].rearrange("p (c h o) -> p c h o", c=1, o=1).to_broadcast([P, KT, HPC, SEQ]),
                            ALU.mult).then_inc(q_masked, 1)

                    pipelined(pool, BATCH, front, nothing)

                @block.tensor
                def _(pe):
                    pe.wait_ge(loaded, 64)
                    pe.sem_inc(scored, 2 * GROUPS)
                    pe.sem_inc(attended, 2)
                    for c in range(KT):
                        last = nc.tensor.matmul(ps_o[0:BATCH, 0:D], ends[:, c, :], w[:, c, D:2 * D],
                                                start=(c == 0), stop=(c == KT - 1))
                    last.then_inc(end_made, 1)
                    pe.wait_ge(end_copied, 1)
                    pe.wait_ge(end_placed, 64)

                    def front(t, i, s):
                        s = s % 2
                        pe.wait_ge(ctx_loaded[s], i * 16 + 16)
                        pe.wait_ge(k_copied, t + 1)
                        for m in range(KT):
                            for c in range(KT):
                                last = nc.tensor.matmul(ps_k[:, m, 0:CTX], w[:, c, m * P:(m + 1) * P], ctx_t[s][:, c, :],
                                                        start=(c == 0), stop=(c == KT - 1))
                        last.then_inc(k_made, 1)
                        pe.wait_ge(v_copied, t + 1)
                        for n in range(FULL):
                            for c in range(KT):
                                last = nc.tensor.matmul(ps_v[:, n, :], ctx_t[s][:, c, n * P:(n + 1) * P], w[:, c, D:2 * D],
                                                        start=(c == 0), stop=(c == KT - 1))
                        last.then_inc(v_made, 1)

                    def score(t, s, g):
                        s = s % 2
                        if g == 0:
                            pe.wait_ge(k_copied, t + 2)
                            pe.wait_ge(q_masked, t + 1)
                        pe.wait_ge(exps, t * GROUPS + (g + 1))
                        at = (g * P) % (HPC * SEQ)
                        nc.tensor.matmul(ps_s[g % 2][:, 0:CTX], q_own[s][:, g * HPG // HPC, at:at + P],
                                         k_t[s][:, g * HPG // HPC, :], start=True, stop=True).then_inc(scored, 1)

                    def transposes(t, s):
                        s = s % 2
                        pe.wait_ge(exps, t * GROUPS + (GROUPS + 2))
                        pe.wait_ge(t_copied, t * (FULL + 1) + (FULL + 1))
                        for n in range(FULL):
                            for g in range(GROUPS):
                                last = nc.tensor.transpose(ps_t[n % 2][:, g * P:(g + 1) * P],
                                                           probs[s][:, g, n * P:(n + 1) * P], ident[:, :])
                            last.then_inc(turned, 1)

                    def end_transpose(t, s):
                        s = s % 2
                        pe.wait_ge(t_copied, t * (FULL + 1) + (FULL + 2))
                        nc.tensor.transpose(ps_t[0][0:GROUPS, 0:P], probs[s][:, :, CTX - 1], ident[:, :]).then_inc(turned, 1)

                    def values(t, s):
                        s = s % 2
                        pe.wait_ge(t_copied, t * (FULL + 1) + 2 * (FULL + 1))
                        pe.wait_ge(extracted, t + 1)
                        nc.tensor.matmul(ps_o[:, 0:D], end_t[:, :], v_end[:, bass.ds(t, 1), :].rearrange("g o d -> g (o d)"),
                                         start=True, stop=False, skip_group_check=True)
                        for g in range(GROUPS):
                            for n in range(FULL):
                                last = nc.tensor.matmul(ps_o[:, g * W:(g + 1) * W], probs_t[:, n, g * P:(g + 1) * P],
                                                        v[s][:, n, g * W:(g + 1) * W], start=False,
                                                        stop=(n == FULL - 1), skip_group_check=True)
                        last.then_inc(attended, 1)

                    def scores_of(t, s, groups):
                        for g in groups:
                            score(t, s, g)

                    front(0, 0, 0)
                    scores_of(0, 0, range(GROUPS))

                    def turn(i, steps):
                        for k in range(2):
                            t = i * 2 + k
                            nxt, ni, nk = i * 2 + (k + 1), i + (k + 1) // 2, (k + 1) % 2
                            if k < steps:
                                front(nxt, ni, nk)
                            transposes(t, k)
                            if k < steps:
                                scores_of(nxt, nk, range(2))
                            end_transpose(t, k)
                            if k < steps:
                                scores_of(nxt, nk, range(2, GROUPS))
                            values(t, k)

                    with pe.Fori(0, BATCH // 2 - 1) as i:
                        turn(i, 2)
                    turn(BATCH // 2 - 1, 1)

                @block.scalar
                def _(act):
                    act.wait_ge(loaded, 64)
                    act.sem_inc(k_copied, 1)
                    act.sem_inc(v_copied, 1)
                    act.sem_inc(t_copied, FULL + 1)
                    act.sem_inc(exps, 2)
                    act.wait_ge(end_made, 1)
                    nc.scalar.copy(v_end_rows[:, :], ps_o[0:BATCH, 0:D]).then_inc(end_copied, 1)

                    def take_kv(t, s):
                        act.wait_ge(k_made, t + 1)
                        act.wait_ge(scored, t * GROUPS + GROUPS)
                        for c in range(KT):
                            nc.scalar.activation(k_t[s][:, c, :], ps_k[:, c, 0:CTX], ACT.Identity,
                                                 bias=b_k[:, c:c + 1]).then_inc(k_copied if c == KT - 1 else act_acc, 1)
                        act.wait_ge(v_made, t + 1)
                        act.wait_ge(attended, t + 1)
                        nc.scalar.copy(v[s][:, :, :], ps_v[:, :, :]).then_inc(v_copied, 1)

                    def exp(t, s, groups):
                        for g in groups:
                            act.wait_ge(negated, t * GROUPS + (g + 1))
                            nc.scalar.activation(probs[s][:, g, :], ps_s[g % 2][:, 0:CTX], ACT.Exp, bias=row[s][:, 1, g:g + 1],
                                                 accum_out=row[s][:, 2, g:g + 1]).then_inc(exps, 1)

                    def take_turned(t, n):
                        act.wait_ge(turned, t * (FULL + 1) + (n + 1))
                        if n == 0:
                            act.wait_ge(attended, t + 2)
                        if n < FULL:
                            nc.scalar.copy(probs_t[:, n, :], ps_t[n % 2][:, :]).then_inc(t_copied, 1)
                        else:
                            nc.scalar.copy(end_t[:, :], ps_t[0][0:GROUPS, 0:P]).then_inc(t_copied, 1)

                    take_kv(0, 0)
                    exp(0, 0, range(GROUPS))

                    def turn(i, steps):
                        for k in range(2):
                            t, nxt, nk = i * 2 + k, i * 2 + (k + 1), (k + 1) % 2
                            if k < steps:
                                take_kv(nxt, nk)
                            for n in range(FULL):
                                take_turned(t, n)
                            if k < steps:
                                exp(nxt, nk, range(2))
                            take_turned(t, FULL)
                            if k < steps:
                                exp(nxt, nk, range(2, GROUPS))

                    with act.Fori(0, BATCH // 2 - 1) as i:
                        turn(i, 2)
                    turn(BATCH // 2 - 1, 1)

                @block.vector
                def _(dve):
                    dve.sem_inc(extracted, 1)

                    def front(t, i, s):
                        r = row[s % 2]
                        for g in range(GROUPS):
                            dve.wait_ge(scored, t * GROUPS + (2 * GROUPS + g + 1))
                            nc.vector.tensor_reduce(r[:, 0, g:g + 1], ps_s[g % 2][:, 0:CTX], AX.X, ALU.max).then_inc(maxed, 1)
                            dve.wait_ge(maxed, t * GROUPS + (g + 1))
                            nc.vector.tensor_scalar(r[:, 1, g:g + 1], r[:, 0, g:g + 1], -1.0, None,
                                                    ALU.mult).then_inc(negated, 1)

                    def back(t, i, s):
                        r = row[s % 2]
                        dve.wait_ge(exps, t * GROUPS + (GROUPS + 2))
                        nc.vector.reciprocal(r[:, 3, :], r[:, 2, :]).then_inc(summed, 1)
                        dve.wait_ge(summed, t + 1)
                        dve.wait_ge(attended, t + 3)
                        for h in range(HPG):
                            rows = slice(h * SEQ, (h + 1) * SEQ)
                            out = attended_rows[s * SEQ:(s + 1) * SEQ, bass.ds(i, 1), :].rearrange(
                                "p o (g h d) -> p (o g) h d", g=GROUPS, h=HPG)[:, :, h, :]
                            nc.vector.tensor_tensor(
                                out, ps_o[rows, 0:D].rearrange("p (g h d) -> p g h d", g=GROUPS, h=HPG)[:, :, h, :],
                                r[rows, 3, :].rearrange("p (g o) -> p g o", o=1).to_broadcast([SEQ, GROUPS, HD]),
                                ALU.mult).then_inc(extracted if h == HPG - 1 else dve_acc, 1)

                    pipelined(dve, BATCH, front, back, BPT)

        project_rows(nc, "cross0_out", X, attended_rows, ident, A["L0_xattn_Wo"], A["L0_xattn_b_v"], A["L0_xattn_b_o"])


SUBLAYERS[0] = cross_attention_0


def latent_rows(nc, A, X, LT, ident, tail):
    SLOTS = TILES + 1
    with Space(nc, "latents") as sp:
        affine = sp.sb("affine", [P, 4, D])
        rows = sp.sb("rows", [P, SLOTS, D])
        final = sp.sb("final", [P, SLOTS, D])
        stats = [sp.sb(f"stats{k}", [P, n, 6]) for k, n in ((0, TILES), (1, SLOTS))]
        tmp = [sp.sb(f"tmp{k}", [P, 7, n]) for k, n in ((0, TILES), (1, SLOTS))]
        mean = [sp.sb(f"mean{k}", [P, n]) for k, n in ((0, TILES), (1, SLOTS))]
        rstd = [sp.sb(f"rstd{k}", [P, n]) for k, n in ((0, TILES), (1, SLOTS))]
        turned = [sp.ps(f"turned{k}", [P, BANK]) for k in range(2)]
        step, loaded, zeroed, stats_ready, var_ready, root_ready, rows_normed, final_ready, turned_made, copied, stored = (
            sp.sem(n) for n in ("step", "loaded", "zeroed", "stats_ready", "var_ready", "root_ready", "rows_normed",
                                "final_ready", "turned_made", "copied", "stored"))
        with sp.block() as block:

            @block.sync
            def _(sync):
                sync.dma_start(affine[:, :, :], A["affine"]).then_inc(loaded, 16)
                sync.wait_ge(zeroed, 1)
                sync.dma_start(rows[0:BATCH, TILES, :], A["ctx"][:, CTX - 1, :]).then_inc(loaded, 16)
                for t in range(TILES):
                    sync.wait_ge(final_ready, t + 1)
                    sync.dma_start(tail[t * BPT:(t + 1) * BPT, 0:SEQ, :], final[:, t, :]).then_inc(stored, 16)
                sync.wait_ge(final_ready, SLOTS)
                sync.dma_start(tail[:, SEQ, :], final[0:BATCH, TILES, :]).then_inc(stored, 16)
                sync.wait_ge(stored, 16 * SLOTS)

            @block.gpsimd
            def _(pool):
                nc.gpsimd.memset(rows[:, TILES, :], 0.0).then_inc(zeroed, 1)

            @block.scalar
            def _(act):
                for k in range(2):
                    act.wait_ge(var_ready, k + 1)
                    nc.scalar.activation(tmp[k][:, 6, :], tmp[k][:, 5, :], ACT.Sqrt).then_inc(root_ready, 1)
                for t in range(0, TILES, 2):
                    act.wait_ge(turned_made, t // 2 + 1)
                    nc.scalar.copy(LT[:, :, t * P:(t + 2) * P],
                                   turned[t // 2 % 2][:, :].rearrange("p (c n) -> p c n", c=KT)).then_inc(copied, 1)

            @block.vector
            def _(dve):
                chain = Chain(dve, step)
                v = nc.vector
                with dve.Fori(0, TILES) as t:
                    v.bn_stats(stats[0][:, t, :], X[:, t, :]).then_inc(stats_ready, 1)
                dve.wait_ge(stats_ready, TILES)
                norm_moments(dve, stats[0], tmp[0], mean[0][:, :], chain, var_ready)
                dve.wait_ge(root_ready, 1)
                chain.link(v.reciprocal(rstd[0][:, :], tmp[0][:, 6, :]))
                with dve.Fori(0, TILES) as t:
                    v.tensor_scalar(rows[:, t, :], X[:, t, :], mean[0][:, bass.ds(t, 1)], rstd[0][:, bass.ds(t, 1)],
                                    ALU.subtract, ALU.mult).then_inc(rows_normed, 1)
                dve.wait_ge(rows_normed, TILES)
                dve.wait_ge(loaded, 32)
                with dve.Fori(0, SLOTS) as t:
                    v.bn_stats(stats[1][:, t, :], rows[:, t, :]).then_inc(stats_ready, 1)
                dve.wait_ge(stats_ready, TILES + SLOTS)
                norm_moments(dve, stats[1], tmp[1], mean[1][:, :], chain, var_ready)
                dve.wait_ge(root_ready, 2)
                chain.link(v.reciprocal(rstd[1][:, :], tmp[1][:, 6, :]))
                for t in range(SLOTS):
                    gain = 0 if t < TILES else 2
                    chain.link(v.tensor_scalar(rows[:, t, :], rows[:, t, :], mean[1][:, t:t + 1], rstd[1][:, t:t + 1],
                                               ALU.subtract, ALU.mult))
                    chain.link(v.tensor_tensor(rows[:, t, :], rows[:, t, :], affine[:, gain, :], ALU.mult))
                    v.tensor_tensor(final[:, t, :], rows[:, t, :], affine[:, gain + 1, :], ALU.add).then_inc(final_ready, 1)

            @block.tensor
            def _(pe):
                for t in range(0, TILES, 2):
                    pe.wait_ge(final_ready, t + 2)
                    if t >= 4:
                        pe.wait_ge(copied, t // 2 - 1)
                    for n in range(2):
                        for c in range(KT):
                            last = nc.tensor.transpose(turned[t // 2 % 2][:, (2 * c + n) * P:(2 * c + n + 1) * P],
                                                       final[:, t + n, c * P:(c + 1) * P], ident[:, :])
                    last.then_inc(turned_made, 1)


def cross_attention_1(nc, A, X, LT, ident):
    HD = 64
    INNER = HEADS * HD
    CH = INNER // P
    TAIL = SEQ + 1
    FULL = CTX // P
    KEYS = FULL * P + TAIL
    NT = FULL + 1
    tail = nc.dram_tensor("tail_rows", (BATCH, TAIL, D), F32, kind="Internal").ap()
    latent_rows(nc, A, X, LT, ident, tail)
    with Space(nc, "cross1") as sp:
        wq = sp.sb("wq", [P, KT, INNER])
        wk_t = sp.sb("wk_t", [P, CH, D])
        wv = sp.sb("wv", [P, KT, INNER])
        wo = sp.sb("wo", [P, CH, D])
        affine = sp.sb("affine", [P, 2, KT * D])
        minus_half = sp.sb("minus_half", [P, FULL])
        raw = [sp.sb(f"raw{s}", [P, FULL, D]) for s in range(4)]
        kv = [sp.sb(f"kv{s}", [P, NT, D]) for s in range(4)]
        kv_t = [sp.sb(f"kv_t{s}", [P, KT, KEYS]) for s in range(2)]
        stats = sp.sb("stats", [P, FULL, 6])
        tmp = sp.sb("tmp", [P, 7, FULL])
        mean = sp.sb("mean", [P, FULL])
        q_t = sp.sb("q_t", [P, CH, P])
        q_keys = sp.sb("q_keys", [P, KT, BPT, HEADS * SEQ])
        probs = [sp.sb(f"probs{s}", [P, GROUPS, NT * P]) for s in range(2)]
        probs_t = sp.sb("probs_t", [P, NT, GROUPS * P])
        row = [sp.sb(f"row{s}", [P, 4, GROUPS]) for s in range(2)]
        z_t = sp.sb("z_t", [P, KT, HEADS, BPT, SEQ])
        out_t = sp.sb("out_t", [P, CH, P])
        ps_x = sp.ps("ps_x", [P, 2, BANK])
        ps_s = [sp.ps(f"ps_s{s}", [P, BANK]) for s in range(2)]
        ps_t = [sp.ps(f"ps_t{s}", [P, GROUPS * P]) for s in range(2)]
        ps_z = sp.ps("ps_z", [P, 2, BANK])
        names = ("loaded", "half_ready", "var_ready", "roots", "normed", "gained", "scaled", "kv_turned", "kv_copied",
                 "scored", "maxed", "negated", "exps", "summed", "p_scaled", "p_ready", "turned", "t_copied", "z_made", "z_copied",
                 "q_made", "q_copied", "qk_made", "qk_act", "qk_dve", "o_made", "o_copied", "y_made", "y_added", "step",
                 "stats_ready", "norm_acc", "zeroed")
        S = {n: sp.sem(n) for n in names}
        raw_loaded = [sp.sem(f"raw_loaded{s}") for s in range(4)]
        tail_loaded = [sp.sem(f"tail_loaded{s}") for s in range(4)]

        def schedule(engine, prologue, norm, front_back, tile_front, tile_back):
            def call(f, *a):
                if f:
                    f(*a)

            call(norm, 0, 0, 0)
            call(norm, 1, 0, 1)
            call(tile_front, 0)
            call(prologue)

            def turn(i, last):
                for k in range(BPT):
                    if not (last and k >= BPT - 2):
                        call(norm, i * BPT + (k + 2), i + (k + 2) // BPT, (k + 2) % BPT)
                    call(front_back, i * BPT + k, i, k, not (last and k == BPT - 1))
                    if k == BPT - 2 and not last:
                        call(tile_front, i + 1)
                call(tile_back, i)

            with engine.Fori(0, TILES - 1) as i:
                turn(i, False)
            turn(TILES - 1, True)

        def take_qk(copy, ps, r, odd, sem):
            for c in range(KT):
                src = ps[:, odd, 2 * c * P:(2 * c + 2) * P].rearrange("p (j b q) -> p j b q", j=2, q=SEQ)
                dst = q_keys[:, c, :, :].rearrange("p b (r j o q) -> p r o j b q", r=4, j=2, o=2)[:, r, odd, :, :, :]
                copy(dst, src).then_inc(sem, 1)

        with sp.block() as block:

            @block.sync
            def _(sync):
                for k, name in ((0, "L1_xattn_Wq"), (1, "L1_xattn_WkT"), (2, "L1_xattn_Wv"), (3, "L1_xattn_Wo")):
                    dst = (wq, wk_t, wv, wo)[k]
                    sync.dma_start(dst[:, :, :], A[name]).then_inc(S["loaded"], 16)
                sync.dma_start(affine[:, :, :].rearrange("p a (n d) -> p a n d", n=KT), A["ctx_affine"]).then_inc(S["loaded"], 16)

                def load(t, s):
                    sync.dma_start(raw[s][:, :, :], A["ctx"][t, 0:FULL * P, :].rearrange("(n p) d -> p n d", p=P)
                                   ).then_inc(raw_loaded[s], 16)
                    sync.dma_start(kv[s][0:TAIL, FULL, :], tail[t]).then_inc(tail_loaded[s], 16)

                for s in range(4):
                    load(s, s)
                with sync.Fori(0, BATCH // 4 - 1) as i:
                    for s in range(4):
                        sync.wait_ge(S["z_made"], i * 4 + (s + 1 + 4))
                        load(i * 4 + (s + 4), s)

            @block.gpsimd
            def _(pool):
                for s in range(2):
                    nc.gpsimd.memset(probs[s][:, :, KEYS:], 0.0).then_inc(S["zeroed"], 1)
                nc.gpsimd.memset(minus_half[:, :], -0.5).then_inc(S["half_ready"], 1)
                pool.wait_ge(S["half_ready"], 1)
                pool.wait_ge(S["loaded"], 16 * 5)

                def norm(t, i, s):
                    pool.wait_ge(S["var_ready"], t + 1)
                    nc.gpsimd.tensor_tensor(tmp[:, 6, :], tmp[:, 5, :], minus_half[:, :], ALU.pow).then_inc(S["roots"], 1)
                    pool.wait_ge(S["normed"], t + 1)
                    rows = kv[s][:, 0:FULL, :].rearrange("p n d -> p (n d)")
                    nc.gpsimd.tensor_tensor(rows, rows, affine[:, 0, :], ALU.mult).then_inc(S["gained"], 1)
                    pool.wait_ge(S["gained"], t + 1)
                    nc.gpsimd.tensor_tensor(rows, rows, affine[:, 1, :], ALU.add).then_inc(S["scaled"], 1)

                schedule(pool, None, norm, None, None, None)

            @block.tensor
            def _(pe):
                pe.wait_ge(S["loaded"], 16 * 5)
                pe.wait_ge(S["zeroed"], 2)
                pe.sem_inc(S["scored"], 2 * GROUPS)
                pe.sem_inc(S["z_made"], 4)

                def turn_kv(t, i, s4):
                    pe.wait_ge(S["scaled"], t + 1)
                    pe.wait_ge(tail_loaded[s4], i * 16 + 16)
                    pe.wait_ge(S["kv_copied"], t + 1)
                    pe.wait_ge(S["qk_act"], i * 8 + 8)
                    pe.wait_ge(S["qk_dve"], i * 8 + 8)
                    if s4 != 0:
                        pe.wait_ge(S["o_copied"], i + 1)
                    for c in range(KT):
                        for n in range(NT):
                            k = P if n < FULL else TAIL
                            last = nc.tensor.transpose(ps_x[:, c, n * P:n * P + k], kv[s4][0:k, n, c * P:(c + 1) * P],
                                                       ident[0:k, 0:k])
                    last.then_inc(S["kv_turned"], 1)

                def score(t, s2, s4, groups):
                    for g in groups:
                        if g == 0:
                            pe.wait_ge(S["kv_copied"], t + 2)
                        pe.wait_ge(S["exps"], t * GROUPS + (g + 1))
                        for c in range(KT):
                            last = nc.tensor.matmul(ps_s[g % 2][:, 0:KEYS], q_keys[:, c, s4, g * P:(g + 1) * P],
                                                    kv_t[s2][:, c, :], start=(c == 0), stop=(c == KT - 1))
                        last.then_inc(S["scored"], 1)

                def turn_probs(t, s2, tiles):
                    for n in tiles:
                        if n == 0:
                            pe.wait_ge(S["p_ready"], t + 1)
                            pe.wait_ge(S["t_copied"], t * NT + NT)
                        if n == 2:
                            pe.wait_ge(S["t_copied"], t * NT + (NT + 1))
                        for g in range(GROUPS):
                            last = nc.tensor.transpose(ps_t[n % 2][:, g * P:(g + 1) * P],
                                                       probs[s2][:, g, n * P:(n + 1) * P], ident[:, :])
                        last.then_inc(S["turned"], 1)

                def attend(t, i, s4):
                    pe.wait_ge(S["t_copied"], t * NT + 2 * NT)
                    pe.wait_ge(S["z_copied"], t + 1)
                    pe.wait_ge(S["y_added"], i + 1)
                    for c in range(KT):
                        for n in range(NT):
                            k = P if n < FULL else TAIL
                            last = nc.tensor.matmul(ps_z[:, c, :], kv[s4][0:k, n, c * P:(c + 1) * P], probs_t[0:k, n, :],
                                                    start=(n == 0), stop=(n == NT - 1))
                    last.then_inc(S["z_made"], 1)

                def prologue():
                    turn_kv(0, 0, 0)
                    score(0, 0, 0, range(GROUPS))

                def front_back(t, i, k, ahead):
                    s2, n2, n4, ni = k % 2, (k + 1) % 2, (k + 1) % 4, i + (k + 1) // 4
                    nt = t + 1 if isinstance(t, int) else i * BPT + (k + 1)
                    if ahead:
                        turn_kv(nt, ni, n4)
                    turn_probs(t, s2, range(FULL))
                    if ahead:
                        score(nt, n2, n4, (0, 1))
                    turn_probs(t, s2, (FULL,))
                    if ahead:
                        score(nt, n2, n4, (2, 3))
                    attend(t, i, k)

                def tile_front(i):
                    first = isinstance(i, int) and i == 0
                    if not first:
                        pe.wait_ge(S["kv_copied"], i * BPT + 1)
                    for m in range(CH):
                        for c in range(KT):
                            last = nc.tensor.matmul(ps_x[:, m // 4, (m % 4) * P:(m % 4 + 1) * P], wq[:, c, m * P:(m + 1) * P],
                                                    LT[:, c, bass.ds(i * P, P)], start=(c == 0), stop=(c == KT - 1))
                    last.then_inc(S["q_made"], 1)
                    pe.wait_ge(S["q_copied"], i + 1)
                    for r in range(4):
                        ps = ps_x if r % 2 else ps_z
                        if r == 0 and not first:
                            pe.wait_ge(S["z_copied"], i * BPT)
                        if r >= 2:
                            pe.wait_ge(S["qk_act"], i * 8 + 2 * (r - 1))
                            pe.wait_ge(S["qk_dve"], i * 8 + 2 * (r - 1))
                        for j in range(2):
                            for c in range(KT):
                                for odd in range(2):
                                    half = slice(64 * odd, 64 * odd + 64)
                                    last = nc.tensor.matmul(ps[:, odd, (2 * c + j) * P:(2 * c + j + 1) * P],
                                                            wk_t[half, 2 * r + j, c * P:(c + 1) * P], q_t[half, 2 * r + j, :],
                                                            start=True, stop=True)
                        last.then_inc(S["qk_made"], 1)

                def tile_back(i):
                    pe.wait_ge(S["z_copied"], i * BPT + (BPT + 1))
                    if not (isinstance(i, int) and i == TILES - 1):
                        pe.wait_ge(S["kv_copied"], i * BPT + (BPT + 2))
                    for h in range(HEADS):
                        half = slice(64 * (h % 2), 64 * (h % 2) + 64)
                        for c in range(KT):
                            last = nc.tensor.matmul(ps_x[half, h // 8, (h // 2 % 4) * P:(h // 2 % 4 + 1) * P],
                                                    wv[:, c, h * HD:(h + 1) * HD],
                                                    z_t[:, c, h, :, :].rearrange("p b q -> p (b q)"),
                                                    start=(c == 0), stop=(c == KT - 1))
                    last.then_inc(S["o_made"], 1)
                    pe.wait_ge(S["o_copied"], i + 2)
                    for m in range(CH):
                        last = nc.tensor.matmul(ps_z[:, 0, 0:D], out_t[:, m, :], wo[:, m, :], start=(m == 0), stop=(m == CH - 1))
                    last.then_inc(S["y_made"], 1)

                schedule(pe, prologue, None, front_back, tile_front, tile_back)

            @block.scalar
            def _(act):
                act.sem_inc(S["kv_copied"], 1)
                act.sem_inc(S["t_copied"], NT)
                act.sem_inc(S["exps"], 2)
                act.sem_inc(S["o_copied"], 1)

                def take_kv(t, s2):
                    act.wait_ge(S["kv_turned"], t + 1)
                    act.wait_ge(S["scored"], t * GROUPS + GROUPS)
                    nc.scalar.copy(kv_t[s2][:, :, :], ps_x[:, :, 0:KEYS]).then_inc(S["kv_copied"], 1)

                def exp(t, s2, groups):
                    for g in groups:
                        act.wait_ge(S["negated"], t * GROUPS + (g + 1))
                        nc.scalar.activation(probs[s2][:, g, 0:KEYS], ps_s[g % 2][:, 0:KEYS], ACT.Exp, bias=row[s2][:, 1, g:g + 1],
                                             accum_out=row[s2][:, 2, g:g + 1]).then_inc(S["exps"], 1)

                def take_turned(t, n):
                    act.wait_ge(S["turned"], t * NT + (n + 1))
                    if n == 0:
                        act.wait_ge(S["z_made"], t + 4)
                    k = P if n < FULL else TAIL
                    nc.scalar.copy(probs_t[0:k, n, :], ps_t[n % 2][0:k, :]).then_inc(S["t_copied"], 1)

                def prologue():
                    take_kv(0, 0)
                    exp(0, 0, range(GROUPS))

                def front_back(t, i, k, ahead):
                    s2, n2 = k % 2, (k + 1) % 2
                    nt = i * BPT + (k + 1)
                    if ahead:
                        take_kv(nt, n2)
                    take_turned(t, 0)
                    take_turned(t, 1)
                    if ahead:
                        exp(nt, n2, (0, 1))
                    take_turned(t, 2)
                    if ahead:
                        exp(nt, n2, (2, 3))

                def tile_front(i):
                    act.wait_ge(S["q_made"], i + 1)
                    nc.scalar.activation(q_t[:, :, :].rearrange("p (a m) n -> p a (m n)", a=2), ps_x[:, :, :], ACT.Copy,
                                         scale=HD ** -0.5).then_inc(S["q_copied"], 1)
                    for r in range(4):
                        ps = ps_x if r % 2 else ps_z
                        act.wait_ge(S["qk_made"], i * 4 + (r + 1))
                        take_qk(nc.scalar.copy, ps, r, 0, S["qk_act"])

                def tile_back(i):
                    act.wait_ge(S["o_made"], i + 1)
                    nc.scalar.copy(out_t[:, :, :].rearrange("p (a m) n -> p a (m n)", a=2), ps_x[:, :, :]).then_inc(S["o_copied"], 1)

                schedule(act, prologue, None, front_back, tile_front, tile_back)

            @block.vector
            def _(dve):
                dve.wait_ge(S["loaded"], 16 * 5)
                dve.sem_inc(S["z_copied"], 1)
                dve.sem_inc(S["y_added"], 1)
                v = nc.vector

                def norm(t, i, s):
                    dve.wait_ge(raw_loaded[s], i * 16 + 16)
                    for n in range(FULL):
                        last = v.bn_stats(stats[:, n, :], raw[s][:, n, :]).then_inc(S["stats_ready"], 1)
                    dve.wait_ge(S["stats_ready"], t * FULL + FULL)
                    norm_moments(dve, stats, tmp, mean[:, :], Chain(dve, S["step"], t * MOMENT_LINKS), S["var_ready"])
                    dve.wait_ge(S["roots"], t + 1)
                    dve.wait_ge(S["z_made"], t + 1)
                    for n in range(FULL):
                        v.tensor_scalar(kv[s][:, n, :], raw[s][:, n, :], mean[:, n:n + 1], tmp[:, 6, n:n + 1],
                                        ALU.subtract, ALU.mult).then_inc(S["normed"] if n == FULL - 1 else S["norm_acc"], 1)

                def softmax(t, s2):
                    r = row[s2]
                    for g in range(GROUPS):
                        dve.wait_ge(S["scored"], t * GROUPS + (2 * GROUPS + g + 1))
                        v.tensor_reduce(r[:, 0, g:g + 1], ps_s[g % 2][:, 0:KEYS], AX.X, ALU.max).then_inc(S["maxed"], 1)
                        dve.wait_ge(S["maxed"], t * GROUPS + (g + 1))
                        v.tensor_scalar(r[:, 1, g:g + 1], r[:, 0, g:g + 1], -1.0, None, ALU.mult).then_inc(S["negated"], 1)
                    dve.wait_ge(S["exps"], t * GROUPS + (GROUPS + 2))
                    v.reciprocal(r[:, 3, :], r[:, 2, :]).then_inc(S["summed"], 1)
                    dve.wait_ge(S["summed"], t + 1)
                    for g in range(GROUPS):
                        v.tensor_scalar(probs[s2][:, g, 0:KEYS], probs[s2][:, g, 0:KEYS], r[:, 3, g:g + 1], None,
                                        ALU.mult).then_inc(S["p_ready"] if g == GROUPS - 1 else S["p_scaled"], 1)

                def prologue():
                    softmax(0, 0)

                def front_back(t, i, k, ahead):
                    if ahead:
                        softmax(i * BPT + (k + 1), (k + 1) % 2)
                    dve.wait_ge(S["z_made"], t + 5)
                    v.tensor_copy(z_t[:, :, :, k, :], ps_z[:, :, :].rearrange("p c (h q) -> p c h q", q=SEQ)
                                  ).then_inc(S["z_copied"], 1)

                def tile_front(i):
                    for r in range(4):
                        ps = ps_x if r % 2 else ps_z
                        dve.wait_ge(S["qk_made"], i * 4 + (r + 1))
                        take_qk(v.tensor_copy, ps, r, 1, S["qk_dve"])

                def tile_back(i):
                    dve.wait_ge(S["y_made"], i + 1)
                    v.tensor_tensor(X[:, bass.ds(i, 1), :].rearrange("p o d -> p (o d)"),
                                    X[:, bass.ds(i, 1), :].rearrange("p o d -> p (o d)"), ps_z[:, 0, 0:D],
                                    ALU.add).then_inc(S["y_added"], 1)

                schedule(dve, prologue, norm, front_back, tile_front, tile_back)


SUBLAYERS[3] = cross_attention_1


def mamba(nc, A, X, XT, ident):
    INNER, STATE, CONV, RANK = 2 * D, 16, 4, 16
    CH = INNER // P
    N = TOKENS // 2
    NQ = N // 2
    DBL = RANK + 2 * STATE
    with Space(nc, "mamba") as top:
        H = top.sb("H", [P, KT, TOKENS])
        project_queries(nc, A, XT, H, "mamba_fc1", A["L1_attn_fc1_w"], A["L1_attn_fc1_b"])
        decay = top.sb("decay", [P, CH, STATE])
        diag = top.sb("diag", [P, CH, P])
        w_out = top.sb("w_out", [P, CH, D])
        w_fc2 = top.sb("w_fc2", [P, KT, D])
        b_fc2 = top.sb("b_fc2", [1, D])
        ones = top.sb("ones", [1, P])
        with Space(nc, "mamba_set") as sp:
            a_log = sp.sb("a_log", [P, CH, STATE])
            d = sp.sb("d", [P, CH])
            loaded, exped, ones_set, done = (sp.sem(n) for n in ("loaded", "exped", "ones_set", "done"))
            with sp.block() as block:

                @block.sync
                def _(sync):
                    sync.dma_start(a_log[:, :, :], A["L1_attn_A_log"]).then_inc(loaded, 16)
                    sync.dma_start(d[:, :], A["L1_attn_D"]).then_inc(loaded, 16)
                    sync.dma_start(w_out[:, :, :], A["L1_attn_out_proj_w"]).then_inc(loaded, 16)
                    sync.dma_start(w_fc2[:, :, :], A["L1_attn_fc2_w"]).then_inc(loaded, 16)
                    sync.dma_start(b_fc2[:, :], A["L1_attn_fc2_b"]).then_inc(loaded, 16)
                    sync.wait_ge(loaded, 80)

                @block.gpsimd
                def _(pool):
                    nc.gpsimd.memset(ones[:, :], 1.0).then_inc(ones_set, 1)

                @block.scalar
                def _(act):
                    act.wait_ge(loaded, 80)
                    nc.scalar.activation(a_log[:, :, :], a_log[:, :, :], ACT.Exp).then_inc(exped, 1)

                @block.vector
                def _(dve):
                    dve.wait_ge(loaded, 80)
                    for c in range(CH):
                        nc.vector.tensor_scalar(diag[:, c, :], ident[:, :], d[:, c:c + 1], None, ALU.mult).then_inc(done, 1)
                    dve.wait_ge(exped, 1)
                    nc.vector.tensor_scalar(decay[:, :, :], a_log[:, :, :], -1.0, None, ALU.mult).then_inc(done, 1)

        for half in range(2):
            with Space(nc, f"mamba{half}") as sp:
                u = sp.sb("u", [P, CH, N])
                dt = sp.sb("dt", [P, CH, N])
                dtu = sp.sb("dtu", [P, CH, N])
                gate = sp.sb("gate", [P, CH, N])
                x_dbl = sp.sb("x_dbl", [DBL, N])
                mamba_inputs(nc, A, H, half, u, dt, dtu, gate, x_dbl, INNER, CONV, RANK, DBL, CH, N)
                mamba_scan(nc, half, ident, decay, diag, u, dt, dtu, gate, x_dbl, STATE, RANK, DBL, CH, N, NQ)
                mamba_output(nc, half, X, gate, w_out, w_fc2, b_fc2, ones, CH, N)


def mamba_inputs(nc, A, H, half, u, dt, dtu, gate, x_dbl, INNER, CONV, RANK, DBL, CH, N):
    BS = 512
    with Space(nc, f"mamba{half}_in") as sp:
        w_in = sp.sb("w_in", [P, KT, 2 * INNER])
        w_x = sp.sb("w_x", [P, CH, DBL])
        w_dt = sp.sb("w_dt", [RANK, INNER])
        taps = sp.sb("taps", [P, CH, CONV])
        cols = sp.sb("cols", [P, 2, CH])
        one = sp.sb("one", [P, 1])
        xc = sp.sb("xc", [P, CH, N])
        e = sp.sb("e", [P, CH, N])
        conv = e
        lg = sp.sb("lg", [P, CH, N])
        ps = [sp.ps(f"ps{k}", [P, N]) for k in range(4)]
        loaded, one_set, made, taken, tap_step, conv_ready, u_ready, exp_ready, log_ready, acc, step = (
            sp.sem(n) for n in ("loaded", "one_set", "made", "taken", "tap_step", "conv_ready", "u_ready", "exp_ready",
                                "log_ready", "acc", "step"))
        with sp.block() as block:

            @block.sync
            def _(sync):
                sync.dma_start(w_in[:, :, :], A["L1_attn_in_proj_w"]).then_inc(loaded, 16)
                sync.dma_start(w_x[:, :, :], A["L1_attn_x_proj_w"]).then_inc(loaded, 16)
                sync.dma_start(w_dt[:, :], A["L1_attn_dt_proj_w"]).then_inc(loaded, 16)
                sync.dma_start(taps[:, :, :], A["L1_attn_conv_w"]).then_inc(loaded, 16)
                sync.dma_start(cols[:, :, :], A["mamba_cols"]).then_inc(loaded, 16)

            @block.gpsimd
            def _(pool):
                nc.gpsimd.memset(one[:, :], 1.0).then_inc(one_set, 1)

            @block.tensor
            def _(pe):
                pe.wait_ge(loaded, 80)
                for g in range(3 * CH + 1):
                    if g >= 4:
                        pe.wait_ge(taken, g - 3)
                    if g == 2 * CH:
                        pe.wait_ge(u_ready, CH)
                    if g == 2 * CH + 1:
                        pe.wait_ge(taken, 2 * CH + 1)
                    for n in range(N // BS):
                        cut = slice(n * BS, (n + 1) * BS)
                        if g < 2 * CH:
                            for c in range(KT):
                                last = nc.tensor.matmul(ps[g % 4][:, cut], w_in[:, c, g * P:(g + 1) * P],
                                                        H[:, c, half * N + n * BS:half * N + (n + 1) * BS],
                                                        start=(c == 0), stop=(c == KT - 1))
                        elif g == 2 * CH:
                            for c in range(CH):
                                last = nc.tensor.matmul(ps[g % 4][0:DBL, cut], w_x[:, c, :], u[:, c, cut],
                                                        start=(c == 0), stop=(c == CH - 1))
                        else:
                            m = g - 2 * CH - 1
                            last = nc.tensor.matmul(ps[g % 4][:, cut], w_dt[:, m * P:(m + 1) * P], x_dbl[0:RANK, cut],
                                                    start=True, stop=True)
                    last.then_inc(made, 1)

            @block.scalar
            def _(act):
                act.wait_ge(loaded, 80)
                act.wait_ge(one_set, 1)
                for g in range(CH):
                    act.wait_ge(made, g + 1)
                    nc.scalar.copy(xc[:, g, :], ps[g % 4][:, :]).then_inc(taken, 1)
                for g in range(CH, 2 * CH):
                    act.wait_ge(made, g + 1)
                    nc.scalar.activation(gate[:, g - CH, :], ps[g % 4][:, :], ACT.Silu).then_inc(taken, 1)
                for c in range(CH):
                    act.wait_ge(conv_ready, c + 1)
                    nc.scalar.activation(u[:, c, :], conv[:, c, :], ACT.Silu, bias=cols[:, 0, c:c + 1]).then_inc(u_ready, 1)
                act.wait_ge(made, 2 * CH + 1)
                nc.scalar.copy(x_dbl[:, :], ps[2 * CH % 4][0:DBL, :]).then_inc(taken, 1)
                for c in range(CH):
                    g = 2 * CH + 1 + c
                    act.wait_ge(made, g + 1)
                    nc.scalar.activation(lg[:, c, :], ps[g % 4][:, :], ACT.Abs, bias=cols[:, 1, c:c + 1]).then_inc(acc, 1)
                    nc.scalar.activation(dt[:, c, :], ps[g % 4][:, :], ACT.Relu, bias=cols[:, 1, c:c + 1]).then_inc(taken, 1)
                act.wait_ge(acc, CH)
                nc.scalar.activation(e[:, :, :], lg[:, :, :], ACT.Exp, scale=-1.0).then_inc(exp_ready, 1)
                act.wait_ge(exp_ready, 1)
                nc.scalar.activation(lg[:, :, :], e[:, :, :], ACT.Ln, bias=one[:, 0:1]).then_inc(log_ready, 1)

            @block.vector
            def _(dve):
                dve.wait_ge(loaded, 80)
                chain = Chain(dve, tap_step)
                v = nc.vector
                seqs = lambda a: a.rearrange("p (b s) -> p b s", s=SEQ)
                for c in range(CH):
                    dve.wait_ge(taken, c + 1)
                    x, y = seqs(xc[:, c, :]), seqs(conv[:, c, :])
                    chain.link(v.tensor_scalar(y, x, taps[:, c, CONV - 1:CONV], None, ALU.mult))
                    for back in range(1, CONV):
                        last = v.scalar_tensor_tensor(y[:, :, back:], x[:, :, 0:SEQ - back], taps[:, c, CONV - 1 - back:CONV - back],
                                                      y[:, :, back:], ALU.mult, ALU.add)
                        if back < CONV - 1:
                            chain.link(last)
                    last.then_inc(conv_ready, 1)
                fix = Chain(dve, step)
                dve.wait_ge(exp_ready, 1)
                fix.link(v.tensor_scalar(xc[:, :, :], e[:, :, :], 1.0, 1.0, ALU.add, ALU.subtract))
                fix.link(v.tensor_tensor(xc[:, :, :], e[:, :, :], xc[:, :, :], ALU.subtract))
                dve.wait_ge(log_ready, 1)
                fix.link(v.tensor_tensor(xc[:, :, :], lg[:, :, :], xc[:, :, :], ALU.add))
                fix.link(v.tensor_tensor(dt[:, :, :], dt[:, :, :], xc[:, :, :], ALU.add))
                fix.link(v.tensor_tensor(dtu[:, :, :], dt[:, :, :], u[:, :, :], ALU.mult))


def mamba_scan(nc, half, ident, decay, diag, u, dt, dtu, gate, x_dbl, STATE, RANK, DBL, CH, N, NQ):
    UN = 2 * CH
    with Space(nc, f"mamba{half}_scan") as sp:
        pick = [sp.sb(f"pick{s}", [DBL, 2, P]) for s in range(2)]
        b_all = [sp.sb(f"b_all{s}", [P, NQ]) for s in range(2)]
        dec = [sp.sb(f"dec{s}", [P, NQ]) for s in range(2)]
        inp = [sp.sb(f"inp{s}", [P, NQ]) for s in range(2)]
        h = [sp.sb(f"h{s}", [P, NQ]) for s in range(4)]
        hc = [sp.sb(f"hc{s}", [P, NQ]) for s in range(2)]
        ps_b = [sp.ps(f"ps_b{s}", [P, NQ]) for s in range(2)]
        ps_c = [sp.ps(f"ps_c{s}", [P, NQ]) for s in range(2)]
        ps_y = sp.ps("ps_y", [P, CH, NQ])
        zeroed, picked, b_copied, spread, decayed, fed, scanned, weighed, summed, gated = (
            sp.sem(n) for n in ("zeroed", "picked", "b_copied", "spread", "decayed", "fed", "scanned", "weighed", "summed", "gated"))
        with sp.block() as block:

            @block.gpsimd
            def _(pool):
                for s in range(2):
                    nc.gpsimd.memset(dec[s][:, :], 0.0).then_inc(zeroed, 1)
                pool.sem_inc(fed, 2 * CH)
                for q in range(2):
                    def front(n, i, s):
                        n = n + q * STATE
                        pool.wait_ge(b_copied, n + 3)
                        for c in range(CH):
                            pool.wait_ge(scanned, n * CH + (c + 1))
                            nc.gpsimd.tensor_tensor(inp[c % 2][:, :], dtu[:, c, q * NQ:(q + 1) * NQ], b_all[s][:, :],
                                                    ALU.mult).then_inc(fed, 1)

                    pipelined(pool, STATE, front, nothing)

            @block.scalar
            def _(act):
                act.wait_ge(zeroed, 2)
                act.sem_inc(b_copied, 2)
                for q in range(2):
                    def copy_b(n, s):
                        g = n + q * STATE
                        act.wait_ge(spread, g + 3)
                        act.wait_ge(fed, g * CH + CH)
                        nc.scalar.copy(b_all[s][:, :], ps_b[s][:, :]).then_inc(b_copied, 1)

                    def front(n, i, s):
                        act.wait_ge(spread, n + (q * STATE + 1))
                        for k in range(2):
                            nc.scalar.copy(pick[s][:, k, :], ident[0:DBL, bass.ds(n + (RANK + k * STATE), 1)].to_broadcast([DBL, P])
                                           ).then_inc(picked, 1)
                        if isinstance(n, int) and n == 0:
                            copy_b(0, 0)

                    def back(n, i, s):
                        g = n + q * STATE
                        for c in range(CH):
                            if c == 2 and not (isinstance(n, int) and n == STATE - 1):
                                copy_b(i * 2 + (s + 1), (s + 1) % 2)
                            act.wait_ge(scanned, g * CH + (c + 1))
                            rows = dt[:, c, q * NQ:(q + 1) * NQ].rearrange("p (b s) -> p b s", s=SEQ)
                            nc.scalar.activation(dec[c % 2][:, :].rearrange("p (b s) -> p b s", s=SEQ)[:, :, 1:], rows[:, :, 1:],
                                                 ACT.Exp, scale=decay[:, c, bass.ds(n, 1)]).then_inc(decayed, 1)

                    pipelined(act, STATE, front, back)

            @block.tensor
            def _(pe):
                pe.sem_inc(spread, 2)
                pe.sem_inc(summed, 2)
                for q in range(2):
                    if q:
                        pe.wait_ge(gated, q * CH)
                    for c in range(CH):
                        nc.tensor.matmul(ps_y[:, c, :], diag[:, c, :], u[:, c, q * NQ:(q + 1) * NQ], start=True, stop=False,
                                         skip_group_check=True)

                    def front(n, i, s):
                        n = n + q * STATE
                        pe.wait_ge(picked, n * 2 + 2)
                        pe.wait_ge(b_copied, n + 1)
                        pe.wait_ge(weighed, n * CH + CH)
                        nc.tensor.matmul(ps_b[s][:, :], pick[s][:, 0, :], x_dbl[:, q * NQ:(q + 1) * NQ], start=True, stop=True)
                        nc.tensor.matmul(ps_c[s][:, :], pick[s][:, 1, :], x_dbl[:, q * NQ:(q + 1) * NQ], start=True, stop=True
                                         ).then_inc(spread, 1)

                    def back(n, i, s):
                        n = n + q * STATE
                        for c in range(CH):
                            pe.wait_ge(weighed, n * CH + (c + 1 + 2 * CH))
                            nc.tensor.matmul(ps_y[:, c, :], ident[:, :], hc[c % 2][:, :], start=False, stop=False,
                                             skip_group_check=True).then_inc(summed, 1)

                    pipelined(pe, STATE, front, back)

            @block.vector
            def _(dve):
                dve.sem_inc(scanned, 2)
                dve.sem_inc(weighed, 2 * CH)
                for q in range(2):
                    def scan(t, i, k):
                        g = t + q * STATE * CH
                        dve.wait_ge(decayed, g + 1)
                        dve.wait_ge(fed, g + (1 + 2 * CH))
                        dve.wait_ge(weighed, g + (1 + 2 * CH - 4))
                        nc.vector.tensor_tensor_scan(h[k % 4][:, :], dec[k % 2][:, :], inp[k % 2][:, :], 0.0, ALU.mult, ALU.add
                                                     ).then_inc(scanned, 1)

                    def weigh(t, i, k):
                        g = t + q * STATE * CH
                        dve.wait_ge(scanned, g + 3)
                        dve.wait_ge(summed, g + 1)
                        nc.vector.tensor_tensor(hc[k % 2][:, :], h[k % 4][:, :], ps_c[k // CH][:, :], ALU.mult).then_inc(weighed, 1)

                    pipelined(dve, STATE * CH, scan, weigh, UN)
                    dve.wait_ge(summed, (q + 1) * STATE * CH + 2)
                    for c in range(CH):
                        out = gate[:, c, q * NQ:(q + 1) * NQ]
                        nc.vector.tensor_tensor(out, out, ps_y[:, c, :], ALU.mult).then_inc(gated, 1)


def mamba_output(nc, half, X, gated, w_out, w_fc2, b_fc2, ones, CH, N):
    BS = 512
    with Space(nc, f"mamba{half}_out") as sp:
        mid = sp.sb("mid", [P, KT, N])
        ps_m = [sp.ps(f"ps_m{s}", [P, KT, BS]) for s in range(2)]
        ps_y = [sp.ps(f"ps_y{s}", [P, BANK]) for s in range(2)]
        made, copied, y_made, added = (sp.sem(n) for n in ("made", "copied", "y_made", "added"))
        with sp.block() as block:

            @block.tensor
            def _(pe):
                for n in range(N // BS):
                    for m in range(KT):
                        for c in range(CH):
                            last = nc.tensor.matmul(ps_m[n][:, m, :], w_out[:, c, m * P:(m + 1) * P],
                                                    gated[:, c, n * BS:(n + 1) * BS], start=(c == 0), stop=(c == CH - 1))
                    last.then_inc(made, 1)
                for t in range(N // P):
                    pe.wait_ge(copied, t * P // BS + 1)
                    if t >= 2:
                        pe.wait_ge(added, t - 1)
                    nc.tensor.matmul(ps_y[t % 2][:, 0:D], ones[:, :], b_fc2[:, :], start=True, stop=False)
                    for c in range(KT):
                        last = nc.tensor.matmul(ps_y[t % 2][:, 0:D], mid[:, c, t * P:(t + 1) * P], w_fc2[:, c, :],
                                                start=False, stop=(c == KT - 1))
                    last.then_inc(y_made, 1)

            @block.scalar
            def _(act):
                for n in range(N // BS):
                    act.wait_ge(made, n + 1)
                    nc.scalar.copy(mid[:, :, n * BS:(n + 1) * BS], ps_m[n][:, :, :]).then_inc(copied, 1)

            @block.vector
            def _(dve):
                for t in range(N // P):
                    tile = half * (N // P) + t
                    dve.wait_ge(y_made, t + 1)
                    nc.vector.tensor_tensor(X[:, tile, :], X[:, tile, :], ps_y[t % 2][:, 0:D], ALU.add).then_inc(added, 1)


SUBLAYERS[4] = mamba


def _by_partition(w):
    return w.reshape(-1, 128, w.shape[-1]).transpose(1, 0, 2)


def _expert_layout(w_gate, w_up, w_down, fp):
    e, f, d = w_gate.shape
    gu = np.concatenate([w_gate, w_up], axis=1).transpose(0, 2, 1).reshape(e, d // 128, 128, 2 * f).transpose(0, 2, 1, 3)
    dn = w_down.transpose(0, 2, 1).reshape(e, f // fp, fp, d).transpose(0, 2, 1, 3)
    return gu, dn


def _alibi():
    head = np.arange(HPG)[:, None, None, None] + HPG * np.arange(GROUPS)[None, None, :, None]
    query, key = np.arange(SEQ)[None, :, None, None], np.arange(SEQ)[None, None, None, :]
    slope = (1.0 / (2.0 ** 8) ** ((head + 1) / HEADS)).astype(np.float32)
    bias = np.where(key <= query, slope * (key - query).astype(np.float32), np.float32(NEG))
    return bias.astype(np.float32).reshape(P, GROUPS, SEQ)


def _own(width, value):
    return (np.arange(P)[:, None] // width == np.arange(P // width)).astype(np.float32) * np.float32(value)


def _lay_out(v):
    a = {"x": v["x"]}
    a["alibi"] = _alibi()
    a["own16"] = _own(16, 1 / 16)
    a["own4"] = _own(16, 1 / 4)
    ctx_t = v["ctx_1024"].transpose(0, 2, 1).reshape(BATCH, KT, P, CTX).transpose(0, 2, 1, 3)
    a["ctx_t"], a["ctx_ends"] = ctx_t, ctx_t[:, :, :, -1].transpose(1, 2, 0)
    for n in ("Wq", "Wo"):
        a[f"L0_xattn_{n}"] = _by_partition(v[f"L0_xattn_{n}"])
    a["L0_xattn_Wkv"] = _by_partition(np.concatenate([v["L0_xattn_Wk"], v["L0_xattn_Wv"]], axis=1))
    for n in ("b_q", "b_k", "b_v"):
        a[f"L0_xattn_{n}"] = v[f"L0_xattn_{n}"].reshape(KT, P).T
    a["L0_xattn_b_o"] = v["L0_xattn_b_o"].reshape(1, D)
    a["ctx"] = v["ctx_1024"]
    latent, context = (np.stack([v[f"L1_xattn_{n}_g"], v[f"L1_xattn_{n}_b"]]) for n in ("ln2", "ln1"))
    a["affine"] = np.broadcast_to(np.concatenate([latent, context]), (P, 4, D))
    a["ctx_affine"] = np.broadcast_to(context[:, None, :], (P, 2, 2, D))
    a["L1_xattn_Wq"], a["L1_xattn_Wo"] = _by_partition(v["L1_xattn_Wq"]), _by_partition(v["L1_xattn_Wo"])
    a["L1_xattn_WkT"] = _by_partition(v["L1_xattn_Wkv"][:, :1024].T)
    a["L1_xattn_Wv"] = _by_partition(v["L1_xattn_Wkv"][:, 1024:])
    for n in ("fc1", "in_proj", "x_proj", "out_proj", "fc2"):
        a[f"L1_attn_{n}_w"] = _by_partition(v[f"L1_attn_{n}_w"].T)
    a["L1_attn_dt_proj_w"] = v["L1_attn_dt_proj_w"].T
    a["L1_attn_fc1_b"], a["L1_attn_D"] = v["L1_attn_fc1_b"].reshape(-1, P).T, v["L1_attn_D"].reshape(-1, P).T
    a["L1_attn_fc2_b"] = v["L1_attn_fc2_b"].reshape(1, D)
    a["L1_attn_A_log"], a["L1_attn_conv_w"] = _by_partition(v["L1_attn_A_log"]), _by_partition(v["L1_attn_conv_w"])
    a["mamba_cols"] = np.stack([v["L1_attn_conv_b"].reshape(-1, P).T, v["L1_attn_dt_proj_b"].reshape(-1, P).T], axis=1)
    slot = np.arange(P, dtype=np.float32)
    a["codes"] = np.broadcast_to(HALF - np.arange(HALF, dtype=np.float32), (P, HALF))
    ends = [np.full(P, HALF), np.full(P, 2 * HALF), np.where(slot < REST, HALF, 2 * HALF)]
    a["slot_base"] = np.stack([e - TOKENS - slot for e in ends] + [TOKENS + slot], axis=1).astype(np.float32)
    a["L0_attn_w"] = _by_partition(v["L0_attn_W_kqv"].T)
    a["L0_ffn_gate_w"] = _by_partition(v["L0_ffn_gate_w"].T)
    a["L0_ffn_up"], a["L0_ffn_down"] = _expert_layout(v["L0_ffn_w_gate"], v["L0_ffn_w_up"], v["L0_ffn_w_down"], 96)
    a["L1_ffn_gate_w"] = _by_partition(v["L1_ffn_gate_w"].T)
    a["L1_ffn_up"], a["L1_ffn_down"] = _expert_layout(
        np.concatenate([v["L1_ffn_w1"], v["L1_ffn_sw1"][None]]), np.concatenate([v["L1_ffn_w3"], v["L1_ffn_sw3"][None]]),
        np.concatenate([v["L1_ffn_w2"], v["L1_ffn_sw2"][None]]), 128)
    return a


def kernel(**inputs):
    import concourse.bacc as bacc
    from concourse.bass_utils import run_bass_kernel_spmd

    arrays = {n: np.ascontiguousarray(a) for n, a in _lay_out({n: np.asarray(a) for n, a in inputs.items()}).items()}
    nc = bacc.Bacc("TRN2", target_bir_lowering=False, num_devices=1)
    aps = {n: nc.dram_tensor(f"in_{n}", a.shape, mybir.dt.from_np(a.dtype), kind="ExternalInput").ap() for n, a in arrays.items()}
    out = nc.dram_tensor("out", (BATCH, SEQ, D), F32, kind="ExternalOutput").ap()
    build_program(nc, aps, out)
    result = run_bass_kernel_spmd(nc, [{f"in_{n}": a for n, a in arrays.items()}], core_ids=[0])
    return result.results[0]["out"]
```

```python
import numpy as np
import concourse.bass as bass
from concourse import mybir
from contextlib import ExitStack

F32 = mybir.dt.float32
F32R = mybir.dt.float32r
ALU = mybir.AluOpType
ACT = mybir.ActivationFunctionType
AX = mybir.AxisListType

BATCH, SEQ, D = 64, 32, 256
CTX = 257
TOKENS = BATCH * SEQ
P = 128
TILES = TOKENS // P
BPT = P // SEQ
KT = D // P
BANK = 512
HEADS = 16
HPG = P // SEQ
GROUPS = HEADS // HPG
EPS = 1e-5
NEG = -1e30


class Chain:

    def __init__(self, engine, sem, base=0):
        self.engine, self.sem, self.base, self.n = engine, sem, base, 0

    def link(self, instruction):
        self.n += 1
        instruction.then_inc(self.sem, 1)
        self.engine.wait_ge(self.sem, self.base + self.n)


class Space:

    used = []

    def __init__(self, nc, stage):
        self.nc, self.stage, self.ctx = nc, stage, ExitStack()

    @classmethod
    def clear_used(cls, nc):
        nc.clear_and_free_semaphores(cls.used)
        cls.used = []
        nc.all_engine_barrier()

    def __enter__(self):
        return self

    def __exit__(self, *error):
        return self.ctx.__exit__(*error)

    def sb(self, name, shape, dt=F32):
        return self.ctx.enter_context(self.nc.sbuf_tensor(f"{self.stage}_{name}", shape, dt))

    def ps(self, name, shape, dt=F32):
        return self.ctx.enter_context(self.nc.psum_tensor(f"{self.stage}_{name}", shape, dt))

    def sem(self, name):
        self.used.append(self.nc.alloc_semaphore(f"{self.stage}_{name}"))
        return self.used[-1]

    def block(self):
        return self.nc.Block()


def load_state(nc, x, X, ident):
    with Space(nc, "load") as sp, sp.block() as block:
        loaded, zeroed = sp.sem("loaded"), sp.sem("zeroed")

        @block.sync
        def _(sync):
            rows = x.rearrange("b s d -> (b s) d").rearrange("(t p) d -> p t d", p=P)
            sync.dma_start(X[:, 0:TILES // 2, :], rows[:, 0:TILES // 2, :]).then_inc(loaded, 16)
            sync.wait_ge(loaded, 32)

        @block.scalar
        def _(act):
            rows = x.rearrange("b s d -> (b s) d").rearrange("(t p) d -> p t d", p=P)
            act.dma_start(X[:, TILES // 2:, :], rows[:, TILES // 2:, :]).then_inc(loaded, 16)

        @block.gpsimd
        def _(pool):
            nc.gpsimd.memset(ident[:, :], 0.0).then_inc(zeroed, 1)
            pool.wait_ge(zeroed, 1)
            nc.gpsimd.affine_select(out=ident[:, :], in_=ident[:, :], compare_op=ALU.not_equal, fill=1.0,
                                    base=0, pattern=[[-1, P]], channel_multiplier=1).then_inc(zeroed, 1)


def store_state(nc, out, X):
    with Space(nc, "store") as sp, sp.block() as block:
        stored = sp.sem("stored")
        rows = out.rearrange("b s d -> (b s) d").rearrange("(t p) d -> p t d", p=P)

        @block.sync
        def _(sync):
            sync.dma_start(rows[:, 0:TILES // 2, :], X[:, 0:TILES // 2, :]).then_inc(stored, 16)
            sync.wait_ge(stored, 32)

        @block.scalar
        def _(act):
            act.dma_start(rows[:, TILES // 2:, :], X[:, TILES // 2:, :]).then_inc(stored, 16)
            act.wait_ge(stored, 32)


def norm_moments(dve, stats, tmp, mean, chain, var_ready):
    mean_even, sum_even, mean_odd, sum_odd = (stats[:, :, k] for k in (1, 2, 4, 5))
    chain.link(dve.tensor_tensor(tmp[:, 0, :], mean_even, mean_odd, ALU.add))
    chain.link(dve.tensor_tensor(tmp[:, 1, :], mean_even, mean_odd, ALU.subtract))
    chain.link(dve.tensor_tensor(tmp[:, 2, :], sum_even, sum_odd, ALU.add))
    chain.link(dve.tensor_scalar(mean, tmp[:, 0, :], 0.5, None, ALU.mult))
    chain.link(dve.scalar_tensor_tensor(tmp[:, 3, :], tmp[:, 1, :], 0.25, tmp[:, 1, :], ALU.mult, ALU.mult))
    chain.link(dve.scalar_tensor_tensor(tmp[:, 4, :], tmp[:, 2, :], 1.0 / D, tmp[:, 3, :], ALU.mult, ALU.add))
    dve.tensor_scalar(tmp[:, 5, :], tmp[:, 4, :], EPS, None, ALU.add).then_inc(var_ready, 1)


MOMENT_LINKS = 6


def norm_transposed(nc, stage, X, XT, ident, table=None):
    with Space(nc, stage + "_norm") as sp:
        stats = sp.sb("stats", [P, TILES, 6])
        tmp = sp.sb("tmp", [P, 7, TILES])
        mean = sp.sb("mean", [P, TILES])
        rstd = sp.sb("rstd", [P, TILES])
        xn = sp.sb("xn", [P, 4, D])
        turned = [sp.ps(f"turned{k}", [P, BANK]) for k in range(2)]
        step, stats_ready, var_ready, root_ready = (sp.sem(n) for n in ("step", "stats_ready", "var_ready", "root_ready"))
        rows_ready, turned_pairs, copied_pairs = (sp.sem(n) for n in ("rows_ready", "turned_pairs", "copied_pairs"))
        stored = sp.sem("stored")
        with sp.block() as block:

            if table is not None:
                @block.sync
                def _(sync):
                    rows = table[0:TOKENS, 0:D].rearrange("(t p) d -> p t d", p=P)
                    sync.sem_inc(stored, 16)
                    with sync.Fori(0, TILES // 4) as i:
                        sync.wait_ge(rows_ready, i * 4 + 4)
                        sync.dma_start(rows[:, bass.ds(i * 4, 4), :], xn[:, :, :]).then_inc(stored, 16)
                    sync.wait_ge(stored, 16 * (TILES // 4) + 16)

            @block.vector
            def _(dve):
                with dve.Fori(0, TILES) as t:
                    nc.vector.bn_stats(stats[:, t, :], X[:, t, :]).then_inc(stats_ready, 1)
                dve.wait_ge(stats_ready, TILES)
                chain = Chain(dve, step)
                norm_moments(dve, stats, tmp, mean[:, :], chain, var_ready)
                dve.wait_ge(root_ready, 1)
                chain.link(nc.vector.reciprocal(rstd[:, :], tmp[:, 6, :]))
                with dve.Fori(0, TILES // 4) as i:
                    for k in range(4):
                        if k % 2 == 0:
                            dve.wait_ge(turned_pairs, i * 2 + (k // 2 + 1))
                        if k == 0 and table is not None:
                            dve.wait_ge(stored, i * 16 + 16)
                        t = i * 4 + k
                        nc.vector.tensor_scalar(xn[:, k, :], X[:, t, :], mean[:, bass.ds(t, 1)], rstd[:, bass.ds(t, 1)],
                                                ALU.subtract, ALU.mult).then_inc(rows_ready, 1)

            @block.scalar
            def _(act):
                act.sem_inc(copied_pairs, 2)
                act.wait_ge(var_ready, 1)
                nc.scalar.activation(tmp[:, 6, :], tmp[:, 5, :], ACT.Sqrt).then_inc(root_ready, 1)
                with act.Fori(0, TILES // 4) as i:
                    for k in range(2):
                        act.wait_ge(turned_pairs, i * 2 + (k + 3))
                        nc.scalar.copy(XT[:, :, bass.ds(i * (4 * P) + k * 2 * P, 2 * P)],
                                       turned[k][:, :].rearrange("p (c n) -> p c n", c=KT)).then_inc(copied_pairs, 1)

            @block.tensor
            def _(pe):
                pe.sem_inc(turned_pairs, 2)
                with pe.Fori(0, TILES // 4) as i:
                    for k in range(2):
                        pe.wait_ge(copied_pairs, i * 2 + (k + 1))
                        for n in range(2):
                            pe.wait_ge(rows_ready, i * 4 + (2 * k + n + 1))
                            for c in range(KT):
                                last = nc.tensor.transpose(turned[k][:, (2 * c + n) * P:(2 * c + n + 1) * P],
                                                           xn[:, 2 * k + n, c * P:(c + 1) * P], ident[:, :])
                        last.then_inc(turned_pairs, 1)


def route(nc, stage, XT, gate, experts, top_k, eps, W):
    with Space(nc, stage + "_route") as sp:
        gate_w = sp.sb("gate_w", [P, KT, experts])
        shifted = sp.sb("shifted", [P, TILES, experts])
        probs = sp.sb("probs", [P, TILES, experts])
        rest = sp.sb("rest", [P, TILES, experts])
        best = sp.sb("best", [P, TILES, 8])
        row = sp.sb("row", [P, 4, TILES])
        logits = sp.ps("logits", [P, TILES, experts])
        loaded, logits_ready, shifted_ready, exp_ready, step = (
            sp.sem(n) for n in ("loaded", "logits_ready", "shifted_ready", "exp_ready", "step"))

        def wide(column):
            return column.rearrange("p (t o) -> p t o", o=1).to_broadcast([P, TILES, experts])

        with sp.block() as block:

            @block.sync
            def _(sync):
                sync.dma_start(gate_w[:, :, :], gate).then_inc(loaded, 16)

            @block.tensor
            def _(pe):
                pe.wait_ge(loaded, 16)
                for t in range(TILES):
                    for c in range(KT):
                        last = nc.tensor.matmul(logits[:, t, :], XT[:, c, t * P:(t + 1) * P], gate_w[:, c, :],
                                                start=(c == 0), stop=(c == KT - 1))
                last.then_inc(logits_ready, 1)

            @block.scalar
            def _(act):
                act.wait_ge(shifted_ready, 1)
                nc.scalar.activation(probs[:, :, :], shifted[:, :, :], ACT.Exp).then_inc(exp_ready, 1)

            @block.vector
            def _(dve):
                chain = Chain(dve, step)
                link = chain.link
                dve.wait_ge(logits_ready, 1)
                link(nc.vector.tensor_reduce(row[:, 0, :], logits[:, :, :], AX.X, ALU.max))
                nc.vector.tensor_tensor(shifted[:, :, :], logits[:, :, :], wide(row[:, 0, :]),
                                        ALU.subtract).then_inc(shifted_ready, 1)
                dve.wait_ge(exp_ready, 1)
                link(nc.vector.tensor_reduce(row[:, 1, :], probs[:, :, :], AX.X, ALU.add))
                link(nc.vector.reciprocal(row[:, 2, :], row[:, 1, :]))
                link(nc.vector.tensor_tensor(probs[:, :, :], probs[:, :, :], wide(row[:, 2, :]), ALU.mult))
                for t in range(TILES):
                    last = nc.vector.max(best[:, t, :], probs[:, t, :])
                link(last)
                if top_k < 8:
                    link(nc.vector.memset(best[:, :, top_k:8], -1.0))
                for t in range(TILES):
                    last = nc.vector.match_replace(rest[:, t, :], best[:, t, :], probs[:, t, :], 0.0)
                link(last)
                link(nc.vector.tensor_tensor(probs[:, :, :], probs[:, :, :], rest[:, :, :], ALU.subtract))
                link(nc.vector.tensor_reduce(row[:, 1, :], probs[:, :, :], AX.X, ALU.add))
                if eps:
                    link(nc.vector.tensor_scalar(row[:, 1, :], row[:, 1, :], eps, None, ALU.add))
                link(nc.vector.reciprocal(row[:, 3, :], row[:, 1, :]))
                link(nc.vector.tensor_tensor(W[:, :, 0:experts], probs[:, :, :], wide(row[:, 3, :]), ALU.mult))
                if W.shape[2] > experts:
                    link(nc.vector.memset(W[:, :, experts:], 1.0))


def experts_sum(nc, stage, X, XT, W, w_up, w_down, n_experts, FP, FT):
    NB = 512
    CHUNKS = TOKENS // NB
    TPC = NB // P
    PAIRS = 2 * CHUNKS * FT
    PRODUCTS = ((0, 0), (0, 1), (1, 0))
    with Space(nc, stage + "_experts") as sp:
        x = [sp.sb(f"x{k}", [P, KT, TOKENS], F32R) for k in range(2)]
        wgu = [sp.sb(f"wgu{s}", [P, KT, 2 * FT * FP]) for s in range(2)]
        wd = [sp.sb(f"wd{s}", [FP, FT, D]) for s in range(2)]
        wgu_parts = [[sp.sb(f"wgu{s}_{k}", [P, KT, 2 * FT * FP], F32R) for k in range(2)] for s in range(2)]
        wd_parts = [[sp.sb(f"wd{s}_{k}", [FP, FT, D], F32R) for k in range(2)] for s in range(2)]
        gated = sp.sb("gated", [FP, 2, NB])
        hidden = sp.sb("hidden", [FP, 2, NB])
        hidden_parts = [[sp.sb(f"hidden{s}_{k}", [FP, FT, NB], F32R) for k in range(2)] for s in range(2)]
        pair = [sp.ps(f"pair{s}", [FP, 2, NB]) for s in range(2)]
        y = [sp.ps(f"y{s}", [P, TPC, D]) for s in range(2)]
        w_loaded = [sp.sem(f"w_loaded{s}") for s in range(2)]
        x_high, x_low, w_high, w_low, hidden_high, hidden_low = (
            sp.sem(n) for n in ("x_high", "x_low", "w_high", "w_low", "hidden_high", "hidden_low"))
        pair_made, gate_made, hidden_made, y_made, combined = (
            sp.sem(n) for n in ("pair_made", "gate_made", "hidden_made", "y_made", "combined"))
        acc = sp.sem("acc")

        def run(engine, body):
            odd = n_experts % 2
            body(0, 2, True, False)
            with engine.Fori(1, n_experts // 2 - (1 - odd)) as i:
                body(i, 2, False, False)
            body(n_experts // 2 - (1 - odd), 2 - odd, False, True)

        with sp.block() as block:

            @block.sync
            def _(sync):
                def load(e, s):
                    sync.dma_start(wgu[s][:, :, :], w_up[e]).then_inc(w_loaded[s], 16)
                    sync.dma_start(wd[s][:, :, :], w_down[e]).then_inc(w_loaded[s], 16)

                for s in range(2):
                    load(s, s)
                with sync.Fori(0, n_experts // 2 - 1) as i:
                    for s in range(2):
                        sync.wait_ge(w_low, i * 4 + (2 * s + 2))
                        load(i * 2 + (2 + s), s)
                if n_experts % 2:
                    sync.wait_ge(w_low, 2 * (n_experts - 2))
                    load(n_experts - 1, 0)

            @block.gpsimd
            def _(pool):
                def low(i, s):
                    for k, (whole, parts) in enumerate(((wgu, wgu_parts), (wd, wd_parts))):
                        pool.wait_ge(w_high, i * 4 + (2 * s + k + 1))
                        nc.gpsimd.tensor_tensor(parts[s][1][:, :, :], whole[s][:, :, :], parts[s][0][:, :, :], ALU.subtract
                                                ).then_inc(w_low, 1)

                with pool.Fori(0, n_experts // 2) as i:
                    for s in range(2):
                        low(i, s)
                if n_experts % 2:
                    low(n_experts // 2, 0)

            @block.tensor
            def _(pe):
                pe.sem_inc(y_made, 2)

                def up(i, c, first):
                    s, q = c // CHUNKS, c % CHUNKS
                    if first and s == 0:
                        pe.wait_ge(x_low, q + 1)
                    for j in range(FT):
                        n = c * FT + j
                        pe.wait_ge(hidden_made, i * PAIRS + (n + 1))
                        for half in range(2):
                            col = (half * FT + j) * FP
                            for k in range(KT):
                                for a, b in PRODUCTS:
                                    last = nc.tensor.matmul(pair[n % 2][:, half, :], wgu_parts[s][a][:, k, col:col + FP],
                                                            x[b][:, k, q * NB:(q + 1) * NB], start=(k == 0 and (a, b) == (0, 0)),
                                                            stop=(k == KT - 1 and (a, b) == PRODUCTS[-1]))
                        last.then_inc(pair_made, 1)

                def down(i, c):
                    s = c // CHUNKS % 2
                    pe.wait_ge(hidden_low, i * PAIRS + ((c + 1) * FT + 2))
                    pe.wait_ge(combined, i * (2 * CHUNKS) + (c + 1))
                    for t in range(TPC):
                        for j in range(FT):
                            for a, b in PRODUCTS:
                                last = nc.tensor.matmul(y[c % 2][:, t, :], hidden_parts[c % 2][a][:, j, t * P:(t + 1) * P],
                                                        wd_parts[s][b][:, j, :], start=(j == 0 and (a, b) == (0, 0)),
                                                        stop=(j == FT - 1 and (a, b) == PRODUCTS[-1]))
                    last.then_inc(y_made, 1)

                def body(i, parts, first, last):
                    for s in range(parts):
                        pe.wait_ge(w_low, i * 4 + (2 * s + 2))
                        for c in range(s * CHUNKS, (s + 1) * CHUNKS):
                            up(i, c, first)
                            if c or not first:
                                down(i, c - 1)
                    if last:
                        down(i, parts * CHUNKS - 1)

                run(pe, body)

            @block.scalar
            def _(act):
                def high(i, s):
                    act.wait_ge(w_loaded[s], i * 32 + 32)
                    nc.scalar.copy(wgu_parts[s][0][:, :, :], wgu[s][:, :, :]).then_inc(w_high, 1)
                    nc.scalar.copy(wd_parts[s][0][:, :, :], wd[s][:, :, :]).then_inc(w_high, 1)

                def body(i, parts, first, last):
                    for n in range(parts * CHUNKS * FT):
                        c, j = n // FT, n % FT
                        at = i * PAIRS
                        act.wait_ge(pair_made, at + (n + 1))
                        act.wait_ge(hidden_made, at + (n + 1))
                        nc.scalar.activation(gated[:, n % 2, :], pair[n % 2][:, 0, :], ACT.Silu).then_inc(gate_made, 1)
                        act.wait_ge(hidden_made, at + (n + 3))
                        act.wait_ge(y_made, i * (2 * CHUNKS) + (c + 1))
                        nc.scalar.copy(hidden_parts[c % 2][0][:, j, :], hidden[:, n % 2, :]).then_inc(hidden_high, 1)
                        s = c // CHUNKS
                        if c % CHUNKS == 1 and j == FT - 1 and not (last and s == parts - 1):
                            act.wait_ge(y_made, i * (2 * CHUNKS) + (s * CHUNKS + 2))
                            high(i + (s + 1) // 2, (s + 1) % 2)

                high(0, 0)
                for q in range(CHUNKS):
                    cut = slice(q * NB, (q + 1) * NB)
                    nc.scalar.copy(x[0][:, :, cut], XT[:, :, cut]).then_inc(x_high, 1)
                run(act, body)

            @block.vector
            def _(dve):
                dve.sem_inc(hidden_made, 2)
                dve.sem_inc(hidden_low, 2)
                dve.sem_inc(combined, 2)

                def product(i, c):
                    for j in range(FT):
                        n = c * FT + j
                        dve.wait_ge(gate_made, i * PAIRS + (n + 1))
                        dve.wait_ge(hidden_low, i * PAIRS + (n + 1))
                        nc.vector.tensor_tensor(hidden[:, n % 2, :], gated[:, n % 2, :], pair[n % 2][:, 1, :],
                                                ALU.mult).then_inc(hidden_made, 1)
                        dve.wait_ge(hidden_high, i * PAIRS + (n + 1))
                        nc.vector.tensor_tensor(hidden_parts[c % 2][1][:, j, :], hidden[:, n % 2, :], hidden_parts[c % 2][0][:, j, :],
                                                ALU.subtract).then_inc(hidden_low, 1)

                def combine(i, c):
                    s, q = c // CHUNKS, c % CHUNKS
                    dve.wait_ge(y_made, i * (2 * CHUNKS) + (c + 3))
                    for t in range(TPC):
                        tile = q * TPC + t
                        nc.vector.scalar_tensor_tensor(X[:, tile, :], y[c % 2][:, t, :], W[:, tile, bass.ds(i * 2 + s, 1)],
                                                       X[:, tile, :], ALU.mult, ALU.add
                                                       ).then_inc(combined if t == TPC - 1 else acc, 1)

                def body(i, parts, first, last):
                    for c in range(parts * CHUNKS):
                        product(i, c)
                        if c or not first:
                            combine(i, c - 1)
                    if last:
                        combine(i, parts * CHUNKS - 1)

                for q in range(CHUNKS):
                    cut = slice(q * NB, (q + 1) * NB)
                    dve.wait_ge(x_high, q + 1)
                    nc.vector.tensor_tensor(x[1][:, :, cut], XT[:, :, cut], x[0][:, :, cut], ALU.subtract).then_inc(x_low, 1)
                run(dve, body)


def build_program(nc, A, out, stages=(0, 1, 2, 3, 4, 5)):
    Space.used = []
    with ExitStack() as ctx:
        X = ctx.enter_context(nc.sbuf_tensor("X", [P, TILES, D], F32))
        ident = ctx.enter_context(nc.sbuf_tensor("ident", [P, P], F32))
        load_state(nc, A["x"], X, ident)
        for n in stages:
            with ExitStack() as layer:
                XT = layer.enter_context(nc.sbuf_tensor(f"XT{n}", [P, KT, TOKENS], F32))
                if n not in (2, 3):
                    norm_transposed(nc, f"s{n}", X, XT, ident)
                SUBLAYERS[n](nc, A, X, XT, ident)
            Space.clear_used(nc)
        store_state(nc, out, X)


def sub_moe1(nc, A, X, XT, ident):
    with nc.sbuf_tensor("moe1_W", [P, TILES, 17], F32) as W:
        route(nc, "moe1", XT, A["L1_ffn_gate_w"], 16, 4, 0.0, W)
        experts_sum(nc, "moe1", X, XT, W, A["L1_ffn_up"], A["L1_ffn_down"], 17, 128, 1)


SUBLAYERS = {5: sub_moe1}


E0, TOP0, F0, FT0 = 64, 8, 96, 2
HALVES = P // E0
HALF = TOKENS // HALVES
CAP = 192
REST = CAP - P
SLOT_TILES = HALVES * CAP // P
ROW = D + E0


def expert_lists(nc, A, W, ident, table, sums, slots, flag, left):
    J = HALF // P
    with Space(nc, "lists") as sp:
        mask = sp.sb("mask", [P, J, HALVES, E0])
        codes = sp.sb("codes", [P, HALF])
        values = [sp.sb("values", [P, HALF]), left]
        lists = sp.sb("lists", [P, CAP])
        rests = sp.sb("rests", [E0, HALVES, REST])
        base = sp.sb("base", [P, SLOT_TILES + 1])
        slot_f = sp.sb("slot_f", [P, 3, SLOT_TILES, E0])
        zeros = sp.sb("zeros", [P, (TOKENS // P + 1) * D])
        top = sp.sb("top", [P, 1])
        top_row = sp.sb("top_row", [1, P])
        most = sp.sb("most", [1, 1])
        ps_v = sp.ps("ps_v", [P, HALF])
        ps_l = sp.ps("ps_l", [P, HALVES, E0])
        ps_r = sp.ps("ps_r", [P, BANK])
        ps_m = sp.ps("ps_m", [P, BANK])
        loaded, mask_made, turned, step, moved, lists_turned, stored, zeroed, top_made, top_turned = (
            sp.sem(n) for n in ("loaded", "mask_made", "turned", "step", "moved", "lists_turned", "stored", "zeroed",
                                "top_made", "top_turned"))
        with sp.block() as block:

            @block.sync
            def _(sync):
                sync.dma_start(codes[:, :], A["codes"]).then_inc(loaded, 16)
                sync.dma_start(base[:, :], A["slot_base"]).then_inc(loaded, 16)
                sync.dma_start(table[0:TOKENS, D:].rearrange("(t p) e -> p t e", p=P), W[:, :, :]).then_inc(stored, 16)
                sync.wait_ge(zeroed, 1)
                sync.dma_start(table[TOKENS:, :], zeros[:, 0:ROW]).then_inc(stored, 16)
                for s in sums:
                    sync.dma_start(s.rearrange("(p t) d -> p (t d)", p=P), zeros[:, :]).then_inc(stored, 16)
                sync.wait_ge(stored, 16 * (2 + len(sums)))

            @block.gpsimd
            def _(pool):
                nc.gpsimd.memset(zeros[:, :], 0.0).then_inc(zeroed, 1)

            @block.tensor
            def _(pe):
                pe.wait_ge(mask_made, 1)
                for j in range(J):
                    last = nc.tensor.transpose(ps_v[:, j * P:(j + 1) * P], mask[:, j, :, :].rearrange("p h e -> p (h e)"), ident[:, :])
                last.then_inc(turned, 1)
                pe.wait_ge(moved, HALVES)
                nc.tensor.transpose(ps_l[:, :, :].rearrange("p h e -> p (h e)"), lists[:, 0:P], ident[:, :]).then_inc(lists_turned, 1)
                nc.tensor.transpose(ps_r[:, 0:E0], rests[:, :, :].rearrange("e h s -> e (h s)"), ident[0:E0, 0:E0]
                                    ).then_inc(lists_turned, 1)
                pe.wait_ge(top_made, 1)
                nc.tensor.transpose(ps_m[0:1, 0:P], top[:, 0:1], ident[:, :]).then_inc(top_turned, 1)

            @block.vector
            def _(dve):
                link = Chain(dve, step).link
                v = nc.vector
                v.tensor_scalar(mask[:, :, :, :], W[:, :, :].rearrange("p (h j) e -> p j h e", h=HALVES), 0.0, None,
                                ALU.is_gt).then_inc(mask_made, 1)
                dve.wait_ge(loaded, 32)
                dve.wait_ge(turned, 1)
                link(v.tensor_tensor(values[0][:, :], ps_v[:, :], codes[:, :], ALU.mult))
                for r in range(CAP // 8):
                    best = lists[:, 8 * r:8 * r + 8]
                    link(v.max(best, values[r % 2][:, :]))
                    link(v.match_replace(values[(r + 1) % 2][:, :], best, values[r % 2][:, :], 0.0))
                assert CAP // 8 % 2 == 0
                link(v.tensor_copy(left[:, :], values[0][:, :]))
                v.tensor_reduce(top[:, 0:1], left[:, :], AX.X, ALU.max).then_inc(top_made, 1)
                for h in range(HALVES):
                    v.tensor_copy(rests[:, h, :], lists[h * E0:(h + 1) * E0, P:]).then_inc(moved, 1)
                dve.wait_ge(lists_turned, 2)
                tiles = [ps_l[:, 0, :], ps_l[:, 1, :], ps_r[:, 0:E0]]
                for r, code in enumerate(tiles):
                    link(v.tensor_scalar(slot_f[:, 0, r, :], code, -1.0, base[:, r:r + 1], ALU.mult, ALU.add))
                    link(v.tensor_scalar(slot_f[:, 1, r, :], code, 0.0, None, ALU.is_gt))
                link(v.tensor_tensor(slot_f[:, 2, :, :], slot_f[:, 0, :, :], slot_f[:, 1, :, :], ALU.mult))
                link(v.tensor_scalar(slots[:, :, :].rearrange("p e r -> p r e"), slot_f[:, 2, :, :], base[:, SLOT_TILES:], None, ALU.add))
                dve.wait_ge(top_turned, 1)
                link(v.tensor_reduce(most[:, :], ps_m[0:1, 0:P], AX.X, ALU.max))
                link(v.tensor_scalar(flag[:, :], most[:, :], 0.0, None, ALU.is_gt))


def chosen_experts(nc, A, table, sums, slots, ident):
    N = SLOT_TILES * P
    with Space(nc, "chosen") as sp:
        wgu = [sp.sb(f"wgu{s}", [P, KT, 2 * FT0 * F0]) for s in range(2)]
        wd = [sp.sb(f"wd{s}", [F0, FT0, D]) for s in range(2)]
        index = [sp.sb(f"index{s}", [P, SLOT_TILES], mybir.dt.int32) for s in range(4)]
        rows = [sp.sb(f"rows{s}", [P, SLOT_TILES, ROW]) for s in range(4)]
        x_t = [sp.sb(f"x_t{s}", [P, KT, N]) for s in range(2)]
        gated = sp.sb("gated", [F0, FT0, N])
        hidden = [sp.sb(f"hidden{s}", [F0, FT0, N]) for s in range(2)]
        y = [sp.sb(f"y{s}", [P, SLOT_TILES, D]) for s in range(2)]
        ps_x = sp.ps("ps_x", [P, KT, BANK])
        pair = [sp.ps(f"pair{j}", [F0, 2, BANK]) for j in range(FT0)]
        ps_y = sp.ps("ps_y", [P, 4, D])
        w_loaded = [sp.sem(f"w_loaded{s}") for s in range(2)]
        gathered = [sp.sem(f"gathered{s}") for s in range(4)]
        scattered = [sp.sem(f"scattered{s}") for s in range(4)]
        index_made, x_turned, x_copied, y_made, y_scaled, pair_made, gate_made, hidden_made, y_acc = (
            sp.sem(n) for n in ("index_made", "x_turned", "x_copied", "y_made", "y_scaled", "pair_made", "gate_made",
                                "hidden_made", "y_acc"))
        issued = sp.sem("issued")

        def turns(engine, step):
            for s in range(4):
                step(s, 0, s, s == 0, False)
            with engine.Fori(1, E0 // 4 - 1) as i:
                for s in range(4):
                    step(i * 4 + s, i, s, False, False)
            for s in range(4):
                step(E0 - 4 + s, E0 // 4 - 1, s, False, s == 3)

        with sp.block() as block:

            @block.sync
            def _(sync):
                def load(e, s):
                    sync.dma_start(wgu[s][:, :, :], A["L0_ffn_up"][e]).then_inc(w_loaded[s], 16)
                    sync.dma_start(wd[s][:, :, :], A["L0_ffn_down"][e]).then_inc(w_loaded[s], 16)

                for s in range(2):
                    load(s, s)
                with sync.Fori(0, E0 // 2 - 1) as i:
                    for s in range(2):
                        sync.wait_ge(y_made, i * 2 + (s + 1))
                        load(i * 2 + (s + 2), s)

            @block.gpsimd
            def _(pool):
                def gather(e, s):
                    nc.gpsimd.tensor_copy(index[s][:, :], slots[:, bass.ds(e, 1), :].rearrange("p o r -> p (o r)")
                                          ).then_inc(index_made, 1)
                    pool.wait_ge(index_made, e + 1)
                    pool.sem_inc(issued, 1)
                    for r in range(SLOT_TILES):
                        nc.gpsimd.indirect_dma_start(rows[s][:, r, :], None, table[:, :],
                                                     bass.IndirectOffsetOnAxis(ap=index[s][:, r:r + 1], axis=0)
                                                     ).then_inc(gathered[s], 16)

                def step(e, i, s, first, last):
                    p, ip = (s - 1) % 4, i - (1 if s == 0 else 0)
                    if not first:
                        pool.wait_ge(scattered[p], (ip * 16 + 16) * SLOT_TILES)
                    if not (isinstance(e, int) and e + 3 >= E0):
                        gather(i * 4 + (s + 3), p)
                    pool.wait_ge(y_scaled, e + 1)
                    pool.sem_inc(issued, 1)
                    for r in range(SLOT_TILES):
                        nc.gpsimd.indirect_dma_start(sums[r], bass.IndirectOffsetOnAxis(ap=index[s][:, r:r + 1], axis=0),
                                                     y[s % 2][:, r, :], None, compute_op=ALU.add).then_inc(scattered[s], 16)

                for s in range(3):
                    gather(s, s)
                turns(pool, step)
                pool.wait_ge(scattered[3], E0 // 4 * 16 * SLOT_TILES)

            @block.tensor
            def _(pe):
                def turn_x(e, i, s):
                    pe.wait_ge(gathered[s], (i * 16 + 16) * SLOT_TILES)
                    if not (isinstance(e, int) and e == 0):
                        pe.wait_ge(x_copied, e)
                    for c in range(KT):
                        for r in range(SLOT_TILES):
                            last = nc.tensor.transpose(ps_x[:, c, r * P:(r + 1) * P], rows[s][:, r, c * P:(c + 1) * P], ident[:, :])
                    last.then_inc(x_turned, 1)

                def up(e, i, s, j, first):
                    s, turn = s % 2, s // 2
                    if j == 0:
                        pe.wait_ge(x_copied, e + 1)
                        pe.wait_ge(w_loaded[s], i * 64 + (turn * 32 + 32))
                    if not first:
                        pe.wait_ge(hidden_made, (e - 1) * FT0 + (j + 1))
                    for side in range(2):
                        for c in range(KT):
                            col = (side * FT0 + j) * F0
                            last = nc.tensor.matmul(pair[j][:, side, 0:N], wgu[s][:, c, col:col + F0], x_t[s][:, c, :],
                                                    start=(c == 0), stop=(c == KT - 1))
                    last.then_inc(pair_made, 1)

                def down(e, s, very_first):
                    pe.wait_ge(hidden_made, e * FT0 + FT0)
                    if not very_first:
                        pe.wait_ge(y_scaled, e)
                    for r in range(SLOT_TILES):
                        for j in range(FT0):
                            last = nc.tensor.matmul(ps_y[:, r, :], hidden[s][:, j, r * P:(r + 1) * P], wd[s][:, j, :],
                                                    start=(j == 0), stop=(j == FT0 - 1))
                    last.then_inc(y_made, 1)

                turn_x(0, 0, 0)

                def step(e, i, s, first, last):
                    up(e, i, s, 0, first)
                    if not first:
                        down(i * 4 + (s - 1), (s - 1) % 2, isinstance(e, int) and e == 1)
                    up(e, i, s, 1, first)
                    if not last:
                        turn_x(i * 4 + (s + 1), i + (s + 1) // 4, (s + 1) % 4)

                turns(pe, step)
                down(E0 - 1, 1, False)

            @block.scalar
            def _(act):
                def take_x(e, s, early):
                    act.wait_ge(x_turned, e + 1)
                    if not early:
                        act.wait_ge(pair_made, (e - 1) * FT0)
                    nc.scalar.copy(x_t[s][:, :, :], ps_x[:, :, 0:N]).then_inc(x_copied, 1)

                take_x(0, 0, True)

                def step(e, i, s, first, last):
                    for j in range(FT0):
                        act.wait_ge(pair_made, e * FT0 + (j + 1))
                        if not first:
                            act.wait_ge(hidden_made, (e - 1) * FT0 + (j + 1))
                        nc.scalar.activation(gated[:, j, :], pair[j][:, 0, 0:N], ACT.Silu).then_inc(gate_made, 1)
                    if not last:
                        take_x(i * 4 + (s + 1), (s + 1) % 2, isinstance(e, int) and e == 0)

                turns(act, step)

            @block.vector
            def _(dve):
                def scale(e, i, s):
                    dve.wait_ge(y_made, e + 1)
                    if not (isinstance(e, int) and e < 2):
                        dve.wait_ge(scattered[(s - 2) % 4], (i * 16 + (16 if s >= 2 else 0)) * SLOT_TILES)
                    for r in range(SLOT_TILES):
                        nc.vector.tensor_scalar(y[s % 2][:, r, :], ps_y[:, r, :], rows[s][:, r, bass.ds(e + D, 1)], None,
                                                ALU.mult).then_inc(y_scaled if r == SLOT_TILES - 1 else y_acc, 1)

                def step(e, i, s, first, last):
                    for j in range(FT0):
                        dve.wait_ge(gate_made, e * FT0 + (j + 1))
                        if not (isinstance(e, int) and e < 2):
                            dve.wait_ge(y_made, e - 1)
                        nc.vector.tensor_tensor(hidden[s % 2][:, j, :], gated[:, j, :], pair[j][:, 1, 0:N], ALU.mult
                                                ).then_inc(hidden_made, 1)
                        if j == 0 and not first:
                            scale(i * 4 + (s - 1), i - (1 if s == 0 else 0), (s - 1) % 4)

                turns(dve, step)
                scale(E0 - 1, E0 // 4 - 1, 3)


def add_sums(nc, X, sums):
    with Space(nc, "add_sums") as sp:
        part = [sp.sb(f"part{r}", [P, TILES, D]) for r in range(len(sums))]
        loaded = [sp.sem(f"loaded{r}") for r in range(len(sums))]
        added = sp.sem("added")
        with sp.block() as block:

            @block.sync
            def _(sync):
                for r, s in enumerate(sums):
                    sync.dma_start(part[r][:, :, :], s[0:TOKENS, :].rearrange("(t p) d -> p t d", p=P)).then_inc(loaded[r], 16)

            @block.vector
            def _(dve):
                link = Chain(dve, added).link
                for r in range(len(sums)):
                    dve.wait_ge(loaded[r], 16)
                    link(nc.vector.tensor_tensor(X[:, :, :], X[:, :, :], part[r][:, :, :], ALU.add))


def keep_left(nc, W, left, ident):
    J = HALF // P
    with Space(nc, "keep_left") as sp:
        over = sp.sb("over", [P, HALF])
        ps = sp.ps("ps", [P, J, HALVES, E0])
        marked, turned, done = (sp.sem(n) for n in ("marked", "turned", "done"))
        with sp.block() as block:

            @block.vector
            def _(dve):
                nc.vector.tensor_scalar(over[:, :], left[:, :], 0.0, None, ALU.is_gt).then_inc(marked, 1)
                dve.wait_ge(turned, 1)
                for h in range(HALVES):
                    part = W[:, h * J:(h + 1) * J, :]
                    nc.vector.tensor_tensor(part, part, ps[:, :, h, :], ALU.mult).then_inc(done, 1)

            @block.tensor
            def _(pe):
                pe.wait_ge(marked, 1)
                for j in range(J):
                    last = nc.tensor.transpose(ps[:, j, :, :].rearrange("p h e -> p (h e)"), over[:, j * P:(j + 1) * P], ident[:, :])
                last.then_inc(turned, 1)


def top8_experts(nc, A, X, XT, ident):
    table = nc.dram_tensor("table", (TOKENS + P, ROW), F32, kind="Internal").ap()
    sums = [nc.dram_tensor(f"sums{r}", (TOKENS + P, D), F32, kind="Internal").ap() for r in range(SLOT_TILES)]
    norm_transposed(nc, "s2", X, XT, ident, table)
    with Space(nc, "top8") as sp:
        W = sp.sb("W", [P, TILES, E0])
        left = sp.sb("left", [P, HALF])
        slots = sp.sb("slots", [P, E0, SLOT_TILES], mybir.dt.int32)
        flag = sp.sb("flag", [1, 1], mybir.dt.int32)
        route(nc, "moe0", XT, A["L0_ffn_gate_w"], E0, TOP0, 1e-20, W)
        expert_lists(nc, A, W, ident, table, sums, slots, flag, left)
        chosen_experts(nc, A, table, sums, slots, ident)
        add_sums(nc, X, sums)
        overflow = nc.values_load(flag[0:1, 0:1], min_val=0, max_val=1)
        with nc.If(overflow > 0):
            nc.all_engine_barrier()
            keep_left(nc, W, left, ident)
            experts_sum(nc, "moe0", X, XT, W, A["L0_ffn_up"], A["L0_ffn_down"], E0, F0, FT0)
        nc.end_all_ifs()


SUBLAYERS[2] = top8_experts


def pipelined(engine, n, front, back, unroll=2):
    front(0, 0, 0)

    def turn(i, steps):
        for k in range(unroll):
            if k < steps:
                front(i * unroll + (k + 1), i + (k + 1) // unroll, (k + 1) % unroll)
            back(i * unroll + k, i, k)

    with engine.Fori(0, n // unroll - 1) as i:
        turn(i, unroll)
    turn(n // unroll - 1, unroll - 1)


def nothing(t, i, s):
    pass


def self_attention(nc, A, X, XT, ident):
    HD = D // HEADS
    HPC = P // HD
    with Space(nc, "self") as sp:
        w = sp.sb("w", [P, KT, 3 * D])
        bias = sp.sb("bias", [P, GROUPS, SEQ])
        own = sp.sb("own", [P, HPC])
        xt = [sp.sb(f"xt{s}", [P, KT, P]) for s in range(2)]
        k_t = [sp.sb(f"k_t{s}", [P, KT, P]) for s in range(2)]
        v = [sp.sb(f"v{s}", [P, D]) for s in range(2)]
        q_own = [sp.sb(f"q_own{s}", [P, KT, BPT, HPC * SEQ]) for s in range(2)]
        soft = sp.sb("soft", [P, GROUPS, P])
        shifted = [sp.sb(f"shifted{s}", [P, GROUPS, P]) for s in range(2)]
        probs = [sp.sb(f"probs{s}", [P, GROUPS, P]) for s in range(2)]
        probs_t = sp.sb("probs_t", [P, GROUPS, P])
        row = sp.sb("row", [P, 3, GROUPS * BPT])
        ps_q = sp.ps("ps_q", [P, BANK])
        ps_kv = sp.ps("ps_kv", [P, 2, D])
        ps_s = sp.ps("ps_s", [P, GROUPS, P])
        ps_t = sp.ps("ps_t", [P, GROUPS, P])
        ps_o = sp.ps("ps_o", [P, BPT, 2 * GROUPS, HPG * HD])
        loaded = sp.sem("loaded")
        names = ("xt_copied", "projected", "scored", "turned", "attended", "kv_copied", "exps", "t_copied",
                 "q_masked", "shifts", "normed", "added")
        xt_copied, projected, scored, turned, attended, kv_copied, exps, t_copied, q_masked, shifts, normed, added = (
            sp.sem(n) for n in names)
        step, acc = sp.sem("step"), sp.sem("acc")

        with sp.block() as block:

            @block.sync
            def _(sync):
                sync.dma_start(w[:, :, :], A["L0_attn_w"]).then_inc(loaded, 16)
                sync.dma_start(bias[:, :, :], A["alibi"]).then_inc(loaded, 16)
                sync.dma_start(own[:, :], A["own16"]).then_inc(loaded, 16)

            @block.gpsimd
            def _(pool):
                pool.sem_inc(xt_copied, 2)

                def front(t, i, s):
                    pool.wait_ge(projected, t + 1)
                    nc.gpsimd.tensor_copy(xt[s][:, :, :], XT[:, :, bass.ds(t * P, P)]).then_inc(xt_copied, 1)

                pipelined(pool, TILES, front, nothing)

            @block.tensor
            def _(pe):
                pe.wait_ge(loaded, 48)
                pe.sem_inc(projected, 2)
                pe.sem_inc(attended, 2)
                pe.sem_inc(turned, 2)

                def project(t, s):
                    pe.wait_ge(xt_copied, t + 3)
                    pe.wait_ge(kv_copied, t + 1)
                    pe.wait_ge(q_masked, t * KT + KT)
                    for m in range(2 * KT):
                        col = (D if m < KT else 0) + (m % KT) * P
                        for c in range(KT):
                            out = ps_q[:, m * P:(m + 1) * P] if m < KT else ps_kv[:, 0, (m - KT) * P:(m - KT + 1) * P]
                            nc.tensor.matmul(out, w[:, c, col:col + P], xt[s][:, c, :],
                                             start=(c == 0), stop=(c == KT - 1))
                    for c in range(KT):
                        last = nc.tensor.matmul(ps_kv[:, 1, :], xt[s][:, c, :], w[:, c, 2 * D:3 * D],
                                                start=(c == 0), stop=(c == KT - 1))
                    last.then_inc(projected, 1)

                def score(t, s):
                    pe.wait_ge(q_masked, t * KT + 2 * KT)
                    pe.wait_ge(kv_copied, t + 2)
                    pe.wait_ge(shifts, t + 2)
                    for b in range(BPT):
                        at = slice(b * SEQ, (b + 1) * SEQ)
                        for g in range(GROUPS):
                            last = nc.tensor.matmul(ps_s[:, g, at], q_own[s][:, g * HPG // HPC, b, (g * P) % (HPC * SEQ):(g * P) % (HPC * SEQ) + P],
                                                    k_t[s][:, g * HPG // HPC, at], start=True, stop=True)
                    last.then_inc(scored, 1)

                def attend(t, s):
                    pe.wait_ge(normed, t + 1)
                    pe.wait_ge(t_copied, t + 1)
                    for g in range(GROUPS):
                        last = nc.tensor.transpose(ps_t[:, g, :], probs[s][:, g, :], ident[:, :])
                    last.then_inc(turned, 1)
                    pe.wait_ge(t_copied, t + 2)
                    pe.wait_ge(added, t + 1)
                    for g in range(GROUPS):
                        for b in range(BPT):
                            at = slice(b * SEQ, (b + 1) * SEQ)
                            last = nc.tensor.matmul(ps_o[:, b, g, :], probs_t[at, g, :],
                                                    v[s][at, g * HPG * HD:(g + 1) * HPG * HD], start=True, stop=True)
                    last.then_inc(attended, 1)

                project(0, 0)
                score(0, 0)

                def turn(i, steps):
                    for k in range(2):
                        if k < steps:
                            project(i * 2 + (k + 1), (k + 1) % 2)
                        attend(i * 2 + k, k)
                        if k < steps:
                            score(i * 2 + (k + 1), (k + 1) % 2)

                with pe.Fori(0, TILES // 2 - 1) as i:
                    turn(i, 2)
                turn(TILES // 2 - 1, 1)

            @block.scalar
            def _(act):
                act.sem_inc(kv_copied, 1)
                act.sem_inc(t_copied, 1)

                def take_kv(t, s):
                    act.wait_ge(projected, t + 3)
                    act.wait_ge(attended, t + 1)
                    nc.scalar.copy(v[s][:, :], ps_kv[:, 1, :]).then_inc(acc, 1)
                    nc.scalar.copy(k_t[s][:, :, :], ps_kv[:, 0, :].rearrange("p (c n) -> p c n", c=KT)).then_inc(kv_copied, 1)

                def exp(t, s):
                    act.wait_ge(shifts, t + 3)
                    nc.scalar.activation(shifted[s][:, :, :], shifted[s][:, :, :], ACT.Exp).then_inc(exps, 1)

                def take_turned(t):
                    act.wait_ge(turned, t + 3)
                    act.wait_ge(attended, t + 2)
                    nc.scalar.copy(probs_t[:, :, :], ps_t[:, :, :]).then_inc(t_copied, 1)

                take_kv(0, 0)
                exp(0, 0)

                def turn(i, steps):
                    for k in range(2):
                        if k < steps:
                            take_kv(i * 2 + (k + 1), (k + 1) % 2)
                        take_turned(i * 2 + k)
                        if k < steps:
                            exp(i * 2 + (k + 1), (k + 1) % 2)

                with act.Fori(0, TILES // 2 - 1) as i:
                    turn(i, 2)
                turn(TILES // 2 - 1, 1)

            @block.vector
            def _(dve):
                STEPS = 4
                dve.wait_ge(loaded, 48)
                dve.sem_inc(q_masked, KT)
                dve.sem_inc(shifts, 2)
                dve.sem_inc(added, 1)

                def wide(k):
                    return row[:, k, :].rearrange("p (n o) -> p n o", o=1).to_broadcast([P, GROUPS * BPT, SEQ])

                def by_row(a):
                    return a[:, :, :].rearrange("p g (b k) -> p (g b) k", k=SEQ)

                def mask(t, s):
                    dve.wait_ge(projected, t + 3)
                    for c in range(KT):
                        nc.vector.tensor_tensor(
                            q_own[s][:, c, :, :].rearrange("p b (h q) -> p b h q", q=SEQ),
                            ps_q[:, c * P:(c + 1) * P].rearrange("p (b o q) -> p b o q", o=1, q=SEQ).to_broadcast([P, BPT, HPC, SEQ]),
                            own[:, :].rearrange("p (b h o) -> p b h o", b=1, o=1).to_broadcast([P, BPT, HPC, SEQ]),
                            ALU.mult).then_inc(q_masked, 1)

                def softmax(t, s):
                    chain = Chain(dve, step, t * STEPS)
                    dve.wait_ge(scored, t + 1)
                    chain.link(nc.vector.tensor_tensor(
                        soft[:, :, :].rearrange("p g (b k) -> p g b k", k=SEQ),
                        ps_s[:, :, :].rearrange("p g (b k) -> p g b k", k=SEQ),
                        bias[:, :, :].rearrange("p g (o k) -> p g o k", o=1).to_broadcast([P, GROUPS, BPT, SEQ]), ALU.add))
                    chain.link(nc.vector.tensor_reduce(row[:, 0, :], by_row(soft), AX.X, ALU.max))
                    nc.vector.tensor_tensor(by_row(shifted[s]), by_row(soft), wide(0), ALU.subtract).then_inc(shifts, 1)
                    dve.wait_ge(exps, t + 1)
                    chain.link(nc.vector.tensor_reduce(row[:, 1, :], by_row(shifted[s]), AX.X, ALU.add))
                    chain.link(nc.vector.reciprocal(row[:, 2, :], row[:, 1, :]))
                    dve.wait_ge(turned, t + 1)
                    nc.vector.tensor_tensor(by_row(probs[s]), by_row(shifted[s]), wide(2), ALU.mult).then_inc(normed, 1)

                def add(t):
                    dve.wait_ge(attended, t + 3)
                    for b in range(BPT):
                        rows = slice(b * SEQ, (b + 1) * SEQ)
                        for h in range(HPG):
                            out = X[rows, bass.ds(t, 1), :].rearrange("p o (g h d) -> p (o g) h d", g=GROUPS, h=HPG)[:, :, h, :]
                            last = nc.vector.tensor_tensor(out, ps_o[h * SEQ:(h + 1) * SEQ, b, 0:GROUPS, h * HD:(h + 1) * HD],
                                                           out, ALU.add)
                            last.then_inc(added if (b, h) == (BPT - 1, HPG - 1) else acc, 1)

                mask(0, 0)
                softmax(0, 0)

                def turn(i, steps):
                    for k in range(2):
                        if k < steps:
                            mask(i * 2 + (k + 1), (k + 1) % 2)
                        add(i * 2 + k)
                        if k < steps:
                            softmax(i * 2 + (k + 1), (k + 1) % 2)

                with dve.Fori(0, TILES // 2 - 1) as i:
                    turn(i, 2)
                turn(TILES // 2 - 1, 1)


SUBLAYERS[1] = self_attention


def project_queries(nc, A, XT, Q, stage, weights, bias):
    NB = 512
    with Space(nc, stage) as sp:
        w = sp.sb("w", [P, KT, D])
        b = sp.sb("b", [P, KT])
        ps = [sp.ps(f"ps{s}", [P, KT, NB]) for s in range(2)]
        loaded, made, copied = (sp.sem(n) for n in ("loaded", "made", "copied"))
        with sp.block() as block:

            @block.sync
            def _(sync):
                sync.dma_start(w[:, :, :], weights).then_inc(loaded, 16)
                sync.dma_start(b[:, :], bias).then_inc(loaded, 16)

            @block.tensor
            def _(pe):
                pe.wait_ge(loaded, 32)
                for q in range(TOKENS // NB):
                    if q >= 2:
                        pe.wait_ge(copied, KT * (q - 1))
                    for m in range(KT):
                        for c in range(KT):
                            last = nc.tensor.matmul(ps[q % 2][:, m, :], w[:, c, m * P:(m + 1) * P],
                                                    XT[:, c, q * NB:(q + 1) * NB], start=(c == 0), stop=(c == KT - 1))
                    last.then_inc(made, 1)

            @block.scalar
            def _(act):
                act.wait_ge(loaded, 32)
                for q in range(TOKENS // NB):
                    act.wait_ge(made, q + 1)
                    for m in range(KT):
                        nc.scalar.activation(Q[:, m, q * NB:(q + 1) * NB], ps[q % 2][:, m, :], ACT.Identity,
                                             bias=b[:, m:m + 1]).then_inc(copied, 1)


def project_rows(nc, stage, X, rows, ident, weights, bias_in, bias_out):
    with Space(nc, stage) as sp:
        w = sp.sb("w", [P, KT, D])
        b_in = sp.sb("b_in", [P, KT])
        b_out = sp.sb("b_out", [1, D])
        ones = sp.sb("ones", [1, P])
        rows_t = [sp.sb(f"rows_t{s}", [P, KT, P]) for s in range(2)]
        ps_t = [sp.ps(f"ps_t{s}", [P, BANK]) for s in range(2)]
        ps_y = [sp.ps(f"ps_y{s}", [P, BANK]) for s in range(2)]
        loaded, ones_ready, turned, copied, made, added = (
            sp.sem(n) for n in ("loaded", "ones_ready", "turned", "copied", "made", "added"))
        with sp.block() as block:

            @block.sync
            def _(sync):
                sync.dma_start(w[:, :, :], weights).then_inc(loaded, 16)
                sync.dma_start(b_in[:, :], bias_in).then_inc(loaded, 16)
                sync.dma_start(b_out[:, :], bias_out).then_inc(loaded, 16)

            @block.gpsimd
            def _(pool):
                nc.gpsimd.memset(ones[:, :], 1.0).then_inc(ones_ready, 1)

            @block.tensor
            def _(pe):
                pe.wait_ge(loaded, 48)
                pe.wait_ge(ones_ready, 1)

                def turn(t):
                    if t >= 2:
                        pe.wait_ge(copied, KT * (t - 1))
                    for c in range(KT):
                        last = nc.tensor.transpose(ps_t[t % 2][:, c * P:(c + 1) * P], rows[:, t, c * P:(c + 1) * P], ident[:, :])
                    last.then_inc(turned, 1)

                turn(0)
                for t in range(TILES):
                    if t + 1 < TILES:
                        turn(t + 1)
                    pe.wait_ge(copied, KT * (t + 1))
                    if t >= 2:
                        pe.wait_ge(added, t - 1)
                    nc.tensor.matmul(ps_y[t % 2][:, 0:D], ones[:, :], b_out[:, :], start=True, stop=False)
                    for c in range(KT):
                        last = nc.tensor.matmul(ps_y[t % 2][:, 0:D], rows_t[t % 2][:, c, :], w[:, c, :],
                                                start=False, stop=(c == KT - 1))
                    last.then_inc(made, 1)

            @block.scalar
            def _(act):
                act.wait_ge(loaded, 48)
                for t in range(TILES):
                    act.wait_ge(turned, t + 1)
                    if t >= 2:
                        act.wait_ge(made, t - 1)
                    for c in range(KT):
                        nc.scalar.activation(rows_t[t % 2][:, c, :], ps_t[t % 2][:, c * P:(c + 1) * P], ACT.Identity,
                                             bias=b_in[:, c:c + 1]).then_inc(copied, 1)

            @block.vector
            def _(dve):
                for t in range(TILES):
                    dve.wait_ge(made, t + 1)
                    nc.vector.tensor_tensor(X[:, t, :], X[:, t, :], ps_y[t % 2][:, 0:D], ALU.add).then_inc(added, 1)


def cross_attention_0(nc, A, X, XT, ident):
    HD = D // HEADS
    HPC = P // HD
    W = HPG * HD
    FULL = CTX // P
    with Space(nc, "cross0") as outer:
        Q = outer.sb("Q", [P, KT, TOKENS])
        attended_rows = outer.sb("attended_rows", [P, TILES, D])
        project_queries(nc, A, XT, Q, "cross0_q", A["L0_xattn_Wq"], A["L0_xattn_b_q"])
        with Space(nc, "cross0_in") as sp:
            w = sp.sb("w", [P, KT, 2 * D])
            b_k = sp.sb("b_k", [P, KT])
            own = sp.sb("own", [P, HPC])
            ends = sp.sb("ends", [P, KT, BATCH])
            v_end_rows = sp.sb("v_end_rows", [BATCH, D])
            v_end = sp.sb("v_end", [GROUPS, BATCH, D])
            ctx_t = [sp.sb(f"ctx_t{s}", [P, KT, CTX]) for s in range(2)]
            q_own = [sp.sb(f"q_own{s}", [P, KT, HPC * SEQ]) for s in range(2)]
            k_t = [sp.sb(f"k_t{s}", [P, KT, CTX]) for s in range(2)]
            v = [sp.sb(f"v{s}", [P, FULL, D]) for s in range(2)]
            probs = [sp.sb(f"probs{s}", [P, GROUPS, CTX]) for s in range(2)]
            probs_t = sp.sb("probs_t", [P, FULL, GROUPS * P])
            end_t = sp.sb("end_t", [GROUPS, P])
            row = [sp.sb(f"row{s}", [P, 4, GROUPS]) for s in range(2)]
            ps_k = sp.ps("ps_k", [P, KT, BANK])
            ps_v = sp.ps("ps_v", [P, FULL, D])
            ps_s = [sp.ps(f"ps_s{s}", [P, BANK]) for s in range(2)]
            ps_t = [sp.ps(f"ps_t{s}", [P, GROUPS * P]) for s in range(2)]
            ps_o = sp.ps("ps_o", [P, BANK])
            names = ("loaded", "ctx_loaded0", "ctx_loaded1", "zeroed", "end_made", "end_copied", "end_placed", "q_masked",
                     "k_made", "v_made", "k_copied", "v_copied", "scored", "maxed", "negated", "exps", "turned", "t_copied",
                     "summed", "attended", "extracted", "act_acc", "dve_acc")
            sems = {n: sp.sem(n) for n in names}
            (loaded, ctx_loaded0, ctx_loaded1, zeroed, end_made, end_copied, end_placed, q_masked,
             k_made, v_made, k_copied, v_copied, scored, maxed, negated, exps, turned, t_copied,
             summed, attended, extracted, act_acc, dve_acc) = (sems[n] for n in names)
            ctx_loaded = (ctx_loaded0, ctx_loaded1)
            with sp.block() as block:

                @block.sync
                def _(sync):
                    sync.dma_start(ends[:, :, :], A["ctx_ends"]).then_inc(loaded, 16)
                    sync.dma_start(w[:, :, :], A["L0_xattn_Wkv"]).then_inc(loaded, 16)
                    sync.dma_start(b_k[:, :], A["L0_xattn_b_k"]).then_inc(loaded, 16)
                    sync.dma_start(own[:, :], A["own4"]).then_inc(loaded, 16)
                    for s in range(2):
                        sync.dma_start(ctx_t[s][:, :, :], A["ctx_t"][s]).then_inc(ctx_loaded[s], 16)
                    sync.wait_ge(end_copied, 1)
                    sync.wait_ge(zeroed, 1)
                    for g in range(GROUPS):
                        sync.dma_start(v_end[g:g + 1, :, g * W:(g + 1) * W],
                                       v_end_rows[:, g * W:(g + 1) * W]).then_inc(end_placed, 16)
                    with sync.Fori(0, BATCH // 2 - 1) as i:
                        for s in range(2):
                            sync.wait_ge(v_made, i * 2 + (s + 1))
                            sync.dma_start(ctx_t[s][:, :, :], A["ctx_t"][i * 2 + (s + 2)]).then_inc(ctx_loaded[s], 16)

                @block.gpsimd
                def _(pool):
                    nc.gpsimd.memset(v_end[:, :, :], 0.0).then_inc(zeroed, 1)
                    pool.wait_ge(loaded, 64)

                    def front(t, i, s):
                        s = s % 2
                        pool.wait_ge(scored, t * GROUPS + GROUPS)
                        nc.gpsimd.tensor_tensor(
                            q_own[s][:, :, :].rearrange("p c (h q) -> p c h q", q=SEQ),
                            Q[:, :, bass.ds(t * SEQ, SEQ)].rearrange("p c (o q) -> p c o q", o=1).to_broadcast([P, KT, HPC, SEQ]),
                            own[:, :].rearrange("p (c h o) -> p c h o", c=1, o=1).to_broadcast([P, KT, HPC, SEQ]),
                            ALU.mult).then_inc(q_masked, 1)

                    pipelined(pool, BATCH, front, nothing)

                @block.tensor
                def _(pe):
                    pe.wait_ge(loaded, 64)
                    pe.sem_inc(scored, 2 * GROUPS)
                    pe.sem_inc(attended, 2)
                    for c in range(KT):
                        last = nc.tensor.matmul(ps_o[0:BATCH, 0:D], ends[:, c, :], w[:, c, D:2 * D],
                                                start=(c == 0), stop=(c == KT - 1))
                    last.then_inc(end_made, 1)
                    pe.wait_ge(end_copied, 1)
                    pe.wait_ge(end_placed, 64)

                    def front(t, i, s):
                        s = s % 2
                        pe.wait_ge(ctx_loaded[s], i * 16 + 16)
                        pe.wait_ge(k_copied, t + 1)
                        for m in range(KT):
                            for c in range(KT):
                                last = nc.tensor.matmul(ps_k[:, m, 0:CTX], w[:, c, m * P:(m + 1) * P], ctx_t[s][:, c, :],
                                                        start=(c == 0), stop=(c == KT - 1))
                        last.then_inc(k_made, 1)
                        pe.wait_ge(v_copied, t + 1)
                        for n in range(FULL):
                            for c in range(KT):
                                last = nc.tensor.matmul(ps_v[:, n, :], ctx_t[s][:, c, n * P:(n + 1) * P], w[:, c, D:2 * D],
                                                        start=(c == 0), stop=(c == KT - 1))
                        last.then_inc(v_made, 1)

                    def score(t, s, g):
                        s = s % 2
                        if g == 0:
                            pe.wait_ge(k_copied, t + 2)
                            pe.wait_ge(q_masked, t + 1)
                        pe.wait_ge(exps, t * GROUPS + (g + 1))
                        at = (g * P) % (HPC * SEQ)
                        nc.tensor.matmul(ps_s[g % 2][:, 0:CTX], q_own[s][:, g * HPG // HPC, at:at + P],
                                         k_t[s][:, g * HPG // HPC, :], start=True, stop=True).then_inc(scored, 1)

                    def transposes(t, s):
                        s = s % 2
                        pe.wait_ge(exps, t * GROUPS + (GROUPS + 2))
                        pe.wait_ge(t_copied, t * (FULL + 1) + (FULL + 1))
                        for n in range(FULL):
                            for g in range(GROUPS):
                                last = nc.tensor.transpose(ps_t[n % 2][:, g * P:(g + 1) * P],
                                                           probs[s][:, g, n * P:(n + 1) * P], ident[:, :])
                            last.then_inc(turned, 1)

                    def end_transpose(t, s):
                        s = s % 2
                        pe.wait_ge(t_copied, t * (FULL + 1) + (FULL + 2))
                        nc.tensor.transpose(ps_t[0][0:GROUPS, 0:P], probs[s][:, :, CTX - 1], ident[:, :]).then_inc(turned, 1)

                    def values(t, s):
                        s = s % 2
                        pe.wait_ge(t_copied, t * (FULL + 1) + 2 * (FULL + 1) - 1)
                        pe.wait_ge(extracted, t + 1)
                        for n in range(FULL):
                            for g in range(GROUPS):
                                nc.tensor.matmul(ps_o[:, g * W:(g + 1) * W], probs_t[:, n, g * P:(g + 1) * P],
                                                 v[s][:, n, g * W:(g + 1) * W], start=(n == 0 and g == 0), stop=False,
                                                 skip_group_check=True)
                        pe.wait_ge(t_copied, t * (FULL + 1) + 2 * (FULL + 1))
                        nc.tensor.matmul(ps_o[:, 0:D], end_t[:, :], v_end[:, bass.ds(t, 1), :].rearrange("g o d -> g (o d)"),
                                         start=False, stop=True, skip_group_check=True).then_inc(attended, 1)

                    def scores_of(t, s, groups):
                        for g in groups:
                            score(t, s, g)

                    front(0, 0, 0)
                    scores_of(0, 0, range(GROUPS))

                    def turn(i, steps):
                        for k in range(2):
                            t = i * 2 + k
                            nxt, ni, nk = i * 2 + (k + 1), i + (k + 1) // 2, (k + 1) % 2
                            if k < steps:
                                front(nxt, ni, nk)
                            transposes(t, k)
                            if k < steps:
                                scores_of(nxt, nk, range(2))
                            end_transpose(t, k)
                            values(t, k)
                            if k < steps:
                                scores_of(nxt, nk, range(2, GROUPS))

                    with pe.Fori(0, BATCH // 2 - 1) as i:
                        turn(i, 2)
                    turn(BATCH // 2 - 1, 1)

                @block.scalar
                def _(act):
                    act.wait_ge(loaded, 64)
                    act.sem_inc(k_copied, 1)
                    act.sem_inc(v_copied, 1)
                    act.sem_inc(t_copied, FULL + 1)
                    act.sem_inc(exps, 2)
                    act.wait_ge(end_made, 1)
                    nc.scalar.copy(v_end_rows[:, :], ps_o[0:BATCH, 0:D]).then_inc(end_copied, 1)

                    def take_kv(t, s):
                        act.wait_ge(k_made, t + 1)
                        act.wait_ge(scored, t * GROUPS + GROUPS)
                        for c in range(KT):
                            nc.scalar.activation(k_t[s][:, c, :], ps_k[:, c, 0:CTX], ACT.Identity,
                                                 bias=b_k[:, c:c + 1]).then_inc(k_copied if c == KT - 1 else act_acc, 1)
                        act.wait_ge(v_made, t + 1)
                        act.wait_ge(attended, t + 1)
                        nc.scalar.copy(v[s][:, :, :], ps_v[:, :, :]).then_inc(v_copied, 1)

                    def exp(t, s, groups):
                        for g in groups:
                            act.wait_ge(negated, t * GROUPS + (g + 1))
                            nc.scalar.activation(probs[s][:, g, :], ps_s[g % 2][:, 0:CTX], ACT.Exp, bias=row[s][:, 1, g:g + 1],
                                                 accum_out=row[s][:, 2, g:g + 1]).then_inc(exps, 1)

                    def take_turned(t, n):
                        act.wait_ge(turned, t * (FULL + 1) + (n + 1))
                        if n == 0:
                            act.wait_ge(attended, t + 2)
                        if n < FULL:
                            nc.scalar.copy(probs_t[:, n, :], ps_t[n % 2][:, :]).then_inc(t_copied, 1)
                        else:
                            nc.scalar.copy(end_t[:, :], ps_t[0][0:GROUPS, 0:P]).then_inc(t_copied, 1)

                    take_kv(0, 0)
                    exp(0, 0, range(GROUPS))

                    def turn(i, steps):
                        for k in range(2):
                            t, nxt, nk = i * 2 + k, i * 2 + (k + 1), (k + 1) % 2
                            if k < steps:
                                take_kv(nxt, nk)
                            for n in range(FULL + 1):
                                take_turned(t, n)
                            if k < steps:
                                exp(nxt, nk, range(GROUPS))

                    with act.Fori(0, BATCH // 2 - 1) as i:
                        turn(i, 2)
                    turn(BATCH // 2 - 1, 1)

                @block.vector
                def _(dve):
                    dve.sem_inc(extracted, 1)

                    def front(t, i, s):
                        r = row[s % 2]
                        for g in range(GROUPS):
                            dve.wait_ge(scored, t * GROUPS + (2 * GROUPS + g + 1))
                            nc.vector.tensor_reduce(r[:, 0, g:g + 1], ps_s[g % 2][:, 0:CTX], AX.X, ALU.max).then_inc(maxed, 1)
                            dve.wait_ge(maxed, t * GROUPS + (g + 1))
                            nc.vector.tensor_scalar(r[:, 1, g:g + 1], r[:, 0, g:g + 1], -1.0, None,
                                                    ALU.mult).then_inc(negated, 1)

                    def back(t, i, s):
                        r = row[s % 2]
                        dve.wait_ge(exps, t * GROUPS + (GROUPS + 2))
                        nc.vector.reciprocal(r[:, 3, :], r[:, 2, :]).then_inc(summed, 1)
                        dve.wait_ge(summed, t + 1)
                        dve.wait_ge(attended, t + 3)
                        for h in range(HPG):
                            rows = slice(h * SEQ, (h + 1) * SEQ)
                            out = attended_rows[s * SEQ:(s + 1) * SEQ, bass.ds(i, 1), :].rearrange(
                                "p o (g h d) -> p (o g) h d", g=GROUPS, h=HPG)[:, :, h, :]
                            nc.vector.tensor_tensor(
                                out, ps_o[rows, 0:D].rearrange("p (g h d) -> p g h d", g=GROUPS, h=HPG)[:, :, h, :],
                                r[rows, 3, :].rearrange("p (g o) -> p g o", o=1).to_broadcast([SEQ, GROUPS, HD]),
                                ALU.mult).then_inc(extracted if h == HPG - 1 else dve_acc, 1)

                    pipelined(dve, BATCH, front, back, BPT)

        project_rows(nc, "cross0_out", X, attended_rows, ident, A["L0_xattn_Wo"], A["L0_xattn_b_v"], A["L0_xattn_b_o"])


SUBLAYERS[0] = cross_attention_0


def latent_rows(nc, A, X, LT, ident, tail):
    SLOTS = TILES + 1
    with Space(nc, "latents") as sp:
        affine = sp.sb("affine", [P, 4, D])
        rows = sp.sb("rows", [P, SLOTS, D])
        final = sp.sb("final", [P, SLOTS, D])
        stats = [sp.sb(f"stats{k}", [P, n, 6]) for k, n in ((0, TILES), (1, SLOTS))]
        tmp = [sp.sb(f"tmp{k}", [P, 7, n]) for k, n in ((0, TILES), (1, SLOTS))]
        mean = [sp.sb(f"mean{k}", [P, n]) for k, n in ((0, TILES), (1, SLOTS))]
        rstd = [sp.sb(f"rstd{k}", [P, n]) for k, n in ((0, TILES), (1, SLOTS))]
        turned = [sp.ps(f"turned{k}", [P, BANK]) for k in range(2)]
        step, loaded, zeroed, stats_ready, var_ready, root_ready, rows_normed, final_ready, turned_made, copied, stored = (
            sp.sem(n) for n in ("step", "loaded", "zeroed", "stats_ready", "var_ready", "root_ready", "rows_normed",
                                "final_ready", "turned_made", "copied", "stored"))
        with sp.block() as block:

            @block.sync
            def _(sync):
                sync.dma_start(affine[:, :, :], A["affine"]).then_inc(loaded, 16)
                sync.wait_ge(zeroed, 1)
                sync.dma_start(rows[0:BATCH, TILES, :], A["ctx"][:, CTX - 1, :]).then_inc(loaded, 16)
                for t in range(TILES):
                    sync.wait_ge(final_ready, t + 1)
                    sync.dma_start(tail[t * BPT:(t + 1) * BPT, 0:SEQ, :], final[:, t, :]).then_inc(stored, 16)
                sync.wait_ge(final_ready, SLOTS)
                sync.dma_start(tail[:, SEQ, :], final[0:BATCH, TILES, :]).then_inc(stored, 16)
                sync.wait_ge(stored, 16 * SLOTS)

            @block.gpsimd
            def _(pool):
                nc.gpsimd.memset(rows[:, TILES, :], 0.0).then_inc(zeroed, 1)

            @block.scalar
            def _(act):
                for k in range(2):
                    act.wait_ge(var_ready, k + 1)
                    nc.scalar.activation(tmp[k][:, 6, :], tmp[k][:, 5, :], ACT.Sqrt).then_inc(root_ready, 1)
                for t in range(0, TILES, 2):
                    act.wait_ge(turned_made, t // 2 + 1)
                    nc.scalar.copy(LT[:, :, t * P:(t + 2) * P],
                                   turned[t // 2 % 2][:, :].rearrange("p (c n) -> p c n", c=KT)).then_inc(copied, 1)

            @block.vector
            def _(dve):
                chain = Chain(dve, step)
                v = nc.vector
                with dve.Fori(0, TILES) as t:
                    v.bn_stats(stats[0][:, t, :], X[:, t, :]).then_inc(stats_ready, 1)
                dve.wait_ge(stats_ready, TILES)
                norm_moments(dve, stats[0], tmp[0], mean[0][:, :], chain, var_ready)
                dve.wait_ge(root_ready, 1)
                chain.link(v.reciprocal(rstd[0][:, :], tmp[0][:, 6, :]))
                with dve.Fori(0, TILES) as t:
                    v.tensor_scalar(rows[:, t, :], X[:, t, :], mean[0][:, bass.ds(t, 1)], rstd[0][:, bass.ds(t, 1)],
                                    ALU.subtract, ALU.mult).then_inc(rows_normed, 1)
                dve.wait_ge(rows_normed, TILES)
                dve.wait_ge(loaded, 32)
                with dve.Fori(0, SLOTS) as t:
                    v.bn_stats(stats[1][:, t, :], rows[:, t, :]).then_inc(stats_ready, 1)
                dve.wait_ge(stats_ready, TILES + SLOTS)
                norm_moments(dve, stats[1], tmp[1], mean[1][:, :], chain, var_ready)
                dve.wait_ge(root_ready, 2)
                chain.link(v.reciprocal(rstd[1][:, :], tmp[1][:, 6, :]))
                for t in range(SLOTS):
                    gain = 0 if t < TILES else 2
                    chain.link(v.tensor_scalar(rows[:, t, :], rows[:, t, :], mean[1][:, t:t + 1], rstd[1][:, t:t + 1],
                                               ALU.subtract, ALU.mult))
                    chain.link(v.tensor_tensor(rows[:, t, :], rows[:, t, :], affine[:, gain, :], ALU.mult))
                    v.tensor_tensor(final[:, t, :], rows[:, t, :], affine[:, gain + 1, :], ALU.add).then_inc(final_ready, 1)

            @block.tensor
            def _(pe):
                for t in range(0, TILES, 2):
                    pe.wait_ge(final_ready, t + 2)
                    if t >= 4:
                        pe.wait_ge(copied, t // 2 - 1)
                    for n in range(2):
                        for c in range(KT):
                            last = nc.tensor.transpose(turned[t // 2 % 2][:, (2 * c + n) * P:(2 * c + n + 1) * P],
                                                       final[:, t + n, c * P:(c + 1) * P], ident[:, :])
                    last.then_inc(turned_made, 1)


def cross_attention_1(nc, A, X, LT, ident):
    HD = 64
    INNER = HEADS * HD
    CH = INNER // P
    TAIL = SEQ + 1
    FULL = CTX // P
    KEYS = FULL * P + TAIL
    NT = FULL + 1
    tail = nc.dram_tensor("tail_rows", (BATCH, TAIL, D), F32, kind="Internal").ap()
    latent_rows(nc, A, X, LT, ident, tail)
    with Space(nc, "cross1") as sp:
        wq = sp.sb("wq", [P, KT, INNER])
        wk_t = sp.sb("wk_t", [P, CH, D])
        wv = sp.sb("wv", [P, KT, INNER])
        wo = sp.sb("wo", [P, CH, D])
        affine = sp.sb("affine", [P, 2, KT * D])
        minus_half = sp.sb("minus_half", [P, FULL])
        raw = [sp.sb(f"raw{s}", [P, FULL, D]) for s in range(4)]
        kv = [sp.sb(f"kv{s}", [P, NT, D]) for s in range(4)]
        kv_t = [sp.sb(f"kv_t{s}", [P, KT, KEYS]) for s in range(2)]
        stats = sp.sb("stats", [P, FULL, 6])
        tmp = sp.sb("tmp", [P, 7, FULL])
        mean = sp.sb("mean", [P, FULL])
        q_t = sp.sb("q_t", [P, CH, P])
        q_keys = sp.sb("q_keys", [P, KT, BPT, HEADS * SEQ])
        probs = [sp.sb(f"probs{s}", [P, GROUPS, NT * P]) for s in range(2)]
        probs_t = sp.sb("probs_t", [P, NT, GROUPS * P])
        row = [sp.sb(f"row{s}", [P, 4, GROUPS]) for s in range(2)]
        z_t = sp.sb("z_t", [P, KT, HEADS, BPT, SEQ])
        out_t = sp.sb("out_t", [P, CH, P])
        ps_x = sp.ps("ps_x", [P, 2, BANK])
        ps_s = [sp.ps(f"ps_s{s}", [P, BANK]) for s in range(2)]
        ps_t = [sp.ps(f"ps_t{s}", [P, GROUPS * P]) for s in range(2)]
        ps_z = sp.ps("ps_z", [P, 2, BANK])
        names = ("loaded", "half_ready", "var_ready", "roots", "normed", "gained", "scaled", "kv_turned", "kv_copied",
                 "scored", "maxed", "negated", "exps", "summed", "p_scaled", "p_ready", "turned", "t_copied", "z_made", "half_made", "z_copied", "z_copied_1",
                 "q_made", "q_copied", "qk_made", "qk_act", "qk_dve", "o_made", "o_copied", "y_made", "y_added", "step",
                 "stats_ready", "norm_acc", "zeroed")
        S = {n: sp.sem(n) for n in names}
        raw_loaded = [sp.sem(f"raw_loaded{s}") for s in range(4)]
        tail_loaded = [sp.sem(f"tail_loaded{s}") for s in range(4)]

        def schedule(engine, prologue, norm, front_back, tile_front, tile_back, norm_inside=False):
            def call(f, *a):
                if f:
                    f(*a)

            call(norm, 0, 0, 0)
            call(norm, 1, 0, 1)
            call(tile_front, 0)
            call(prologue)

            def turn(i, last):
                for k in range(BPT):
                    more = not (last and k >= BPT - 2)
                    if more and not norm_inside:
                        call(norm, i * BPT + (k + 2), i + (k + 2) // BPT, (k + 2) % BPT)
                    call(front_back, i * BPT + k, i, k, not (last and k == BPT - 1), more)
                    if k == BPT - 2 and not last:
                        call(tile_front, i + 1)
                call(tile_back, i)

            with engine.Fori(0, TILES - 1) as i:
                turn(i, False)
            turn(TILES - 1, True)

        def take_qk(copy, ps, r, odd, sem):
            for c in range(KT):
                src = ps[:, odd, 2 * c * P:(2 * c + 2) * P].rearrange("p (j b q) -> p j b q", j=2, q=SEQ)
                dst = q_keys[:, c, :, :].rearrange("p b (r j o q) -> p r o j b q", r=4, j=2, o=2)[:, r, odd, :, :, :]
                copy(dst, src).then_inc(sem, 1)

        with sp.block() as block:

            @block.sync
            def _(sync):
                for k, name in ((0, "L1_xattn_Wq"), (1, "L1_xattn_WkT"), (2, "L1_xattn_Wv"), (3, "L1_xattn_Wo")):
                    dst = (wq, wk_t, wv, wo)[k]
                    sync.dma_start(dst[:, :, :], A[name]).then_inc(S["loaded"], 16)
                sync.dma_start(affine[:, :, :].rearrange("p a (n d) -> p a n d", n=KT), A["ctx_affine"]).then_inc(S["loaded"], 16)

                def load(t, s):
                    sync.dma_start(raw[s][:, :, :], A["ctx"][t, 0:FULL * P, :].rearrange("(n p) d -> p n d", p=P)
                                   ).then_inc(raw_loaded[s], 16)
                    sync.dma_start(kv[s][0:TAIL, FULL, :], tail[t]).then_inc(tail_loaded[s], 16)

                for s in range(4):
                    load(s, s)
                with sync.Fori(0, BATCH // 4 - 1) as i:
                    for s in range(4):
                        sync.wait_ge(S["z_made"], i * 4 + (s + 1 + 4))
                        load(i * 4 + (s + 4), s)

            @block.gpsimd
            def _(pool):
                for s in range(2):
                    nc.gpsimd.memset(probs[s][:, :, KEYS:], 0.0).then_inc(S["zeroed"], 1)
                nc.gpsimd.memset(minus_half[:, :], -0.5).then_inc(S["half_ready"], 1)
                pool.wait_ge(S["half_ready"], 1)
                pool.wait_ge(S["loaded"], 16 * 5)

                def norm(t, i, s):
                    pool.wait_ge(S["var_ready"], t + 1)
                    nc.gpsimd.tensor_tensor(tmp[:, 6, :], tmp[:, 5, :], minus_half[:, :], ALU.pow).then_inc(S["roots"], 1)
                    pool.wait_ge(S["normed"], t + 1)
                    rows = kv[s][:, 0:FULL, :].rearrange("p n d -> p (n d)")
                    nc.gpsimd.tensor_tensor(rows, rows, affine[:, 0, :], ALU.mult).then_inc(S["gained"], 1)
                    pool.wait_ge(S["gained"], t + 1)
                    nc.gpsimd.tensor_tensor(rows, rows, affine[:, 1, :], ALU.add).then_inc(S["scaled"], 1)

                schedule(pool, None, norm, None, None, None)

            @block.tensor
            def _(pe):
                pe.wait_ge(S["loaded"], 16 * 5)
                pe.wait_ge(S["zeroed"], 2)
                pe.sem_inc(S["scored"], 2 * GROUPS)
                pe.sem_inc(S["z_made"], 4)

                def turn_kv(t, i, s4):
                    pe.wait_ge(S["scaled"], t + 1)
                    pe.wait_ge(tail_loaded[s4], i * 16 + 16)
                    pe.wait_ge(S["kv_copied"], t + 1)
                    pe.wait_ge(S["qk_act"], i * 8 + 8)
                    pe.wait_ge(S["qk_dve"], i * 8 + 8)
                    if s4 != 0:
                        pe.wait_ge(S["o_copied"], i * 2 + 2)
                    for c in range(KT):
                        for n in range(NT):
                            k = P if n < FULL else TAIL
                            last = nc.tensor.transpose(ps_x[:, c, n * P:n * P + k], kv[s4][0:k, n, c * P:(c + 1) * P],
                                                       ident[0:k, 0:k])
                    last.then_inc(S["kv_turned"], 1)

                def score(t, s2, s4, groups):
                    for g in groups:
                        if g == 0:
                            pe.wait_ge(S["kv_copied"], t + 2)
                        pe.wait_ge(S["exps"], t * GROUPS + (g + 1))
                        for c in range(KT):
                            last = nc.tensor.matmul(ps_s[g % 2][:, 0:KEYS], q_keys[:, c, s4, g * P:(g + 1) * P],
                                                    kv_t[s2][:, c, :], start=(c == 0), stop=(c == KT - 1))
                        last.then_inc(S["scored"], 1)

                def turn_probs(t, s2, tiles):
                    for n in tiles:
                        if n == 0:
                            pe.wait_ge(S["p_ready"], t + 1)
                            pe.wait_ge(S["t_copied"], t * NT + NT)
                        if n == 2:
                            pe.wait_ge(S["t_copied"], t * NT + (NT + 1))
                        for g in range(GROUPS):
                            last = nc.tensor.transpose(ps_t[n % 2][:, g * P:(g + 1) * P],
                                                       probs[s2][:, g, n * P:(n + 1) * P], ident[:, :])
                        last.then_inc(S["turned"], 1)

                def attend(t, i, s4, c):
                    pe.wait_ge(S["z_copied_1" if c else "z_copied"], t + 1)
                    if c == 0:
                        pe.wait_ge(S["y_added"], i + 1)
                    for n in range(NT):
                        k = P if n < FULL else TAIL
                        if c == 0:
                            pe.wait_ge(S["t_copied"], t * NT + (NT + n + 1))
                        last = nc.tensor.matmul(ps_z[:, c, :], kv[s4][0:k, n, c * P:(c + 1) * P], probs_t[0:k, n, :],
                                                start=(n == 0), stop=(n == NT - 1))
                    last.then_inc(S["z_made" if c == KT - 1 else "half_made"], 1)

                def prologue():
                    turn_kv(0, 0, 0)
                    score(0, 0, 0, range(GROUPS))

                def front_back(t, i, k, ahead, more):
                    s2, n2, n4, ni = k % 2, (k + 1) % 2, (k + 1) % 4, i + (k + 1) // 4
                    nt = t + 1 if isinstance(t, int) else i * BPT + (k + 1)
                    if ahead:
                        turn_kv(nt, ni, n4)
                    turn_probs(t, s2, range(FULL))
                    if ahead:
                        score(nt, n2, n4, (0, 1))
                    turn_probs(t, s2, (FULL,))
                    attend(t, i, k, 0)
                    if ahead:
                        score(nt, n2, n4, (2, 3))
                    attend(t, i, k, 1)

                def tile_front(i):
                    first = isinstance(i, int) and i == 0
                    if not first:
                        pe.wait_ge(S["kv_copied"], i * BPT + 1)
                    for m in range(CH):
                        for c in range(KT):
                            last = nc.tensor.matmul(ps_x[:, m // 4, (m % 4) * P:(m % 4 + 1) * P], wq[:, c, m * P:(m + 1) * P],
                                                    LT[:, c, bass.ds(i * P, P)], start=(c == 0), stop=(c == KT - 1))
                        if m % 4 == 3:
                            last.then_inc(S["q_made"], 1)
                    for r in range(4):
                        ps = ps_x if r % 2 else ps_z
                        pe.wait_ge(S["q_copied"], i * 2 + (1 if r == 0 else 2))
                        if r == 0 and not first:
                            pe.wait_ge(S["z_copied_1"], i * BPT)
                            pe.wait_ge(S["z_copied"], i * BPT)
                        if r >= 2:
                            pe.wait_ge(S["qk_act"], i * 8 + 2 * (r - 1))
                            pe.wait_ge(S["qk_dve"], i * 8 + 2 * (r - 1))
                        for j in range(2):
                            for c in range(KT):
                                for odd in range(2):
                                    half = slice(64 * odd, 64 * odd + 64)
                                    last = nc.tensor.matmul(ps[:, odd, (2 * c + j) * P:(2 * c + j + 1) * P],
                                                            wk_t[half, 2 * r + j, c * P:(c + 1) * P], q_t[half, 2 * r + j, :],
                                                            start=True, stop=True)
                        last.then_inc(S["qk_made"], 1)

                def tile_back(i):
                    pe.wait_ge(S["z_copied"], i * BPT + (BPT + 1))
                    pe.wait_ge(S["z_copied_1"], i * BPT + (BPT + 1))
                    if not (isinstance(i, int) and i == TILES - 1):
                        pe.wait_ge(S["kv_copied"], i * BPT + (BPT + 2))
                    for h in range(HEADS):
                        half = slice(64 * (h % 2), 64 * (h % 2) + 64)
                        for c in range(KT):
                            last = nc.tensor.matmul(ps_x[half, h // 8, (h // 2 % 4) * P:(h // 2 % 4 + 1) * P],
                                                    wv[:, c, h * HD:(h + 1) * HD],
                                                    z_t[:, c, h, :, :].rearrange("p b q -> p (b q)"),
                                                    start=(c == 0), stop=(c == KT - 1))
                        if h % 8 == 7:
                            last.then_inc(S["o_made"], 1)
                    for m in range(CH):
                        if m % 4 == 0:
                            pe.wait_ge(S["o_copied"], i * 2 + (m // 4 + 3))
                        last = nc.tensor.matmul(ps_z[:, 0, 0:D], out_t[:, m, :], wo[:, m, :], start=(m == 0), stop=(m == CH - 1))
                    last.then_inc(S["y_made"], 1)

                schedule(pe, prologue, None, front_back, tile_front, tile_back)

            @block.scalar
            def _(act):
                act.sem_inc(S["kv_copied"], 1)
                act.sem_inc(S["t_copied"], NT)
                act.sem_inc(S["exps"], 2)
                act.sem_inc(S["o_copied"], 2)
                act.sem_inc(S["z_copied_1"], 1)

                def take_kv(t, s2):
                    act.wait_ge(S["kv_turned"], t + 1)
                    act.wait_ge(S["scored"], t * GROUPS + GROUPS)
                    nc.scalar.copy(kv_t[s2][:, :, :], ps_x[:, :, 0:KEYS]).then_inc(S["kv_copied"], 1)

                def exp(t, s2, groups):
                    for g in groups:
                        act.wait_ge(S["negated"], t * GROUPS + (g + 1))
                        nc.scalar.activation(probs[s2][:, g, 0:KEYS], ps_s[g % 2][:, 0:KEYS], ACT.Exp, bias=row[s2][:, 1, g:g + 1],
                                             accum_out=row[s2][:, 2, g:g + 1]).then_inc(S["exps"], 1)

                def take_turned(t, n):
                    act.wait_ge(S["turned"], t * NT + (n + 1))
                    if n == 0:
                        act.wait_ge(S["z_made"], t + 4)
                    k = P if n < FULL else TAIL
                    nc.scalar.copy(probs_t[0:k, n, :], ps_t[n % 2][0:k, :]).then_inc(S["t_copied"], 1)

                def prologue():
                    take_kv(0, 0)
                    exp(0, 0, range(GROUPS))

                def front_back(t, i, k, ahead, more):
                    s2, n2 = k % 2, (k + 1) % 2
                    nt = i * BPT + (k + 1)
                    if ahead:
                        take_kv(nt, n2)
                    take_turned(t, 0)
                    take_turned(t, 1)
                    if ahead:
                        exp(nt, n2, (0,))
                    take_turned(t, 2)
                    if ahead:
                        exp(nt, n2, (1, 2, 3))
                    act.wait_ge(S["z_made"], t + 5)
                    nc.scalar.copy(z_t[:, 1, :, k, :], ps_z[:, 1, :].rearrange("p (h q) -> p h q", q=SEQ)
                                   ).then_inc(S["z_copied_1"], 1)

                def tile_front(i):
                    for a in range(2):
                        act.wait_ge(S["q_made"], i * 2 + (a + 1))
                        nc.scalar.activation(q_t[:, 4 * a:4 * a + 4, :].rearrange("p m n -> p (m n)"), ps_x[:, a, :], ACT.Copy,
                                             scale=HD ** -0.5).then_inc(S["q_copied"], 1)
                    for r in range(4):
                        ps = ps_x if r % 2 else ps_z
                        act.wait_ge(S["qk_made"], i * 4 + (r + 1))
                        take_qk(nc.scalar.copy, ps, r, 0, S["qk_act"])

                def tile_back(i):
                    for a in range(2):
                        act.wait_ge(S["o_made"], i * 2 + (a + 1))
                        nc.scalar.copy(out_t[:, 4 * a:4 * a + 4, :].rearrange("p m n -> p (m n)"), ps_x[:, a, :]
                                       ).then_inc(S["o_copied"], 1)

                schedule(act, prologue, None, front_back, tile_front, tile_back)

            @block.vector
            def _(dve):
                dve.wait_ge(S["loaded"], 16 * 5)
                dve.sem_inc(S["z_copied"], 1)
                dve.sem_inc(S["y_added"], 1)
                v = nc.vector

                def measure(t, i, s):
                    dve.wait_ge(raw_loaded[s], i * 16 + 16)
                    for n in range(FULL):
                        last = v.bn_stats(stats[:, n, :], raw[s][:, n, :]).then_inc(S["stats_ready"], 1)
                    dve.wait_ge(S["stats_ready"], t * FULL + FULL)
                    norm_moments(dve, stats, tmp, mean[:, :], Chain(dve, S["step"], t * MOMENT_LINKS), S["var_ready"])

                def apply(t, i, s):
                    dve.wait_ge(S["roots"], t + 1)
                    dve.wait_ge(S["z_made"], t + 1)
                    for n in range(FULL):
                        v.tensor_scalar(kv[s][:, n, :], raw[s][:, n, :], mean[:, n:n + 1], tmp[:, 6, n:n + 1],
                                        ALU.subtract, ALU.mult).then_inc(S["normed"] if n == FULL - 1 else S["norm_acc"], 1)

                def norm(t, i, s):
                    measure(t, i, s)
                    apply(t, i, s)

                def maxima(t, s2, groups):
                    r = row[s2]
                    for g in groups:
                        dve.wait_ge(S["scored"], t * GROUPS + (2 * GROUPS + g + 1))
                        v.tensor_reduce(r[:, 0, g:g + 1], ps_s[g % 2][:, 0:KEYS], AX.X, ALU.max).then_inc(S["maxed"], 1)
                        dve.wait_ge(S["maxed"], t * GROUPS + (g + 1))
                        v.tensor_scalar(r[:, 1, g:g + 1], r[:, 0, g:g + 1], -1.0, None, ALU.mult).then_inc(S["negated"], 1)

                def scale(t, s2):
                    r = row[s2]
                    dve.wait_ge(S["exps"], t * GROUPS + (GROUPS + 2))
                    v.reciprocal(r[:, 3, :], r[:, 2, :]).then_inc(S["summed"], 1)
                    dve.wait_ge(S["summed"], t + 1)
                    for g in range(GROUPS):
                        v.tensor_scalar(probs[s2][:, g, 0:KEYS], probs[s2][:, g, 0:KEYS], r[:, 3, g:g + 1], None,
                                        ALU.mult).then_inc(S["p_ready"] if g == GROUPS - 1 else S["p_scaled"], 1)

                def prologue():
                    maxima(0, 0, range(GROUPS))
                    scale(0, 0)

                def front_back(t, i, k, ahead, more):
                    nt, n2 = i * BPT + (k + 1), (k + 1) % 2
                    later = (i * BPT + (k + 2), i + (k + 2) // BPT, (k + 2) % BPT)
                    if ahead:
                        maxima(nt, n2, (0, 1))
                    if more:
                        measure(*later)
                    if ahead:
                        maxima(nt, n2, (2,))
                    if more:
                        apply(*later)
                    if ahead:
                        maxima(nt, n2, (3,))
                        scale(nt, n2)
                    dve.wait_ge(S["half_made"], t + 1)
                    v.tensor_copy(z_t[:, 0, :, k, :], ps_z[:, 0, :].rearrange("p (h q) -> p h q", q=SEQ)
                                  ).then_inc(S["z_copied"], 1)

                def tile_front(i):
                    for r in range(4):
                        ps = ps_x if r % 2 else ps_z
                        dve.wait_ge(S["qk_made"], i * 4 + (r + 1))
                        take_qk(v.tensor_copy, ps, r, 1, S["qk_dve"])

                def tile_back(i):
                    dve.wait_ge(S["y_made"], i + 1)
                    v.tensor_tensor(X[:, bass.ds(i, 1), :].rearrange("p o d -> p (o d)"),
                                    X[:, bass.ds(i, 1), :].rearrange("p o d -> p (o d)"), ps_z[:, 0, 0:D],
                                    ALU.add).then_inc(S["y_added"], 1)

                schedule(dve, prologue, norm, front_back, tile_front, tile_back, norm_inside=True)


SUBLAYERS[3] = cross_attention_1


def mamba(nc, A, X, XT, ident):
    INNER, STATE, CONV, RANK = 2 * D, 16, 4, 16
    CH = INNER // P
    N = TOKENS // 2
    NQ = N // 2
    DBL = RANK + 2 * STATE
    with Space(nc, "mamba") as top:
        H = top.sb("H", [P, KT, TOKENS])
        project_queries(nc, A, XT, H, "mamba_fc1", A["L1_attn_fc1_w"], A["L1_attn_fc1_b"])
        decay = top.sb("decay", [P, CH, STATE])
        diag = top.sb("diag", [P, CH, P])
        w_out = top.sb("w_out", [P, CH, D])
        w_fc2 = top.sb("w_fc2", [P, KT, D])
        b_fc2 = top.sb("b_fc2", [1, D])
        ones = top.sb("ones", [1, P])
        with Space(nc, "mamba_set") as sp:
            a_log = sp.sb("a_log", [P, CH, STATE])
            d = sp.sb("d", [P, CH])
            loaded, exped, ones_set, done = (sp.sem(n) for n in ("loaded", "exped", "ones_set", "done"))
            with sp.block() as block:

                @block.sync
                def _(sync):
                    sync.dma_start(a_log[:, :, :], A["L1_attn_A_log"]).then_inc(loaded, 16)
                    sync.dma_start(d[:, :], A["L1_attn_D"]).then_inc(loaded, 16)
                    sync.dma_start(w_out[:, :, :], A["L1_attn_out_proj_w"]).then_inc(loaded, 16)
                    sync.dma_start(w_fc2[:, :, :], A["L1_attn_fc2_w"]).then_inc(loaded, 16)
                    sync.dma_start(b_fc2[:, :], A["L1_attn_fc2_b"]).then_inc(loaded, 16)
                    sync.wait_ge(loaded, 80)

                @block.gpsimd
                def _(pool):
                    nc.gpsimd.memset(ones[:, :], 1.0).then_inc(ones_set, 1)

                @block.scalar
                def _(act):
                    act.wait_ge(loaded, 80)
                    nc.scalar.activation(a_log[:, :, :], a_log[:, :, :], ACT.Exp).then_inc(exped, 1)

                @block.vector
                def _(dve):
                    dve.wait_ge(loaded, 80)
                    for c in range(CH):
                        nc.vector.tensor_scalar(diag[:, c, :], ident[:, :], d[:, c:c + 1], None, ALU.mult).then_inc(done, 1)
                    dve.wait_ge(exped, 1)
                    nc.vector.tensor_scalar(decay[:, :, :], a_log[:, :, :], -1.0, None, ALU.mult).then_inc(done, 1)

        for half in range(2):
            with Space(nc, f"mamba{half}") as sp:
                u = sp.sb("u", [P, CH, N])
                dt = sp.sb("dt", [P, CH, N])
                dtu = sp.sb("dtu", [P, CH, N])
                gate = sp.sb("gate", [P, CH, N])
                x_dbl = sp.sb("x_dbl", [DBL, N])
                x_parts = sp.sb("x_parts", [DBL, 2, N], F32R)
                mamba_inputs(nc, A, H, half, u, dt, dtu, gate, x_dbl, x_parts, INNER, CONV, RANK, DBL, CH, N)
                mamba_scan(nc, half, ident, decay, diag, u, dt, dtu, gate, x_parts, STATE, RANK, DBL, CH, N, NQ)
                mamba_output(nc, half, X, gate, w_out, w_fc2, b_fc2, ones, CH, N)


def mamba_inputs(nc, A, H, half, u, dt, dtu, gate, x_dbl, x_parts, INNER, CONV, RANK, DBL, CH, N):
    BS = 512
    with Space(nc, f"mamba{half}_in") as sp:
        w_in = sp.sb("w_in", [P, KT, 2 * INNER])
        w_x = sp.sb("w_x", [P, CH, DBL])
        w_dt = sp.sb("w_dt", [RANK, INNER])
        taps = sp.sb("taps", [P, CH, CONV])
        cols = sp.sb("cols", [P, 2, CH])
        one = sp.sb("one", [P, 1])
        xc = sp.sb("xc", [P, CH, N])
        e = sp.sb("e", [P, CH, N])
        conv = e
        lg = sp.sb("lg", [P, CH, N])
        ps = [sp.ps(f"ps{k}", [P, N]) for k in range(4)]
        loaded, one_set, made, taken, tap_step, conv_ready, u_ready, exp_ready, log_ready, acc, step, x_high, dt_ready, acc_pool = (
            sp.sem(n) for n in ("loaded", "one_set", "made", "taken", "tap_step", "conv_ready", "u_ready", "exp_ready",
                                "log_ready", "acc", "step", "x_high", "dt_ready", "acc_pool"))
        with sp.block() as block:

            @block.sync
            def _(sync):
                sync.dma_start(w_in[:, :, :], A["L1_attn_in_proj_w"]).then_inc(loaded, 16)
                sync.dma_start(w_x[:, :, :], A["L1_attn_x_proj_w"]).then_inc(loaded, 16)
                sync.dma_start(w_dt[:, :], A["L1_attn_dt_proj_w"]).then_inc(loaded, 16)
                sync.dma_start(taps[:, :, :], A["L1_attn_conv_w"]).then_inc(loaded, 16)
                sync.dma_start(cols[:, :, :], A["mamba_cols"]).then_inc(loaded, 16)

            @block.gpsimd
            def _(pool):
                nc.gpsimd.memset(one[:, :], 1.0).then_inc(one_set, 1)
                pool.wait_ge(x_high, 1)
                nc.gpsimd.tensor_tensor(x_parts[:, 1, :], x_dbl[:, :], x_parts[:, 0, :], ALU.subtract).then_inc(acc_pool, 1)
                for c in range(CH):
                    pool.wait_ge(dt_ready, c + 1)
                    nc.gpsimd.tensor_tensor(dtu[:, c, :], dt[:, c, :], u[:, c, :], ALU.mult).then_inc(acc_pool, 1)

            @block.tensor
            def _(pe):
                pe.wait_ge(loaded, 80)
                for g in range(3 * CH + 1):
                    if g >= 4:
                        pe.wait_ge(taken, g - 3)
                    if g == 2 * CH:
                        pe.wait_ge(u_ready, CH)
                    if g == 2 * CH + 1:
                        pe.wait_ge(taken, 2 * CH + 1)
                    for n in range(N // BS):
                        cut = slice(n * BS, (n + 1) * BS)
                        if g < 2 * CH:
                            for c in range(KT):
                                last = nc.tensor.matmul(ps[g % 4][:, cut], w_in[:, c, g * P:(g + 1) * P],
                                                        H[:, c, half * N + n * BS:half * N + (n + 1) * BS],
                                                        start=(c == 0), stop=(c == KT - 1))
                        elif g == 2 * CH:
                            for c in range(CH):
                                last = nc.tensor.matmul(ps[g % 4][0:DBL, cut], w_x[:, c, :], u[:, c, cut],
                                                        start=(c == 0), stop=(c == CH - 1))
                        else:
                            m = g - 2 * CH - 1
                            last = nc.tensor.matmul(ps[g % 4][:, cut], w_dt[:, m * P:(m + 1) * P], x_dbl[0:RANK, cut],
                                                    start=True, stop=True)
                    last.then_inc(made, 1)

            @block.scalar
            def _(act):
                act.wait_ge(loaded, 80)
                act.wait_ge(one_set, 1)
                for g in range(CH):
                    act.wait_ge(made, g + 1)
                    nc.scalar.copy(xc[:, g, :], ps[g % 4][:, :]).then_inc(taken, 1)
                for g in range(CH, 2 * CH):
                    act.wait_ge(made, g + 1)
                    nc.scalar.activation(gate[:, g - CH, :], ps[g % 4][:, :], ACT.Silu).then_inc(taken, 1)
                for c in range(CH):
                    act.wait_ge(conv_ready, c + 1)
                    nc.scalar.activation(u[:, c, :], conv[:, c, :], ACT.Silu, bias=cols[:, 0, c:c + 1]).then_inc(u_ready, 1)
                act.wait_ge(made, 2 * CH + 1)
                nc.scalar.copy(x_dbl[:, :], ps[2 * CH % 4][0:DBL, :]).then_inc(taken, 1)
                act.wait_ge(taken, 2 * CH + 1)
                nc.scalar.copy(x_parts[:, 0, :], x_dbl[:, :]).then_inc(x_high, 1)
                for c in range(CH):
                    g = 2 * CH + 1 + c
                    act.wait_ge(made, g + 1)
                    nc.scalar.activation(lg[:, c, :], ps[g % 4][:, :], ACT.Abs, bias=cols[:, 1, c:c + 1]).then_inc(acc, 1)
                    nc.scalar.activation(dt[:, c, :], ps[g % 4][:, :], ACT.Relu, bias=cols[:, 1, c:c + 1]).then_inc(taken, 1)
                for c in range(CH):
                    act.wait_ge(acc, c + 1)
                    nc.scalar.activation(e[:, c, :], lg[:, c, :], ACT.Exp, scale=-1.0).then_inc(exp_ready, 1)
                for c in range(CH):
                    act.wait_ge(exp_ready, c + 1)
                    nc.scalar.activation(lg[:, c, :], e[:, c, :], ACT.Ln, bias=one[:, 0:1]).then_inc(log_ready, 1)

            @block.vector
            def _(dve):
                dve.wait_ge(loaded, 80)
                chain = Chain(dve, tap_step)
                v = nc.vector
                seqs = lambda a: a.rearrange("p (b s) -> p b s", s=SEQ)
                for c in range(CH):
                    dve.wait_ge(taken, c + 1)
                    x, y = seqs(xc[:, c, :]), seqs(conv[:, c, :])
                    chain.link(v.tensor_scalar(y, x, taps[:, c, CONV - 1:CONV], None, ALU.mult))
                    for back in range(1, CONV):
                        last = v.scalar_tensor_tensor(y[:, :, back:], x[:, :, 0:SEQ - back], taps[:, c, CONV - 1 - back:CONV - back],
                                                      y[:, :, back:], ALU.mult, ALU.add)
                        if back < CONV - 1:
                            chain.link(last)
                    last.then_inc(conv_ready, 1)
                fix = Chain(dve, step)
                for c in range(CH):
                    dve.wait_ge(exp_ready, c + 1)
                    fix.link(v.tensor_scalar(xc[:, c, :], e[:, c, :], 1.0, 1.0, ALU.add, ALU.subtract))
                    fix.link(v.tensor_tensor(xc[:, c, :], e[:, c, :], xc[:, c, :], ALU.subtract))
                    dve.wait_ge(taken, 2 * CH + 2 + c)
                    fix.link(v.tensor_tensor(xc[:, c, :], dt[:, c, :], xc[:, c, :], ALU.add))
                for c in range(CH):
                    dve.wait_ge(log_ready, c + 1)
                    v.tensor_tensor(dt[:, c, :], lg[:, c, :], xc[:, c, :], ALU.add).then_inc(dt_ready, 1)


def mamba_scan(nc, half, ident, decay, diag, u, dt, dtu, gate, x_parts, STATE, RANK, DBL, CH, N, NQ):
    UN = 2 * CH
    with Space(nc, f"mamba{half}_scan") as sp:
        pick = [[sp.sb(f"pick{k}{s}", [DBL, P], F32R) for s in range(2)] for k in range(2)]
        b_all = [sp.sb(f"b_all{s}", [P, NQ]) for s in range(2)]
        dec = [sp.sb(f"dec{s}", [P, NQ]) for s in range(CH)]
        inp = [sp.sb(f"inp{s}", [P, NQ]) for s in range(CH)]
        h = [sp.sb(f"h{s}", [P, NQ]) for s in range(CH)]
        hc = [sp.sb(f"hc{s}", [P, NQ]) for s in range(CH)]
        ps_b = [sp.ps(f"ps_b{s}", [P, NQ]) for s in range(2)]
        ps_c = [sp.ps(f"ps_c{s}", [P, NQ]) for s in range(2)]
        ps_y = sp.ps("ps_y", [P, CH, NQ])
        picked, spread = ([sp.sem(f"{name}_{k}") for k in "bc"] for name in ("picked", "spread"))
        zeroed, b_copied, decayed, fed, scanned, weighed, summed, gated = (
            sp.sem(n) for n in ("zeroed", "b_copied", "decayed", "fed", "scanned", "weighed", "summed", "gated"))
        with sp.block() as block:

            @block.gpsimd
            def _(pool):
                for s in range(CH):
                    nc.gpsimd.memset(dec[s][:, :], 0.0).then_inc(zeroed, 1)
                pool.sem_inc(fed, 2 * CH)
                for q in range(2):
                    def front(n, i, s):
                        n = n + q * STATE
                        pool.wait_ge(b_copied, n + 3)
                        for c in range(CH):
                            pool.wait_ge(scanned, n * CH + (c + 1))
                            nc.gpsimd.tensor_tensor(inp[c][:, :], dtu[:, c, q * NQ:(q + 1) * NQ], b_all[s][:, :],
                                                    ALU.mult).then_inc(fed, 1)

                    pipelined(pool, STATE, front, nothing)

            @block.scalar
            def _(act):
                act.wait_ge(zeroed, CH)
                act.sem_inc(b_copied, 2)
                for q in range(2):
                    def copy_b(n, s):
                        g = n + q * STATE
                        act.wait_ge(spread[0], g + 3)
                        act.wait_ge(fed, g * CH + CH)
                        nc.scalar.copy(b_all[s][:, :], ps_b[s][:, :]).then_inc(b_copied, 1)

                    def choose(k, n, s):
                        act.wait_ge(spread[k], n + (q * STATE + 1))
                        nc.scalar.copy(pick[k][s][:, :], ident[0:DBL, bass.ds(n + (RANK + k * STATE), 1)].to_broadcast([DBL, P])
                                       ).then_inc(picked[k], 1)

                    def front(n, i, s):
                        choose(1, n, s)
                        if not (isinstance(n, int) and n == STATE - 1):
                            choose(0, n + 1, 1 - s)

                    choose(0, 0, 0)
                    copy_b(0, 0)

                    def back(n, i, s):
                        g = n + q * STATE
                        for c in range(CH):
                            if c == 2 and not (isinstance(n, int) and n == STATE - 1):
                                copy_b(i * 2 + (s + 1), (s + 1) % 2)
                            act.wait_ge(scanned, g * CH + (c + 1))
                            rows = dt[:, c, q * NQ:(q + 1) * NQ].rearrange("p (b s) -> p b s", s=SEQ)
                            nc.scalar.activation(dec[c][:, :].rearrange("p (b s) -> p b s", s=SEQ)[:, :, 1:], rows[:, :, 1:],
                                                 ACT.Exp, scale=decay[:, c, bass.ds(n, 1)]).then_inc(decayed, 1)

                    pipelined(act, STATE, front, back)

            @block.tensor
            def _(pe):
                for k in range(2):
                    pe.sem_inc(spread[k], 2)
                pe.sem_inc(summed, CH)
                for q in range(2):
                    def spread_row(k, n, s):
                        g = n + q * STATE
                        pe.wait_ge(picked[k], g + 1)
                        if k == 0:
                            pe.wait_ge(b_copied, g + 1)
                        else:
                            pe.wait_ge(weighed, g * CH + CH)
                        for part in range(2):
                            last = nc.tensor.matmul((ps_b, ps_c)[k][s][:, :], pick[k][s][:, :], x_parts[:, part, q * NQ:(q + 1) * NQ],
                                                    start=(part == 0), stop=(part == 1))
                        last.then_inc(spread[k], 1)

                    def front(n, i, s):
                        spread_row(1, n, s)
                        if not (isinstance(n, int) and n == STATE - 1):
                            spread_row(0, n + 1, 1 - s)

                    spread_row(0, 0, 0)
                    if q:
                        pe.wait_ge(gated, q * CH)
                    for c in range(CH):
                        nc.tensor.matmul(ps_y[:, c, :], diag[:, c, :], u[:, c, q * NQ:(q + 1) * NQ], start=True, stop=False,
                                         skip_group_check=True)

                    def back(n, i, s):
                        n = n + q * STATE
                        for c in range(CH):
                            pe.wait_ge(weighed, n * CH + (c + 1 + 2 * CH))
                            nc.tensor.matmul(ps_y[:, c, :], ident[:, :], hc[c][:, :], start=False, stop=False,
                                             skip_group_check=True).then_inc(summed, 1)

                    pipelined(pe, STATE, front, back)

            @block.vector
            def _(dve):
                dve.sem_inc(scanned, CH)
                dve.sem_inc(weighed, 2 * CH)
                for q in range(2):
                    def scan(t, i, k):
                        g = t + q * STATE * CH
                        dve.wait_ge(decayed, g + 1)
                        dve.wait_ge(fed, g + (1 + 2 * CH))
                        dve.wait_ge(weighed, g + (1 + CH))
                        nc.vector.tensor_tensor_scan(h[k % CH][:, :], dec[k % CH][:, :], inp[k % CH][:, :], 0.0, ALU.mult, ALU.add
                                                     ).then_inc(scanned, 1)

                    def weigh(t, i, k):
                        g = t + q * STATE * CH
                        dve.wait_ge(scanned, g + (CH + 1))
                        if k % CH == 0:
                            dve.wait_ge(spread[1], i * 2 + (k // CH + q * STATE + 3))
                        dve.wait_ge(summed, g + 1)
                        nc.vector.tensor_tensor(hc[k % CH][:, :], h[k % CH][:, :], ps_c[k // CH][:, :], ALU.mult).then_inc(weighed, 1)

                    pipelined(dve, STATE * CH, scan, weigh, UN)
                    dve.wait_ge(summed, (q + 1) * STATE * CH + CH)
                    for c in range(CH):
                        out = gate[:, c, q * NQ:(q + 1) * NQ]
                        nc.vector.tensor_tensor(out, out, ps_y[:, c, :], ALU.mult).then_inc(gated, 1)


def mamba_output(nc, half, X, gated, w_out, w_fc2, b_fc2, ones, CH, N):
    BS = 512
    with Space(nc, f"mamba{half}_out") as sp:
        mid = sp.sb("mid", [P, KT, N])
        ps_m = [sp.ps(f"ps_m{s}", [P, KT, BS]) for s in range(2)]
        ps_y = [sp.ps(f"ps_y{s}", [P, BANK]) for s in range(2)]
        made, copied, y_made, added = (sp.sem(n) for n in ("made", "copied", "y_made", "added"))
        with sp.block() as block:

            @block.tensor
            def _(pe):
                for n in range(N // BS):
                    for m in range(KT):
                        for c in range(CH):
                            last = nc.tensor.matmul(ps_m[n][:, m, :], w_out[:, c, m * P:(m + 1) * P],
                                                    gated[:, c, n * BS:(n + 1) * BS], start=(c == 0), stop=(c == CH - 1))
                    last.then_inc(made, 1)
                for t in range(N // P):
                    pe.wait_ge(copied, t * P // BS + 1)
                    if t >= 2:
                        pe.wait_ge(added, t - 1)
                    nc.tensor.matmul(ps_y[t % 2][:, 0:D], ones[:, :], b_fc2[:, :], start=True, stop=False)
                    for c in range(KT):
                        last = nc.tensor.matmul(ps_y[t % 2][:, 0:D], mid[:, c, t * P:(t + 1) * P], w_fc2[:, c, :],
                                                start=False, stop=(c == KT - 1))
                    last.then_inc(y_made, 1)

            @block.scalar
            def _(act):
                for n in range(N // BS):
                    act.wait_ge(made, n + 1)
                    nc.scalar.copy(mid[:, :, n * BS:(n + 1) * BS], ps_m[n][:, :, :]).then_inc(copied, 1)

            @block.vector
            def _(dve):
                for t in range(N // P):
                    tile = half * (N // P) + t
                    dve.wait_ge(y_made, t + 1)
                    nc.vector.tensor_tensor(X[:, tile, :], X[:, tile, :], ps_y[t % 2][:, 0:D], ALU.add).then_inc(added, 1)


SUBLAYERS[4] = mamba


def _by_partition(w):
    return w.reshape(-1, 128, w.shape[-1]).transpose(1, 0, 2)


def _expert_layout(w_gate, w_up, w_down, fp):
    e, f, d = w_gate.shape
    gu = np.concatenate([w_gate, w_up], axis=1).transpose(0, 2, 1).reshape(e, d // 128, 128, 2 * f).transpose(0, 2, 1, 3)
    dn = w_down.transpose(0, 2, 1).reshape(e, f // fp, fp, d).transpose(0, 2, 1, 3)
    return gu, dn


def _alibi():
    head = np.arange(HPG)[:, None, None, None] + HPG * np.arange(GROUPS)[None, None, :, None]
    query, key = np.arange(SEQ)[None, :, None, None], np.arange(SEQ)[None, None, None, :]
    slope = (1.0 / (2.0 ** 8) ** ((head + 1) / HEADS)).astype(np.float32)
    bias = np.where(key <= query, slope * (key - query).astype(np.float32), np.float32(NEG))
    return bias.astype(np.float32).reshape(P, GROUPS, SEQ)


def _own(width, value):
    return (np.arange(P)[:, None] // width == np.arange(P // width)).astype(np.float32) * np.float32(value)


def _lay_out(v):
    a = {"x": v["x"]}
    a["alibi"] = _alibi()
    a["own16"] = _own(16, 1 / 16)
    a["own4"] = _own(16, 1 / 4)
    ctx_t = v["ctx_1024"].transpose(0, 2, 1).reshape(BATCH, KT, P, CTX).transpose(0, 2, 1, 3)
    a["ctx_t"], a["ctx_ends"] = ctx_t, ctx_t[:, :, :, -1].transpose(1, 2, 0)
    for n in ("Wq", "Wo"):
        a[f"L0_xattn_{n}"] = _by_partition(v[f"L0_xattn_{n}"])
    a["L0_xattn_Wkv"] = _by_partition(np.concatenate([v["L0_xattn_Wk"], v["L0_xattn_Wv"]], axis=1))
    for n in ("b_q", "b_k", "b_v"):
        a[f"L0_xattn_{n}"] = v[f"L0_xattn_{n}"].reshape(KT, P).T
    a["L0_xattn_b_o"] = v["L0_xattn_b_o"].reshape(1, D)
    a["ctx"] = v["ctx_1024"]
    latent, context = (np.stack([v[f"L1_xattn_{n}_g"], v[f"L1_xattn_{n}_b"]]) for n in ("ln2", "ln1"))
    a["affine"] = np.broadcast_to(np.concatenate([latent, context]), (P, 4, D))
    a["ctx_affine"] = np.broadcast_to(context[:, None, :], (P, 2, 2, D))
    a["L1_xattn_Wq"], a["L1_xattn_Wo"] = _by_partition(v["L1_xattn_Wq"]), _by_partition(v["L1_xattn_Wo"])
    a["L1_xattn_WkT"] = _by_partition(v["L1_xattn_Wkv"][:, :1024].T)
    a["L1_xattn_Wv"] = _by_partition(v["L1_xattn_Wkv"][:, 1024:])
    for n in ("fc1", "in_proj", "x_proj", "out_proj", "fc2"):
        a[f"L1_attn_{n}_w"] = _by_partition(v[f"L1_attn_{n}_w"].T)
    a["L1_attn_dt_proj_w"] = v["L1_attn_dt_proj_w"].T
    a["L1_attn_fc1_b"], a["L1_attn_D"] = v["L1_attn_fc1_b"].reshape(-1, P).T, v["L1_attn_D"].reshape(-1, P).T
    a["L1_attn_fc2_b"] = v["L1_attn_fc2_b"].reshape(1, D)
    a["L1_attn_A_log"], a["L1_attn_conv_w"] = _by_partition(v["L1_attn_A_log"]), _by_partition(v["L1_attn_conv_w"])
    a["mamba_cols"] = np.stack([v["L1_attn_conv_b"].reshape(-1, P).T, v["L1_attn_dt_proj_b"].reshape(-1, P).T], axis=1)
    slot = np.arange(P, dtype=np.float32)
    a["codes"] = np.broadcast_to(HALF - np.arange(HALF, dtype=np.float32), (P, HALF))
    ends = [np.full(P, HALF), np.full(P, 2 * HALF), np.where(slot < REST, HALF, 2 * HALF)]
    a["slot_base"] = np.stack([e - TOKENS - slot for e in ends] + [TOKENS + slot], axis=1).astype(np.float32)
    a["L0_attn_w"] = _by_partition(v["L0_attn_W_kqv"].T)
    a["L0_ffn_gate_w"] = _by_partition(v["L0_ffn_gate_w"].T)
    a["L0_ffn_up"], a["L0_ffn_down"] = _expert_layout(v["L0_ffn_w_gate"], v["L0_ffn_w_up"], v["L0_ffn_w_down"], 96)
    a["L1_ffn_gate_w"] = _by_partition(v["L1_ffn_gate_w"].T)
    a["L1_ffn_up"], a["L1_ffn_down"] = _expert_layout(
        np.concatenate([v["L1_ffn_w1"], v["L1_ffn_sw1"][None]]), np.concatenate([v["L1_ffn_w3"], v["L1_ffn_sw3"][None]]),
        np.concatenate([v["L1_ffn_w2"], v["L1_ffn_sw2"][None]]), 128)
    return a


def kernel(**inputs):
    import concourse.bacc as bacc
    from concourse.bass_utils import run_bass_kernel_spmd

    arrays = {n: np.ascontiguousarray(a) for n, a in _lay_out({n: np.asarray(a) for n, a in inputs.items()}).items()}
    nc = bacc.Bacc("TRN2", target_bir_lowering=False, num_devices=1)
    aps = {n: nc.dram_tensor(f"in_{n}", a.shape, mybir.dt.from_np(a.dtype), kind="ExternalInput").ap() for n, a in arrays.items()}
    out = nc.dram_tensor("out", (BATCH, SEQ, D), F32, kind="ExternalOutput").ap()
    build_program(nc, aps, out)
    result = run_bass_kernel_spmd(nc, [{f"in_{n}": a for n, a in arrays.items()}], core_ids=[0])
    return result.results[0]["out"]
```

```python
import numpy as np
import concourse.bass as bass
from concourse import mybir
from contextlib import ExitStack

F32 = mybir.dt.float32
F32R = mybir.dt.float32r
ALU = mybir.AluOpType
ACT = mybir.ActivationFunctionType
AX = mybir.AxisListType

BATCH, SEQ, D = 64, 32, 256
CTX = 257
TOKENS = BATCH * SEQ
P = 128
TILES = TOKENS // P
BPT = P // SEQ
KT = D // P
BANK = 512
HEADS = 16
HPG = P // SEQ
GROUPS = HEADS // HPG
EPS = 1e-5
NEG = -1e30


class Chain:

    def __init__(self, engine, sem, base=0):
        self.engine, self.sem, self.base, self.n = engine, sem, base, 0

    def link(self, instruction):
        self.n += 1
        instruction.then_inc(self.sem, 1)
        self.engine.wait_ge(self.sem, self.base + self.n)


class Space:

    used = []

    def __init__(self, nc, stage):
        self.nc, self.stage, self.ctx = nc, stage, ExitStack()

    @classmethod
    def clear_used(cls, nc):
        nc.clear_and_free_semaphores(cls.used)
        cls.used = []
        nc.all_engine_barrier()

    def __enter__(self):
        return self

    def __exit__(self, *error):
        return self.ctx.__exit__(*error)

    def sb(self, name, shape, dt=F32):
        return self.ctx.enter_context(self.nc.sbuf_tensor(f"{self.stage}_{name}", shape, dt))

    def ps(self, name, shape, dt=F32):
        return self.ctx.enter_context(self.nc.psum_tensor(f"{self.stage}_{name}", shape, dt))

    def sem(self, name):
        self.used.append(self.nc.alloc_semaphore(f"{self.stage}_{name}"))
        return self.used[-1]

    def block(self):
        return self.nc.Block()


def load_state(nc, x, X, ident):
    with Space(nc, "load") as sp, sp.block() as block:
        loaded, zeroed = sp.sem("loaded"), sp.sem("zeroed")

        @block.sync
        def _(sync):
            rows = x.rearrange("b s d -> (b s) d").rearrange("(t p) d -> p t d", p=P)
            sync.dma_start(X[:, 0:TILES // 2, :], rows[:, 0:TILES // 2, :]).then_inc(loaded, 16)
            sync.wait_ge(loaded, 32)

        @block.scalar
        def _(act):
            rows = x.rearrange("b s d -> (b s) d").rearrange("(t p) d -> p t d", p=P)
            act.dma_start(X[:, TILES // 2:, :], rows[:, TILES // 2:, :]).then_inc(loaded, 16)

        @block.gpsimd
        def _(pool):
            nc.gpsimd.memset(ident[:, :], 0.0).then_inc(zeroed, 1)
            pool.wait_ge(zeroed, 1)
            nc.gpsimd.affine_select(out=ident[:, :], in_=ident[:, :], compare_op=ALU.not_equal, fill=1.0,
                                    base=0, pattern=[[-1, P]], channel_multiplier=1).then_inc(zeroed, 1)


def store_state(nc, out, X):
    with Space(nc, "store") as sp, sp.block() as block:
        stored = sp.sem("stored")
        rows = out.rearrange("b s d -> (b s) d").rearrange("(t p) d -> p t d", p=P)

        @block.sync
        def _(sync):
            sync.dma_start(rows[:, 0:TILES // 2, :], X[:, 0:TILES // 2, :]).then_inc(stored, 16)
            sync.wait_ge(stored, 32)

        @block.scalar
        def _(act):
            act.dma_start(rows[:, TILES // 2:, :], X[:, TILES // 2:, :]).then_inc(stored, 16)
            act.wait_ge(stored, 32)


def norm_moments(dve, stats, tmp, mean, chain, var_ready):
    mean_even, sum_even, mean_odd, sum_odd = (stats[:, :, k] for k in (1, 2, 4, 5))
    chain.link(dve.tensor_tensor(tmp[:, 0, :], mean_even, mean_odd, ALU.add))
    chain.link(dve.tensor_tensor(tmp[:, 1, :], mean_even, mean_odd, ALU.subtract))
    chain.link(dve.tensor_tensor(tmp[:, 2, :], sum_even, sum_odd, ALU.add))
    chain.link(dve.tensor_scalar(mean, tmp[:, 0, :], 0.5, None, ALU.mult))
    chain.link(dve.scalar_tensor_tensor(tmp[:, 3, :], tmp[:, 1, :], 0.25, tmp[:, 1, :], ALU.mult, ALU.mult))
    chain.link(dve.scalar_tensor_tensor(tmp[:, 4, :], tmp[:, 2, :], 1.0 / D, tmp[:, 3, :], ALU.mult, ALU.add))
    dve.tensor_scalar(tmp[:, 5, :], tmp[:, 4, :], EPS, None, ALU.add).then_inc(var_ready, 1)


MOMENT_LINKS = 6


def norm_transposed(nc, stage, X, XT, ident, table=None):
    with Space(nc, stage + "_norm") as sp:
        stats = sp.sb("stats", [P, TILES, 6])
        tmp = sp.sb("tmp", [P, 7, TILES])
        mean = sp.sb("mean", [P, TILES])
        rstd = sp.sb("rstd", [P, TILES])
        xn = sp.sb("xn", [P, 4, D])
        turned = [sp.ps(f"turned{k}", [P, BANK]) for k in range(2)]
        step, stats_ready, var_ready, root_ready = (sp.sem(n) for n in ("step", "stats_ready", "var_ready", "root_ready"))
        rows_ready, turned_pairs, copied_pairs = (sp.sem(n) for n in ("rows_ready", "turned_pairs", "copied_pairs"))
        stored = sp.sem("stored")
        with sp.block() as block:

            if table is not None:
                @block.sync
                def _(sync):
                    rows = table[0:TOKENS, 0:D].rearrange("(t p) d -> p t d", p=P)
                    sync.sem_inc(stored, 16)
                    with sync.Fori(0, TILES // 4) as i:
                        sync.wait_ge(rows_ready, i * 4 + 4)
                        sync.dma_start(rows[:, bass.ds(i * 4, 4), :], xn[:, :, :]).then_inc(stored, 16)
                    sync.wait_ge(stored, 16 * (TILES // 4) + 16)

            @block.vector
            def _(dve):
                for t in range(TILES):
                    nc.vector.bn_stats(stats[:, t, :], X[:, t, :]).then_inc(stats_ready, 1)
                dve.wait_ge(stats_ready, TILES)
                chain = Chain(dve, step)
                norm_moments(dve, stats, tmp, mean[:, :], chain, var_ready)
                dve.wait_ge(root_ready, 1)
                chain.link(nc.vector.reciprocal(rstd[:, :], tmp[:, 6, :]))
                with dve.Fori(0, TILES // 4) as i:
                    for k in range(4):
                        if k % 2 == 0:
                            dve.wait_ge(turned_pairs, i * 2 + (k // 2 + 1))
                        if k == 0 and table is not None:
                            dve.wait_ge(stored, i * 16 + 16)
                        t = i * 4 + k
                        nc.vector.tensor_scalar(xn[:, k, :], X[:, t, :], mean[:, bass.ds(t, 1)], rstd[:, bass.ds(t, 1)],
                                                ALU.subtract, ALU.mult).then_inc(rows_ready, 1)

            @block.scalar
            def _(act):
                act.sem_inc(copied_pairs, 2)
                act.wait_ge(var_ready, 1)
                nc.scalar.activation(tmp[:, 6, :], tmp[:, 5, :], ACT.Sqrt).then_inc(root_ready, 1)
                with act.Fori(0, TILES // 4) as i:
                    for k in range(2):
                        act.wait_ge(turned_pairs, i * 2 + (k + 3))
                        nc.scalar.copy(XT[:, :, bass.ds(i * (4 * P) + k * 2 * P, 2 * P)],
                                       turned[k][:, :].rearrange("p (c n) -> p c n", c=KT)).then_inc(copied_pairs, 1)

            @block.tensor
            def _(pe):
                pe.sem_inc(turned_pairs, 2)
                with pe.Fori(0, TILES // 4) as i:
                    for k in range(2):
                        pe.wait_ge(copied_pairs, i * 2 + (k + 1))
                        for n in range(2):
                            pe.wait_ge(rows_ready, i * 4 + (2 * k + n + 1))
                            for c in range(KT):
                                last = nc.tensor.transpose(turned[k][:, (2 * c + n) * P:(2 * c + n + 1) * P],
                                                           xn[:, 2 * k + n, c * P:(c + 1) * P], ident[:, :])
                        last.then_inc(turned_pairs, 1)


def route(nc, stage, XT, gate, experts, top_k, eps, W):
    with Space(nc, stage + "_route") as sp:
        gate_w = sp.sb("gate_w", [P, KT, experts])
        shifted = sp.sb("shifted", [P, TILES, experts])
        probs = sp.sb("probs", [P, TILES, experts])
        rest = sp.sb("rest", [P, TILES, experts])
        best = sp.sb("best", [P, TILES, 8])
        row = sp.sb("row", [P, 4, TILES])
        logits = sp.ps("logits", [P, TILES, experts])
        loaded, logits_ready, shifted_ready, exp_ready, step = (
            sp.sem(n) for n in ("loaded", "logits_ready", "shifted_ready", "exp_ready", "step"))

        def wide(column):
            return column.rearrange("p (t o) -> p t o", o=1).to_broadcast([P, TILES, experts])

        with sp.block() as block:

            @block.sync
            def _(sync):
                sync.dma_start(gate_w[:, :, :], gate).then_inc(loaded, 16)

            @block.tensor
            def _(pe):
                pe.wait_ge(loaded, 16)
                for t in range(TILES):
                    for c in range(KT):
                        last = nc.tensor.matmul(logits[:, t, :], XT[:, c, t * P:(t + 1) * P], gate_w[:, c, :],
                                                start=(c == 0), stop=(c == KT - 1))
                last.then_inc(logits_ready, 1)

            @block.scalar
            def _(act):
                act.wait_ge(shifted_ready, 1)
                nc.scalar.activation(probs[:, :, :], shifted[:, :, :], ACT.Exp).then_inc(exp_ready, 1)

            @block.vector
            def _(dve):
                chain = Chain(dve, step)
                link = chain.link
                dve.wait_ge(logits_ready, 1)
                link(nc.vector.tensor_reduce(row[:, 0, :], logits[:, :, :], AX.X, ALU.max))
                nc.vector.tensor_tensor(shifted[:, :, :], logits[:, :, :], wide(row[:, 0, :]),
                                        ALU.subtract).then_inc(shifted_ready, 1)
                dve.wait_ge(exp_ready, 1)
                link(nc.vector.tensor_reduce(row[:, 1, :], probs[:, :, :], AX.X, ALU.add))
                link(nc.vector.reciprocal(row[:, 2, :], row[:, 1, :]))
                link(nc.vector.tensor_tensor(probs[:, :, :], probs[:, :, :], wide(row[:, 2, :]), ALU.mult))
                for t in range(TILES):
                    last = nc.vector.max(best[:, t, :], probs[:, t, :])
                link(last)
                if top_k < 8:
                    link(nc.vector.memset(best[:, :, top_k:8], -1.0))
                for t in range(TILES):
                    last = nc.vector.match_replace(rest[:, t, :], best[:, t, :], probs[:, t, :], 0.0)
                link(last)
                link(nc.vector.tensor_tensor(probs[:, :, :], probs[:, :, :], rest[:, :, :], ALU.subtract))
                link(nc.vector.tensor_reduce(row[:, 1, :], probs[:, :, :], AX.X, ALU.add))
                if eps:
                    link(nc.vector.tensor_scalar(row[:, 1, :], row[:, 1, :], eps, None, ALU.add))
                link(nc.vector.reciprocal(row[:, 3, :], row[:, 1, :]))
                link(nc.vector.tensor_tensor(W[:, :, 0:experts], probs[:, :, :], wide(row[:, 3, :]), ALU.mult))
                if W.shape[2] > experts:
                    link(nc.vector.memset(W[:, :, experts:], 1.0))


def experts_sum(nc, stage, X, XT, W, w_up, w_down, n_experts, FP, FT):
    NB = 512
    CHUNKS = TOKENS // NB
    TPC = NB // P
    PAIRS = 2 * CHUNKS * FT
    PRODUCTS = ((0, 0), (0, 1), (1, 0))
    with Space(nc, stage + "_experts") as sp:
        x = [sp.sb(f"x{k}", [P, KT, TOKENS], F32R) for k in range(2)]
        wgu = [sp.sb(f"wgu{s}", [P, KT, 2 * FT * FP]) for s in range(2)]
        wd = [sp.sb(f"wd{s}", [FP, FT, D]) for s in range(2)]
        wgu_parts = [[sp.sb(f"wgu{s}_{k}", [P, KT, 2 * FT * FP], F32R) for k in range(2)] for s in range(2)]
        wd_parts = [[sp.sb(f"wd{s}_{k}", [FP, FT, D], F32R) for k in range(2)] for s in range(2)]
        gated = sp.sb("gated", [FP, 2, NB])
        hidden = sp.sb("hidden", [FP, 2, NB])
        hidden_parts = [[sp.sb(f"hidden{s}_{k}", [FP, FT, NB], F32R) for k in range(2)] for s in range(2)]
        pair = [sp.ps(f"pair{s}", [FP, 2, NB]) for s in range(2)]
        y = [sp.ps(f"y{s}", [P, TPC, D]) for s in range(2)]
        w_loaded = [sp.sem(f"w_loaded{s}") for s in range(2)]
        x_high, x_low, w_high, w_low, hidden_high, hidden_low = (
            sp.sem(n) for n in ("x_high", "x_low", "w_high", "w_low", "hidden_high", "hidden_low"))
        pair_made, gate_made, hidden_made, y_made, combined = (
            sp.sem(n) for n in ("pair_made", "gate_made", "hidden_made", "y_made", "combined"))
        acc = sp.sem("acc")

        def run(engine, body):
            odd = n_experts % 2
            body(0, 2, True, False)
            with engine.Fori(1, n_experts // 2 - (1 - odd)) as i:
                body(i, 2, False, False)
            body(n_experts // 2 - (1 - odd), 2 - odd, False, True)

        with sp.block() as block:

            @block.sync
            def _(sync):
                def load(e, s):
                    sync.dma_start(wgu[s][:, :, :], w_up[e]).then_inc(w_loaded[s], 16)
                    sync.dma_start(wd[s][:, :, :], w_down[e]).then_inc(w_loaded[s], 16)

                for s in range(2):
                    load(s, s)
                with sync.Fori(0, n_experts // 2 - 1) as i:
                    for s in range(2):
                        sync.wait_ge(w_low, i * 4 + (2 * s + 2))
                        load(i * 2 + (2 + s), s)
                if n_experts % 2:
                    sync.wait_ge(w_low, 2 * (n_experts - 2))
                    load(n_experts - 1, 0)

            @block.gpsimd
            def _(pool):
                def low(i, s):
                    for k, (whole, parts) in enumerate(((wgu, wgu_parts), (wd, wd_parts))):
                        pool.wait_ge(w_high, i * 4 + (2 * s + k + 1))
                        nc.gpsimd.tensor_tensor(parts[s][1][:, :, :], whole[s][:, :, :], parts[s][0][:, :, :], ALU.subtract
                                                ).then_inc(w_low, 1)

                with pool.Fori(0, n_experts // 2) as i:
                    for s in range(2):
                        low(i, s)
                if n_experts % 2:
                    low(n_experts // 2, 0)

            @block.tensor
            def _(pe):
                pe.sem_inc(y_made, 2)

                def up(i, c, first):
                    s, q = c // CHUNKS, c % CHUNKS
                    if first and s == 0:
                        pe.wait_ge(x_low, q + 1)
                    for j in range(FT):
                        n = c * FT + j
                        pe.wait_ge(hidden_made, i * PAIRS + (n + 1))
                        for half in range(2):
                            col = (half * FT + j) * FP
                            for k in range(KT):
                                for a, b in PRODUCTS:
                                    last = nc.tensor.matmul(pair[n % 2][:, half, :], wgu_parts[s][a][:, k, col:col + FP],
                                                            x[b][:, k, q * NB:(q + 1) * NB], start=(k == 0 and (a, b) == (0, 0)),
                                                            stop=(k == KT - 1 and (a, b) == PRODUCTS[-1]))
                        last.then_inc(pair_made, 1)

                def down(i, c):
                    s = c // CHUNKS % 2
                    pe.wait_ge(hidden_low, i * PAIRS + ((c + 1) * FT + 2))
                    pe.wait_ge(combined, i * (2 * CHUNKS) + (c + 1))
                    for t in range(TPC):
                        for j in range(FT):
                            for a, b in PRODUCTS:
                                last = nc.tensor.matmul(y[c % 2][:, t, :], hidden_parts[c % 2][a][:, j, t * P:(t + 1) * P],
                                                        wd_parts[s][b][:, j, :], start=(j == 0 and (a, b) == (0, 0)),
                                                        stop=(j == FT - 1 and (a, b) == PRODUCTS[-1]))
                    last.then_inc(y_made, 1)

                def body(i, parts, first, last):
                    for s in range(parts):
                        pe.wait_ge(w_low, i * 4 + (2 * s + 2))
                        for c in range(s * CHUNKS, (s + 1) * CHUNKS):
                            up(i, c, first)
                            if c or not first:
                                down(i, c - 1)
                    if last:
                        down(i, parts * CHUNKS - 1)

                run(pe, body)

            @block.scalar
            def _(act):
                def high(i, s):
                    act.wait_ge(w_loaded[s], i * 32 + 32)
                    nc.scalar.copy(wgu_parts[s][0][:, :, :], wgu[s][:, :, :]).then_inc(w_high, 1)
                    nc.scalar.copy(wd_parts[s][0][:, :, :], wd[s][:, :, :]).then_inc(w_high, 1)

                def body(i, parts, first, last):
                    for n in range(parts * CHUNKS * FT):
                        c, j = n // FT, n % FT
                        at = i * PAIRS
                        act.wait_ge(pair_made, at + (n + 1))
                        act.wait_ge(hidden_made, at + (n + 1))
                        nc.scalar.activation(gated[:, n % 2, :], pair[n % 2][:, 0, :], ACT.Silu).then_inc(gate_made, 1)
                        act.wait_ge(hidden_made, at + (n + 3))
                        act.wait_ge(y_made, i * (2 * CHUNKS) + (c + 1))
                        nc.scalar.copy(hidden_parts[c % 2][0][:, j, :], hidden[:, n % 2, :]).then_inc(hidden_high, 1)
                        s = c // CHUNKS
                        if c % CHUNKS == 1 and j == FT - 1 and not (last and s == parts - 1):
                            act.wait_ge(y_made, i * (2 * CHUNKS) + (s * CHUNKS + 2))
                            high(i + (s + 1) // 2, (s + 1) % 2)

                high(0, 0)
                for q in range(CHUNKS):
                    cut = slice(q * NB, (q + 1) * NB)
                    nc.scalar.copy(x[0][:, :, cut], XT[:, :, cut]).then_inc(x_high, 1)
                run(act, body)

            @block.vector
            def _(dve):
                dve.sem_inc(hidden_made, 2)
                dve.sem_inc(hidden_low, 2)
                dve.sem_inc(combined, 2)

                def product(i, c):
                    for j in range(FT):
                        n = c * FT + j
                        dve.wait_ge(gate_made, i * PAIRS + (n + 1))
                        dve.wait_ge(hidden_low, i * PAIRS + (n + 1))
                        nc.vector.tensor_tensor(hidden[:, n % 2, :], gated[:, n % 2, :], pair[n % 2][:, 1, :],
                                                ALU.mult).then_inc(hidden_made, 1)
                        dve.wait_ge(hidden_high, i * PAIRS + (n + 1))
                        nc.vector.tensor_tensor(hidden_parts[c % 2][1][:, j, :], hidden[:, n % 2, :], hidden_parts[c % 2][0][:, j, :],
                                                ALU.subtract).then_inc(hidden_low, 1)

                def combine(i, c):
                    s, q = c // CHUNKS, c % CHUNKS
                    dve.wait_ge(y_made, i * (2 * CHUNKS) + (c + 3))
                    for t in range(TPC):
                        tile = q * TPC + t
                        nc.vector.scalar_tensor_tensor(X[:, tile, :], y[c % 2][:, t, :], W[:, tile, bass.ds(i * 2 + s, 1)],
                                                       X[:, tile, :], ALU.mult, ALU.add
                                                       ).then_inc(combined if t == TPC - 1 else acc, 1)

                def body(i, parts, first, last):
                    for c in range(parts * CHUNKS):
                        product(i, c)
                        if c or not first:
                            combine(i, c - 1)
                    if last:
                        combine(i, parts * CHUNKS - 1)

                for q in range(CHUNKS):
                    cut = slice(q * NB, (q + 1) * NB)
                    dve.wait_ge(x_high, q + 1)
                    nc.vector.tensor_tensor(x[1][:, :, cut], XT[:, :, cut], x[0][:, :, cut], ALU.subtract).then_inc(x_low, 1)
                run(dve, body)


def build_program(nc, A, out, stages=(0, 1, 2, 3, 4, 5)):
    Space.used = []
    with ExitStack() as ctx:
        X = ctx.enter_context(nc.sbuf_tensor("X", [P, TILES, D], F32))
        ident = ctx.enter_context(nc.sbuf_tensor("ident", [P, P], F32))
        load_state(nc, A["x"], X, ident)
        for n in stages:
            with ExitStack() as layer:
                XT = layer.enter_context(nc.sbuf_tensor(f"XT{n}", [P, KT, TOKENS], F32))
                if n not in (2, 3):
                    norm_transposed(nc, f"s{n}", X, XT, ident)
                SUBLAYERS[n](nc, A, X, XT, ident)
            Space.clear_used(nc)
        store_state(nc, out, X)


def sub_moe1(nc, A, X, XT, ident):
    with nc.sbuf_tensor("moe1_W", [P, TILES, 17], F32) as W:
        route(nc, "moe1", XT, A["L1_ffn_gate_w"], 16, 4, 0.0, W)
        experts_sum(nc, "moe1", X, XT, W, A["L1_ffn_up"], A["L1_ffn_down"], 17, 128, 1)


SUBLAYERS = {5: sub_moe1}


E0, TOP0, F0, FT0 = 64, 8, 96, 2
HALVES = P // E0
HALF = TOKENS // HALVES
CAP = 192
REST = CAP - P
SLOT_TILES = HALVES * CAP // P
ROW = D + E0


def expert_lists(nc, A, W, ident, table, sums, slots, flag, left):
    J = HALF // P
    with Space(nc, "lists") as sp:
        mask = sp.sb("mask", [P, J, HALVES, E0])
        codes = sp.sb("codes", [P, HALF])
        values = [sp.sb("values", [P, HALF]), left]
        lists = sp.sb("lists", [P, CAP])
        rests = sp.sb("rests", [E0, HALVES, REST])
        base = sp.sb("base", [P, SLOT_TILES + 1])
        slot_f = sp.sb("slot_f", [P, 3, SLOT_TILES, E0])
        zeros = sp.sb("zeros", [P, (TOKENS // P + 1) * D])
        top = sp.sb("top", [P, 1])
        top_row = sp.sb("top_row", [1, P])
        most = sp.sb("most", [1, 1])
        ps_v = sp.ps("ps_v", [P, HALF])
        ps_l = sp.ps("ps_l", [P, HALVES, E0])
        ps_r = sp.ps("ps_r", [P, BANK])
        ps_m = sp.ps("ps_m", [P, BANK])
        loaded, mask_made, turned, step, moved, lists_turned, stored, zeroed, top_made, top_turned = (
            sp.sem(n) for n in ("loaded", "mask_made", "turned", "step", "moved", "lists_turned", "stored", "zeroed",
                                "top_made", "top_turned"))
        with sp.block() as block:

            @block.sync
            def _(sync):
                sync.dma_start(codes[:, :], A["codes"]).then_inc(loaded, 16)
                sync.dma_start(base[:, :], A["slot_base"]).then_inc(loaded, 16)
                sync.dma_start(table[0:TOKENS, D:].rearrange("(t p) e -> p t e", p=P), W[:, :, :]).then_inc(stored, 16)
                sync.wait_ge(zeroed, 1)
                sync.dma_start(table[TOKENS:, :], zeros[:, 0:ROW]).then_inc(stored, 16)
                for s in sums:
                    sync.dma_start(s.rearrange("(p t) d -> p (t d)", p=P), zeros[:, :]).then_inc(stored, 16)
                sync.wait_ge(stored, 16 * (2 + len(sums)))

            @block.gpsimd
            def _(pool):
                nc.gpsimd.memset(zeros[:, :], 0.0).then_inc(zeroed, 1)

            @block.tensor
            def _(pe):
                pe.wait_ge(mask_made, 1)
                for j in range(J):
                    last = nc.tensor.transpose(ps_v[:, j * P:(j + 1) * P], mask[:, j, :, :].rearrange("p h e -> p (h e)"), ident[:, :])
                last.then_inc(turned, 1)
                pe.wait_ge(moved, HALVES)
                nc.tensor.transpose(ps_l[:, :, :].rearrange("p h e -> p (h e)"), lists[:, 0:P], ident[:, :]).then_inc(lists_turned, 1)
                nc.tensor.transpose(ps_r[:, 0:E0], rests[:, :, :].rearrange("e h s -> e (h s)"), ident[0:E0, 0:E0]
                                    ).then_inc(lists_turned, 1)
                pe.wait_ge(top_made, 1)
                nc.tensor.transpose(ps_m[0:1, 0:P], top[:, 0:1], ident[:, :]).then_inc(top_turned, 1)

            @block.vector
            def _(dve):
                link = Chain(dve, step).link
                v = nc.vector
                v.tensor_scalar(mask[:, :, :, :], W[:, :, :].rearrange("p (h j) e -> p j h e", h=HALVES), 0.0, None,
                                ALU.is_gt).then_inc(mask_made, 1)
                dve.wait_ge(loaded, 32)
                dve.wait_ge(turned, 1)
                link(v.tensor_tensor(values[0][:, :], ps_v[:, :], codes[:, :], ALU.mult))
                for r in range(CAP // 8):
                    best = lists[:, 8 * r:8 * r + 8]
                    link(v.max(best, values[r % 2][:, :]))
                    link(v.match_replace(values[(r + 1) % 2][:, :], best, values[r % 2][:, :], 0.0))
                assert CAP // 8 % 2 == 0
                link(v.tensor_copy(left[:, :], values[0][:, :]))
                v.tensor_reduce(top[:, 0:1], left[:, :], AX.X, ALU.max).then_inc(top_made, 1)
                for h in range(HALVES):
                    v.tensor_copy(rests[:, h, :], lists[h * E0:(h + 1) * E0, P:]).then_inc(moved, 1)
                dve.wait_ge(lists_turned, 2)
                tiles = [ps_l[:, 0, :], ps_l[:, 1, :], ps_r[:, 0:E0]]
                for r, code in enumerate(tiles):
                    link(v.tensor_scalar(slot_f[:, 0, r, :], code, -1.0, base[:, r:r + 1], ALU.mult, ALU.add))
                    link(v.tensor_scalar(slot_f[:, 1, r, :], code, 0.0, None, ALU.is_gt))
                link(v.tensor_tensor(slot_f[:, 2, :, :], slot_f[:, 0, :, :], slot_f[:, 1, :, :], ALU.mult))
                link(v.tensor_scalar(slots[:, :, :].rearrange("p e r -> p r e"), slot_f[:, 2, :, :], base[:, SLOT_TILES:], None, ALU.add))
                dve.wait_ge(top_turned, 1)
                link(v.tensor_reduce(most[:, :], ps_m[0:1, 0:P], AX.X, ALU.max))
                link(v.tensor_scalar(flag[:, :], most[:, :], 0.0, None, ALU.is_gt))


def chosen_experts(nc, A, table, sums, slots, ident):
    N = SLOT_TILES * P
    with Space(nc, "chosen") as sp:
        wgu = [sp.sb(f"wgu{s}", [P, KT, 2 * FT0 * F0]) for s in range(2)]
        wd = [sp.sb(f"wd{s}", [F0, FT0, D]) for s in range(2)]
        index = [sp.sb(f"index{s}", [P, SLOT_TILES], mybir.dt.int32) for s in range(4)]
        rows = [sp.sb(f"rows{s}", [P, SLOT_TILES, ROW]) for s in range(4)]
        x_t = [sp.sb(f"x_t{s}", [P, KT, N]) for s in range(2)]
        gated = sp.sb("gated", [F0, FT0, N])
        hidden = [sp.sb(f"hidden{s}", [F0, FT0, N]) for s in range(2)]
        y = [sp.sb(f"y{s}", [P, SLOT_TILES, D]) for s in range(2)]
        ps_x = sp.ps("ps_x", [P, KT, BANK])
        pair = [sp.ps(f"pair{j}", [F0, 2, BANK]) for j in range(FT0)]
        ps_y = sp.ps("ps_y", [P, 4, D])
        w_loaded = [sp.sem(f"w_loaded{s}") for s in range(2)]
        gathered = [sp.sem(f"gathered{s}") for s in range(4)]
        scattered = [sp.sem(f"scattered{s}") for s in range(4)]
        index_made, x_turned, x_copied, y_made, y_scaled, pair_made, gate_made, hidden_made, y_acc = (
            sp.sem(n) for n in ("index_made", "x_turned", "x_copied", "y_made", "y_scaled", "pair_made", "gate_made",
                                "hidden_made", "y_acc"))
        issued = sp.sem("issued")

        def turns(engine, step):
            for s in range(4):
                step(s, 0, s, s == 0, False)
            with engine.Fori(1, E0 // 4 - 1) as i:
                for s in range(4):
                    step(i * 4 + s, i, s, False, False)
            for s in range(4):
                step(E0 - 4 + s, E0 // 4 - 1, s, False, s == 3)

        with sp.block() as block:

            @block.sync
            def _(sync):
                def load(e, s):
                    sync.dma_start(wgu[s][:, :, :], A["L0_ffn_up"][e]).then_inc(w_loaded[s], 16)
                    sync.dma_start(wd[s][:, :, :], A["L0_ffn_down"][e]).then_inc(w_loaded[s], 16)

                for s in range(2):
                    load(s, s)
                with sync.Fori(0, E0 // 2 - 1) as i:
                    for s in range(2):
                        sync.wait_ge(y_made, i * 2 + (s + 1))
                        load(i * 2 + (s + 2), s)

            @block.gpsimd
            def _(pool):
                def gather(e, s):
                    nc.gpsimd.tensor_copy(index[s][:, :], slots[:, bass.ds(e, 1), :].rearrange("p o r -> p (o r)")
                                          ).then_inc(index_made, 1)
                    pool.wait_ge(index_made, e + 1)
                    pool.sem_inc(issued, 1)
                    for r in range(SLOT_TILES):
                        nc.gpsimd.indirect_dma_start(rows[s][:, r, :], None, table[:, :],
                                                     bass.IndirectOffsetOnAxis(ap=index[s][:, r:r + 1], axis=0)
                                                     ).then_inc(gathered[s], 16)

                def step(e, i, s, first, last):
                    p, ip = (s - 1) % 4, i - (1 if s == 0 else 0)
                    if not first:
                        pool.wait_ge(scattered[p], (ip * 16 + 16) * SLOT_TILES)
                        pool.sem_inc(issued, 1)
                    pool.wait_ge(y_scaled, e + 1)
                    pool.sem_inc(issued, 1)
                    for r in range(SLOT_TILES):
                        nc.gpsimd.indirect_dma_start(sums[r], bass.IndirectOffsetOnAxis(ap=index[s][:, r:r + 1], axis=0),
                                                     y[s % 2][:, r, :], None, compute_op=ALU.add).then_inc(scattered[s], 16)
                    if not (isinstance(e, int) and e + 3 >= E0):
                        gather(i * 4 + (s + 3), p)

                for s in range(3):
                    gather(s, s)
                turns(pool, step)
                pool.wait_ge(scattered[3], E0 // 4 * 16 * SLOT_TILES)

            @block.tensor
            def _(pe):
                def turn_x(e, i, s):
                    pe.wait_ge(gathered[s], (i * 16 + 16) * SLOT_TILES)
                    if not (isinstance(e, int) and e == 0):
                        pe.wait_ge(x_copied, e * KT)
                    for c in range(KT):
                        for r in range(SLOT_TILES):
                            last = nc.tensor.transpose(ps_x[:, c, r * P:(r + 1) * P], rows[s][:, r, c * P:(c + 1) * P], ident[:, :])
                        last.then_inc(x_turned, 1)

                def up(e, i, s, j, first):
                    s, turn = s % 2, s // 2
                    if j == 0:
                        pe.wait_ge(w_loaded[s], i * 64 + (turn * 32 + 32))
                    if not first:
                        pe.wait_ge(hidden_made, (e - 1) * FT0 + (j + 1))
                    for c in range(KT):
                        if j == 0:
                            pe.wait_ge(x_copied, e * KT + (c + 1))
                        for side in range(2):
                            col = (side * FT0 + j) * F0
                            last = nc.tensor.matmul(pair[j][:, side, 0:N], wgu[s][:, c, col:col + F0], x_t[s][:, c, :],
                                                    start=(c == 0), stop=(c == KT - 1))
                    last.then_inc(pair_made, 1)

                def down(e, s, very_first):
                    pe.wait_ge(hidden_made, e * FT0 + FT0)
                    if not very_first:
                        pe.wait_ge(y_scaled, e)
                    for r in range(SLOT_TILES):
                        for j in range(FT0):
                            last = nc.tensor.matmul(ps_y[:, r, :], hidden[s][:, j, r * P:(r + 1) * P], wd[s][:, j, :],
                                                    start=(j == 0), stop=(j == FT0 - 1))
                    last.then_inc(y_made, 1)

                turn_x(0, 0, 0)

                def step(e, i, s, first, last):
                    up(e, i, s, 0, first)
                    if not first:
                        down(i * 4 + (s - 1), (s - 1) % 2, isinstance(e, int) and e == 1)
                    up(e, i, s, 1, first)
                    if not last:
                        turn_x(i * 4 + (s + 1), i + (s + 1) // 4, (s + 1) % 4)

                turns(pe, step)
                down(E0 - 1, 1, False)

            @block.scalar
            def _(act):
                def take_x(e, s, early):
                    for c in range(KT):
                        act.wait_ge(x_turned, e * KT + (c + 1))
                        if not early and c == 0:
                            act.wait_ge(pair_made, (e - 1) * FT0)
                        nc.scalar.copy(x_t[s][:, c, :], ps_x[:, c, 0:N]).then_inc(x_copied, 1)

                take_x(0, 0, True)

                def step(e, i, s, first, last):
                    for j in range(FT0):
                        act.wait_ge(pair_made, e * FT0 + (j + 1))
                        if not first:
                            act.wait_ge(hidden_made, (e - 1) * FT0 + (j + 1))
                        nc.scalar.activation(gated[:, j, :], pair[j][:, 0, 0:N], ACT.Silu).then_inc(gate_made, 1)
                    if not last:
                        take_x(i * 4 + (s + 1), (s + 1) % 2, isinstance(e, int) and e == 0)

                turns(act, step)

            @block.vector
            def _(dve):
                def scale(e, i, s):
                    dve.wait_ge(y_made, e + 1)
                    if not (isinstance(e, int) and e < 2):
                        dve.wait_ge(scattered[(s - 2) % 4], (i * 16 + (16 if s >= 2 else 0)) * SLOT_TILES)
                    for r in range(SLOT_TILES):
                        nc.vector.tensor_scalar(y[s % 2][:, r, :], ps_y[:, r, :], rows[s][:, r, bass.ds(e + D, 1)], None,
                                                ALU.mult).then_inc(y_scaled if r == SLOT_TILES - 1 else y_acc, 1)

                def step(e, i, s, first, last):
                    for j in range(FT0):
                        dve.wait_ge(gate_made, e * FT0 + (j + 1))
                        if not (isinstance(e, int) and e < 2):
                            dve.wait_ge(y_made, e - 1)
                        nc.vector.tensor_tensor(hidden[s % 2][:, j, :], gated[:, j, :], pair[j][:, 1, 0:N], ALU.mult
                                                ).then_inc(hidden_made, 1)
                        if j == 0 and not first:
                            scale(i * 4 + (s - 1), i - (1 if s == 0 else 0), (s - 1) % 4)

                turns(dve, step)
                scale(E0 - 1, E0 // 4 - 1, 3)


def add_sums(nc, X, sums):
    spans = [slice(h * TILES // HALVES, (h + 1) * TILES // HALVES) for h in range(HALVES)] + [slice(0, TILES)]
    with Space(nc, "add_sums") as sp:
        part = [sp.sb(f"part{r}", [P, TILES, D]) for r in range(len(sums))]
        loaded = [sp.sem(f"loaded{r}") for r in range(len(sums))]
        added = sp.sem("added")
        with sp.block() as block:

            @block.sync
            def _(sync):
                for r, (s, span) in enumerate(zip(sums, spans)):
                    sync.dma_start(part[r][:, span, :], s[0:TOKENS, :].rearrange("(t p) d -> p t d", p=P)[:, span, :]
                                   ).then_inc(loaded[r], 16)

            @block.vector
            def _(dve):
                link = Chain(dve, added).link
                for r, span in enumerate(spans):
                    dve.wait_ge(loaded[r], 16)
                    link(nc.vector.tensor_tensor(X[:, span, :], X[:, span, :], part[r][:, span, :], ALU.add))


def keep_left(nc, W, left, ident):
    J = HALF // P
    with Space(nc, "keep_left") as sp:
        over = sp.sb("over", [P, HALF])
        ps = sp.ps("ps", [P, J, HALVES, E0])
        marked, turned, done = (sp.sem(n) for n in ("marked", "turned", "done"))
        with sp.block() as block:

            @block.vector
            def _(dve):
                nc.vector.tensor_scalar(over[:, :], left[:, :], 0.0, None, ALU.is_gt).then_inc(marked, 1)
                dve.wait_ge(turned, 1)
                for h in range(HALVES):
                    part = W[:, h * J:(h + 1) * J, :]
                    nc.vector.tensor_tensor(part, part, ps[:, :, h, :], ALU.mult).then_inc(done, 1)

            @block.tensor
            def _(pe):
                pe.wait_ge(marked, 1)
                for j in range(J):
                    last = nc.tensor.transpose(ps[:, j, :, :].rearrange("p h e -> p (h e)"), over[:, j * P:(j + 1) * P], ident[:, :])
                last.then_inc(turned, 1)


def top8_experts(nc, A, X, XT, ident):
    table = nc.dram_tensor("table", (TOKENS + P, ROW), F32, kind="Internal").ap()
    sums = [nc.dram_tensor(f"sums{r}", (TOKENS + P, D), F32, kind="Internal").ap() for r in range(SLOT_TILES)]
    norm_transposed(nc, "s2", X, XT, ident, table)
    with Space(nc, "top8") as sp:
        W = sp.sb("W", [P, TILES, E0])
        left = sp.sb("left", [P, HALF])
        slots = sp.sb("slots", [P, E0, SLOT_TILES], mybir.dt.int32)
        flag = sp.sb("flag", [1, 1], mybir.dt.int32)
        route(nc, "moe0", XT, A["L0_ffn_gate_w"], E0, TOP0, 1e-20, W)
        expert_lists(nc, A, W, ident, table, sums, slots, flag, left)
        chosen_experts(nc, A, table, sums, slots, ident)
        add_sums(nc, X, sums)
        overflow = nc.values_load(flag[0:1, 0:1], min_val=0, max_val=1)
        with nc.If(overflow > 0):
            nc.all_engine_barrier()
            keep_left(nc, W, left, ident)
            experts_sum(nc, "moe0", X, XT, W, A["L0_ffn_up"], A["L0_ffn_down"], E0, F0, FT0)
        nc.end_all_ifs()


SUBLAYERS[2] = top8_experts


def pipelined(engine, n, front, back, unroll=2):
    front(0, 0, 0)

    def turn(i, steps):
        for k in range(unroll):
            if k < steps:
                front(i * unroll + (k + 1), i + (k + 1) // unroll, (k + 1) % unroll)
            back(i * unroll + k, i, k)

    with engine.Fori(0, n // unroll - 1) as i:
        turn(i, unroll)
    turn(n // unroll - 1, unroll - 1)


def nothing(t, i, s):
    pass


def self_attention(nc, A, X, XT, ident):
    HD = D // HEADS
    HPC = P // HD
    with Space(nc, "self") as sp:
        w = sp.sb("w", [P, KT, 3 * D])
        bias = sp.sb("bias", [P, GROUPS, SEQ])
        own = sp.sb("own", [P, HPC])
        xt = [sp.sb(f"xt{s}", [P, KT, P]) for s in range(2)]
        k_t = [sp.sb(f"k_t{s}", [P, KT, P]) for s in range(2)]
        v = [sp.sb(f"v{s}", [P, D]) for s in range(2)]
        q_own = [sp.sb(f"q_own{s}", [P, KT, BPT, HPC * SEQ]) for s in range(2)]
        soft = sp.sb("soft", [P, GROUPS, P])
        shifted = [sp.sb(f"shifted{s}", [P, GROUPS, P]) for s in range(2)]
        probs = [sp.sb(f"probs{s}", [P, GROUPS, P]) for s in range(2)]
        probs_t = sp.sb("probs_t", [P, GROUPS, P])
        row = sp.sb("row", [P, 3, GROUPS * BPT])
        ps_q = sp.ps("ps_q", [P, BANK])
        ps_kv = sp.ps("ps_kv", [P, 2, D])
        ps_s = sp.ps("ps_s", [P, GROUPS, P])
        ps_t = sp.ps("ps_t", [P, GROUPS, P])
        ps_o = sp.ps("ps_o", [P, BPT, 2 * GROUPS, HPG * HD])
        loaded = sp.sem("loaded")
        names = ("xt_copied", "projected", "scored", "turned", "attended", "kv_copied", "exps", "t_copied",
                 "q_masked", "shifts", "normed", "added")
        xt_copied, projected, scored, turned, attended, kv_copied, exps, t_copied, q_masked, shifts, normed, added = (
            sp.sem(n) for n in names)
        step, acc = sp.sem("step"), sp.sem("acc")

        with sp.block() as block:

            @block.sync
            def _(sync):
                sync.dma_start(w[:, :, :], A["L0_attn_w"]).then_inc(loaded, 16)
                sync.dma_start(bias[:, :, :], A["alibi"]).then_inc(loaded, 16)
                sync.dma_start(own[:, :], A["own16"]).then_inc(loaded, 16)

            @block.gpsimd
            def _(pool):
                pool.sem_inc(xt_copied, 2)

                def front(t, i, s):
                    pool.wait_ge(projected, t + 1)
                    nc.gpsimd.tensor_copy(xt[s][:, :, :], XT[:, :, bass.ds(t * P, P)]).then_inc(xt_copied, 1)

                pipelined(pool, TILES, front, nothing)

            @block.tensor
            def _(pe):
                pe.wait_ge(loaded, 48)
                pe.sem_inc(projected, 2)
                pe.sem_inc(attended, 2)
                pe.sem_inc(turned, 2)

                def project(t, s):
                    pe.wait_ge(xt_copied, t + 3)
                    pe.wait_ge(kv_copied, t + 1)
                    pe.wait_ge(q_masked, t * KT + KT)
                    for m in range(2 * KT):
                        col = (D if m < KT else 0) + (m % KT) * P
                        for c in range(KT):
                            out = ps_q[:, m * P:(m + 1) * P] if m < KT else ps_kv[:, 0, (m - KT) * P:(m - KT + 1) * P]
                            nc.tensor.matmul(out, w[:, c, col:col + P], xt[s][:, c, :],
                                             start=(c == 0), stop=(c == KT - 1))
                    for c in range(KT):
                        last = nc.tensor.matmul(ps_kv[:, 1, :], xt[s][:, c, :], w[:, c, 2 * D:3 * D],
                                                start=(c == 0), stop=(c == KT - 1))
                    last.then_inc(projected, 1)

                def score(t, s):
                    pe.wait_ge(q_masked, t * KT + 2 * KT)
                    pe.wait_ge(kv_copied, t + 2)
                    pe.wait_ge(shifts, t + 2)
                    for b in range(BPT):
                        at = slice(b * SEQ, (b + 1) * SEQ)
                        for g in range(GROUPS):
                            last = nc.tensor.matmul(ps_s[:, g, at], q_own[s][:, g * HPG // HPC, b, (g * P) % (HPC * SEQ):(g * P) % (HPC * SEQ) + P],
                                                    k_t[s][:, g * HPG // HPC, at], start=True, stop=True)
                    last.then_inc(scored, 1)

                def attend(t, s):
                    pe.wait_ge(normed, t + 1)
                    pe.wait_ge(t_copied, t + 1)
                    for g in range(GROUPS):
                        last = nc.tensor.transpose(ps_t[:, g, :], probs[s][:, g, :], ident[:, :])
                    last.then_inc(turned, 1)
                    pe.wait_ge(t_copied, t + 2)
                    pe.wait_ge(added, t + 1)
                    for g in range(GROUPS):
                        for b in range(BPT):
                            at = slice(b * SEQ, (b + 1) * SEQ)
                            last = nc.tensor.matmul(ps_o[:, b, g, :], probs_t[at, g, :],
                                                    v[s][at, g * HPG * HD:(g + 1) * HPG * HD], start=True, stop=True)
                    last.then_inc(attended, 1)

                project(0, 0)
                score(0, 0)

                def turn(i, steps):
                    for k in range(2):
                        if k < steps:
                            project(i * 2 + (k + 1), (k + 1) % 2)
                        attend(i * 2 + k, k)
                        if k < steps:
                            score(i * 2 + (k + 1), (k + 1) % 2)

                with pe.Fori(0, TILES // 2 - 1) as i:
                    turn(i, 2)
                turn(TILES // 2 - 1, 1)

            @block.scalar
            def _(act):
                act.sem_inc(kv_copied, 1)
                act.sem_inc(t_copied, 1)

                def take_kv(t, s):
                    act.wait_ge(projected, t + 3)
                    act.wait_ge(attended, t + 1)
                    nc.scalar.copy(v[s][:, :], ps_kv[:, 1, :]).then_inc(acc, 1)
                    nc.scalar.copy(k_t[s][:, :, :], ps_kv[:, 0, :].rearrange("p (c n) -> p c n", c=KT)).then_inc(kv_copied, 1)

                def exp(t, s):
                    act.wait_ge(shifts, t + 3)
                    nc.scalar.activation(shifted[s][:, :, :], shifted[s][:, :, :], ACT.Exp).then_inc(exps, 1)

                def take_turned(t):
                    act.wait_ge(turned, t + 3)
                    act.wait_ge(attended, t + 2)
                    nc.scalar.copy(probs_t[:, :, :], ps_t[:, :, :]).then_inc(t_copied, 1)

                take_kv(0, 0)
                exp(0, 0)

                def turn(i, steps):
                    for k in range(2):
                        if k < steps:
                            take_kv(i * 2 + (k + 1), (k + 1) % 2)
                        take_turned(i * 2 + k)
                        if k < steps:
                            exp(i * 2 + (k + 1), (k + 1) % 2)

                with act.Fori(0, TILES // 2 - 1) as i:
                    turn(i, 2)
                turn(TILES // 2 - 1, 1)

            @block.vector
            def _(dve):
                STEPS = 4
                dve.wait_ge(loaded, 48)
                dve.sem_inc(q_masked, KT)
                dve.sem_inc(shifts, 2)
                dve.sem_inc(added, 1)

                def wide(k):
                    return row[:, k, :].rearrange("p (n o) -> p n o", o=1).to_broadcast([P, GROUPS * BPT, SEQ])

                def by_row(a):
                    return a[:, :, :].rearrange("p g (b k) -> p (g b) k", k=SEQ)

                def mask(t, s):
                    dve.wait_ge(projected, t + 3)
                    for c in range(KT):
                        nc.vector.tensor_tensor(
                            q_own[s][:, c, :, :].rearrange("p b (h q) -> p b h q", q=SEQ),
                            ps_q[:, c * P:(c + 1) * P].rearrange("p (b o q) -> p b o q", o=1, q=SEQ).to_broadcast([P, BPT, HPC, SEQ]),
                            own[:, :].rearrange("p (b h o) -> p b h o", b=1, o=1).to_broadcast([P, BPT, HPC, SEQ]),
                            ALU.mult).then_inc(q_masked, 1)

                def softmax(t, s):
                    chain = Chain(dve, step, t * STEPS)
                    dve.wait_ge(scored, t + 1)
                    chain.link(nc.vector.tensor_tensor(
                        soft[:, :, :].rearrange("p g (b k) -> p g b k", k=SEQ),
                        ps_s[:, :, :].rearrange("p g (b k) -> p g b k", k=SEQ),
                        bias[:, :, :].rearrange("p g (o k) -> p g o k", o=1).to_broadcast([P, GROUPS, BPT, SEQ]), ALU.add))
                    chain.link(nc.vector.tensor_reduce(row[:, 0, :], by_row(soft), AX.X, ALU.max))
                    nc.vector.tensor_tensor(by_row(shifted[s]), by_row(soft), wide(0), ALU.subtract).then_inc(shifts, 1)
                    dve.wait_ge(exps, t + 1)
                    chain.link(nc.vector.tensor_reduce(row[:, 1, :], by_row(shifted[s]), AX.X, ALU.add))
                    chain.link(nc.vector.reciprocal(row[:, 2, :], row[:, 1, :]))
                    dve.wait_ge(turned, t + 1)
                    nc.vector.tensor_tensor(by_row(probs[s]), by_row(shifted[s]), wide(2), ALU.mult).then_inc(normed, 1)

                def add(t):
                    dve.wait_ge(attended, t + 3)
                    for b in range(BPT):
                        rows = slice(b * SEQ, (b + 1) * SEQ)
                        for h in range(HPG):
                            out = X[rows, bass.ds(t, 1), :].rearrange("p o (g h d) -> p (o g) h d", g=GROUPS, h=HPG)[:, :, h, :]
                            last = nc.vector.tensor_tensor(out, ps_o[h * SEQ:(h + 1) * SEQ, b, 0:GROUPS, h * HD:(h + 1) * HD],
                                                           out, ALU.add)
                            last.then_inc(added if (b, h) == (BPT - 1, HPG - 1) else acc, 1)

                mask(0, 0)
                softmax(0, 0)

                def turn(i, steps):
                    for k in range(2):
                        if k < steps:
                            mask(i * 2 + (k + 1), (k + 1) % 2)
                        add(i * 2 + k)
                        if k < steps:
                            softmax(i * 2 + (k + 1), (k + 1) % 2)

                with dve.Fori(0, TILES // 2 - 1) as i:
                    turn(i, 2)
                turn(TILES // 2 - 1, 1)


SUBLAYERS[1] = self_attention


def project_queries(nc, A, XT, Q, stage, weights, bias):
    NB = 512
    with Space(nc, stage) as sp:
        w = sp.sb("w", [P, KT, D])
        b = sp.sb("b", [P, KT])
        ps = [sp.ps(f"ps{s}", [P, KT, NB]) for s in range(2)]
        loaded, made, copied = (sp.sem(n) for n in ("loaded", "made", "copied"))
        with sp.block() as block:

            @block.sync
            def _(sync):
                sync.dma_start(w[:, :, :], weights).then_inc(loaded, 16)
                sync.dma_start(b[:, :], bias).then_inc(loaded, 16)

            @block.tensor
            def _(pe):
                pe.wait_ge(loaded, 32)
                for q in range(TOKENS // NB):
                    if q >= 2:
                        pe.wait_ge(copied, KT * (q - 1))
                    for m in range(KT):
                        for c in range(KT):
                            last = nc.tensor.matmul(ps[q % 2][:, m, :], w[:, c, m * P:(m + 1) * P],
                                                    XT[:, c, q * NB:(q + 1) * NB], start=(c == 0), stop=(c == KT - 1))
                    last.then_inc(made, 1)

            @block.scalar
            def _(act):
                act.wait_ge(loaded, 32)
                for q in range(TOKENS // NB):
                    act.wait_ge(made, q + 1)
                    for m in range(KT):
                        nc.scalar.activation(Q[:, m, q * NB:(q + 1) * NB], ps[q % 2][:, m, :], ACT.Identity,
                                             bias=b[:, m:m + 1]).then_inc(copied, 1)


def project_rows(nc, stage, X, rows, ident, weights, bias_in, bias_out):
    with Space(nc, stage) as sp:
        w = sp.sb("w", [P, KT, D])
        b_in = sp.sb("b_in", [P, KT])
        b_out = sp.sb("b_out", [1, D])
        ones = sp.sb("ones", [1, P])
        rows_t = [sp.sb(f"rows_t{s}", [P, KT, P]) for s in range(2)]
        ps_t = [sp.ps(f"ps_t{s}", [P, BANK]) for s in range(2)]
        ps_y = [sp.ps(f"ps_y{s}", [P, BANK]) for s in range(2)]
        loaded, ones_ready, turned, copied, made, added = (
            sp.sem(n) for n in ("loaded", "ones_ready", "turned", "copied", "made", "added"))
        with sp.block() as block:

            @block.sync
            def _(sync):
                sync.dma_start(w[:, :, :], weights).then_inc(loaded, 16)
                sync.dma_start(b_in[:, :], bias_in).then_inc(loaded, 16)
                sync.dma_start(b_out[:, :], bias_out).then_inc(loaded, 16)

            @block.gpsimd
            def _(pool):
                nc.gpsimd.memset(ones[:, :], 1.0).then_inc(ones_ready, 1)

            @block.tensor
            def _(pe):
                pe.wait_ge(loaded, 48)
                pe.wait_ge(ones_ready, 1)

                def turn(t):
                    if t >= 2:
                        pe.wait_ge(copied, KT * (t - 1))
                    for c in range(KT):
                        last = nc.tensor.transpose(ps_t[t % 2][:, c * P:(c + 1) * P], rows[:, t, c * P:(c + 1) * P], ident[:, :])
                    last.then_inc(turned, 1)

                turn(0)
                for t in range(TILES):
                    if t + 1 < TILES:
                        turn(t + 1)
                    pe.wait_ge(copied, KT * (t + 1))
                    if t >= 2:
                        pe.wait_ge(added, t - 1)
                    nc.tensor.matmul(ps_y[t % 2][:, 0:D], ones[:, :], b_out[:, :], start=True, stop=False)
                    for c in range(KT):
                        last = nc.tensor.matmul(ps_y[t % 2][:, 0:D], rows_t[t % 2][:, c, :], w[:, c, :],
                                                start=False, stop=(c == KT - 1))
                    last.then_inc(made, 1)

            @block.scalar
            def _(act):
                act.wait_ge(loaded, 48)
                for t in range(TILES):
                    act.wait_ge(turned, t + 1)
                    if t >= 2:
                        act.wait_ge(made, t - 1)
                    for c in range(KT):
                        nc.scalar.activation(rows_t[t % 2][:, c, :], ps_t[t % 2][:, c * P:(c + 1) * P], ACT.Identity,
                                             bias=b_in[:, c:c + 1]).then_inc(copied, 1)

            @block.vector
            def _(dve):
                for t in range(TILES):
                    dve.wait_ge(made, t + 1)
                    nc.vector.tensor_tensor(X[:, t, :], X[:, t, :], ps_y[t % 2][:, 0:D], ALU.add).then_inc(added, 1)


def cross_attention_0(nc, A, X, XT, ident):
    HD = D // HEADS
    HPC = P // HD
    W = HPG * HD
    FULL = CTX // P
    COLS = CTX + CTX % 2
    PRODUCTS = ((0, 0), (1, 0), (0, 1))
    with Space(nc, "cross0") as outer:
        Q = outer.sb("Q", [P, KT, TOKENS])
        attended_rows = outer.sb("attended_rows", [P, TILES, D])
        project_queries(nc, A, XT, Q, "cross0_q", A["L0_xattn_Wq"], A["L0_xattn_b_q"])
        with Space(nc, "cross0_in") as sp:
            w = sp.sb("w", [P, KT, 2 * D])
            b_k = sp.sb("b_k", [P, KT])
            own = sp.sb("own", [P, HPC])
            ends = sp.sb("ends", [P, KT, BATCH])
            v_end_rows = sp.sb("v_end_rows", [BATCH, D])
            v_end = sp.sb("v_end", [GROUPS, BATCH, D])
            ctx_t = [sp.sb(f"ctx_t{s}", [P, KT, CTX]) for s in range(2)]
            q_own = [sp.sb(f"q_own{s}", [P, KT, HPC * SEQ]) for s in range(2)]
            w_parts = [sp.sb(f"w_{a}", [P, KT, 2 * D], F32R) for a in range(2)]
            ctx_parts = [[sp.sb(f"ctx{s}_{a}", [P, KT, COLS], F32R) for a in range(2)] for s in range(2)]
            q_parts = [[sp.sb(f"q{s}_{a}", [P, KT, HPC * SEQ], F32R) for a in range(2)] for s in range(2)]
            k_parts = [[sp.sb(f"k{s}_{a}", [P, KT, COLS], F32R) for a in range(2)] for s in range(2)]
            v = [sp.sb(f"v{s}", [P, FULL, D]) for s in range(2)]
            probs = [sp.sb(f"probs{s}", [P, GROUPS, CTX]) for s in range(2)]
            probs_t = sp.sb("probs_t", [P, FULL, GROUPS * P])
            end_t = sp.sb("end_t", [GROUPS, P])
            row = [sp.sb(f"row{s}", [P, 3, GROUPS]) for s in range(2)]
            ps_k = sp.ps("ps_k", [P, KT, BANK])
            ps_v = sp.ps("ps_v", [P, FULL, D])
            ps_s = [sp.ps(f"ps_s{s}", [P, BANK]) for s in range(2)]
            ps_t = [sp.ps(f"ps_t{s}", [P, GROUPS * P]) for s in range(2)]
            ps_o = sp.ps("ps_o", [P, BANK])
            names = ("loaded", "ctx_loaded0", "ctx_loaded1", "zeroed", "end_made", "end_copied", "end_placed", "q_masked",
                     "k_made", "v_made", "k_copied", "v_copied", "scored", "negated", "exps", "turned", "t_copied",
                     "summed", "attended", "extracted", "act_acc", "dve_acc", "w_high", "w_low", "ctx_high", "ctx_low",
                     "q_high", "q_low", "k_low")
            sems = {n: sp.sem(n) for n in names}
            (loaded, ctx_loaded0, ctx_loaded1, zeroed, end_made, end_copied, end_placed, q_masked,
             k_made, v_made, k_copied, v_copied, scored, negated, exps, turned, t_copied,
             summed, attended, extracted, act_acc, dve_acc, w_high, w_low, ctx_high, ctx_low, q_high, q_low, k_low) = (sems[n] for n in names)
            ctx_loaded = (ctx_loaded0, ctx_loaded1)
            with sp.block() as block:

                @block.sync
                def _(sync):
                    sync.dma_start(ends[:, :, :], A["ctx_ends"]).then_inc(loaded, 16)
                    sync.dma_start(w[:, :, :], A["L0_xattn_Wkv"]).then_inc(loaded, 16)
                    sync.dma_start(b_k[:, :], A["L0_xattn_b_k"]).then_inc(loaded, 16)
                    sync.dma_start(own[:, :], A["own4"]).then_inc(loaded, 16)
                    for s in range(2):
                        sync.dma_start(ctx_t[s][:, :, :], A["ctx_t"][s]).then_inc(ctx_loaded[s], 16)
                    sync.wait_ge(end_copied, 1)
                    sync.wait_ge(zeroed, 1)
                    for g in range(GROUPS):
                        sync.dma_start(v_end[g:g + 1, :, g * W:(g + 1) * W],
                                       v_end_rows[:, g * W:(g + 1) * W]).then_inc(end_placed, 16)
                    with sync.Fori(0, BATCH // 2 - 1) as i:
                        for s in range(2):
                            sync.wait_ge(ctx_low, i * 2 + (s + 1))
                            sync.dma_start(ctx_t[s][:, :, :], A["ctx_t"][i * 2 + (s + 2)]).then_inc(ctx_loaded[s], 16)

                @block.gpsimd
                def _(pool):
                    nc.gpsimd.memset(v_end[:, :, :], 0.0).then_inc(zeroed, 1)
                    for s in range(2):
                        for a in range(2):
                            for parts in (ctx_parts, k_parts):
                                nc.gpsimd.memset(parts[s][a][:, :, CTX:].bitcast(F32), 0.0).then_inc(zeroed, 1)
                    pool.wait_ge(loaded, 64)

                    def front(t, i, s):
                        s = s % 2
                        pool.wait_ge(q_low, t + 1)
                        nc.gpsimd.tensor_tensor(
                            q_own[s][:, :, :].rearrange("p c (h q) -> p c h q", q=SEQ),
                            Q[:, :, bass.ds(t * SEQ, SEQ)].rearrange("p c (o q) -> p c o q", o=1).to_broadcast([P, KT, HPC, SEQ]),
                            own[:, :].rearrange("p (c h o) -> p c h o", c=1, o=1).to_broadcast([P, KT, HPC, SEQ]),
                            ALU.mult).then_inc(q_masked, 1)

                    pipelined(pool, BATCH, front, nothing)

                @block.tensor
                def _(pe):
                    pe.wait_ge(loaded, 64)
                    pe.sem_inc(scored, 2 * GROUPS)
                    pe.sem_inc(attended, 2)
                    for c in range(KT):
                        last = nc.tensor.matmul(ps_o[0:BATCH, 0:D], ends[:, c, :], w[:, c, D:2 * D],
                                                start=(c == 0), stop=(c == KT - 1))
                    last.then_inc(end_made, 1)
                    pe.wait_ge(end_copied, 1)
                    pe.wait_ge(end_placed, 64)
                    pe.wait_ge(zeroed, 9)
                    pe.wait_ge(w_low, 1)

                    def front(t, i, s):
                        s = s % 2
                        pe.wait_ge(ctx_low, t + 1)
                        pe.wait_ge(k_low, t + 1)
                        for m in range(KT):
                            for a, b in PRODUCTS:
                                for c in range(KT):
                                    last = nc.tensor.matmul(ps_k[:, m, 0:COLS], w_parts[a][:, c, m * P:(m + 1) * P],
                                                            ctx_parts[s][b][:, c, :], start=(c == 0 and a + b == 0),
                                                            stop=(c == KT - 1 and b == 1))
                        last.then_inc(k_made, 1)
                        pe.wait_ge(v_copied, t + 1)
                        for n in range(FULL):
                            for a, b in PRODUCTS:
                                for c in range(KT):
                                    last = nc.tensor.matmul(ps_v[:, n, :], ctx_parts[s][a][:, c, n * P:(n + 1) * P],
                                                            w_parts[b][:, c, D:2 * D], start=(c == 0 and a + b == 0),
                                                            stop=(c == KT - 1 and b == 1))
                        last.then_inc(v_made, 1)

                    def score(t, s, g):
                        s = s % 2
                        if g == 0:
                            pe.wait_ge(k_copied, t + 2)
                            pe.wait_ge(q_low, t + 3)
                            pe.wait_ge(k_low, t + 2)
                        pe.wait_ge(exps, t * GROUPS + (g + 1))
                        at = (g * P) % (HPC * SEQ)
                        for a, b in PRODUCTS:
                            last = nc.tensor.matmul(ps_s[g % 2][:, 0:COLS], q_parts[s][a][:, g * HPG // HPC, at:at + P],
                                                    k_parts[s][b][:, g * HPG // HPC, :], start=(a + b == 0), stop=(b == 1))
                        last.then_inc(scored, 1)

                    def transposes(t, s):
                        s = s % 2
                        pe.wait_ge(exps, t * GROUPS + (GROUPS + 2))
                        pe.wait_ge(t_copied, t * (FULL + 1) + (FULL + 1))
                        for n in range(FULL):
                            for g in range(GROUPS):
                                last = nc.tensor.transpose(ps_t[n % 2][:, g * P:(g + 1) * P],
                                                           probs[s][:, g, n * P:(n + 1) * P], ident[:, :])
                            last.then_inc(turned, 1)

                    def end_transpose(t, s):
                        s = s % 2
                        pe.wait_ge(t_copied, t * (FULL + 1) + (FULL + 2))
                        nc.tensor.transpose(ps_t[0][0:GROUPS, 0:P], probs[s][:, :, CTX - 1], ident[:, :]).then_inc(turned, 1)

                    def values(t, s):
                        s = s % 2
                        pe.wait_ge(t_copied, t * (FULL + 1) + 2 * (FULL + 1) - 1)
                        pe.wait_ge(extracted, t + 1)
                        for n in range(FULL):
                            for g in range(GROUPS):
                                nc.tensor.matmul(ps_o[:, g * W:(g + 1) * W], probs_t[:, n, g * P:(g + 1) * P],
                                                 v[s][:, n, g * W:(g + 1) * W], start=(n == 0 and g == 0), stop=False,
                                                 skip_group_check=True)
                        pe.wait_ge(t_copied, t * (FULL + 1) + 2 * (FULL + 1))
                        nc.tensor.matmul(ps_o[:, 0:D], end_t[:, :], v_end[:, bass.ds(t, 1), :].rearrange("g o d -> g (o d)"),
                                         start=False, stop=True, skip_group_check=True).then_inc(attended, 1)

                    def scores_of(t, s, groups):
                        for g in groups:
                            score(t, s, g)

                    front(0, 0, 0)
                    scores_of(0, 0, range(GROUPS))

                    def turn(i, steps):
                        for k in range(2):
                            t = i * 2 + k
                            nxt, ni, nk = i * 2 + (k + 1), i + (k + 1) // 2, (k + 1) % 2
                            if k < steps:
                                front(nxt, ni, nk)
                            transposes(t, k)
                            if k < steps:
                                scores_of(nxt, nk, range(2))
                            end_transpose(t, k)
                            values(t, k)
                            if k < steps:
                                scores_of(nxt, nk, range(2, GROUPS))

                    with pe.Fori(0, BATCH // 2 - 1) as i:
                        turn(i, 2)
                    turn(BATCH // 2 - 1, 1)

                @block.scalar
                def _(act):
                    act.wait_ge(loaded, 64)
                    act.sem_inc(k_copied, 1)
                    act.sem_inc(v_copied, 1)
                    act.sem_inc(t_copied, FULL + 1)
                    act.sem_inc(exps, 2)
                    act.wait_ge(end_made, 1)
                    nc.scalar.copy(v_end_rows[:, :], ps_o[0:BATCH, 0:D]).then_inc(end_copied, 1)

                    def split_ctx(t, i, s):
                        act.wait_ge(ctx_loaded[s], i * 16 + 16)
                        if not (isinstance(t, int) and t < 2):
                            act.wait_ge(v_made, t - 1)
                        nc.scalar.copy(ctx_parts[s][0][:, :, 0:CTX], ctx_t[s][:, :, :]).then_inc(ctx_high, 1)

                    def take_kv(t, s):
                        act.wait_ge(scored, t * GROUPS + GROUPS)
                        act.wait_ge(q_masked, t + 1)
                        nc.scalar.copy(q_parts[s][0][:, :, :], q_own[s][:, :, :]).then_inc(q_high, 1)
                        act.wait_ge(k_made, t + 1)
                        for c in range(KT):
                            nc.scalar.activation(k_parts[s][0][:, c, 0:CTX], ps_k[:, c, 0:CTX], ACT.Identity,
                                                 bias=b_k[:, c:c + 1]).then_inc(k_copied if c == KT - 1 else act_acc, 1)
                        act.wait_ge(v_made, t + 1)
                        act.wait_ge(attended, t + 1)
                        nc.scalar.copy(v[s][:, :, :], ps_v[:, :, :]).then_inc(v_copied, 1)

                    def exp(t, s, groups):
                        for g in groups:
                            act.wait_ge(negated, t * GROUPS + (g + 1))
                            nc.scalar.activation(probs[s][:, g, :], ps_s[g % 2][:, 0:CTX], ACT.Exp, bias=row[s][:, 0, g:g + 1],
                                                 accum_out=row[s][:, 1, g:g + 1]).then_inc(exps, 1)

                    def take_turned(t, n):
                        act.wait_ge(turned, t * (FULL + 1) + (n + 1))
                        if n == 0:
                            act.wait_ge(attended, t + 2)
                        if n < FULL:
                            nc.scalar.copy(probs_t[:, n, :], ps_t[n % 2][:, :]).then_inc(t_copied, 1)
                        else:
                            nc.scalar.copy(end_t[:, :], ps_t[0][0:GROUPS, 0:P]).then_inc(t_copied, 1)

                    nc.scalar.copy(w_parts[0][:, :, :], w[:, :, :]).then_inc(w_high, 1)
                    for s in range(2):
                        split_ctx(s, 0, s)
                    take_kv(0, 0)
                    exp(0, 0, range(GROUPS))

                    def turn(i, steps):
                        for k in range(2):
                            t, nxt, nk = i * 2 + k, i * 2 + (k + 1), (k + 1) % 2
                            if k < steps:
                                take_kv(nxt, nk)
                            for n in range(FULL + 1):
                                take_turned(t, n)
                            if k < steps:
                                exp(nxt, nk, range(2))
                                if steps == 2:
                                    split_ctx(i * 2 + (k + 2), i + 1, k)
                                exp(nxt, nk, range(2, GROUPS))

                    with act.Fori(0, BATCH // 2 - 1) as i:
                        turn(i, 2)
                    turn(BATCH // 2 - 1, 1)

                @block.vector
                def _(dve):
                    dve.sem_inc(extracted, 1)
                    dve.sem_inc(q_low, 2)
                    dve.sem_inc(k_low, 1)
                    dve.wait_ge(w_high, 1)
                    nc.vector.tensor_tensor(w_parts[1][:, :, :], w[:, :, :], w_parts[0][:, :, :], ALU.subtract).then_inc(w_low, 1)

                    def split_ctx(t, s):
                        high, low = ctx_parts[s % 2]
                        dve.wait_ge(ctx_high, t + 1)
                        nc.vector.tensor_tensor(low[:, :, 0:CTX], ctx_t[s % 2][:, :, :], high[:, :, 0:CTX], ALU.subtract
                                                ).then_inc(ctx_low, 1)

                    for s in range(2):
                        split_ctx(s, s)

                    def front(t, i, s):
                        r = row[s % 2]
                        high, low = q_parts[s % 2]
                        dve.wait_ge(q_high, t + 1)
                        nc.vector.tensor_tensor(low[:, :, :], q_own[s % 2][:, :, :], high[:, :, :], ALU.subtract).then_inc(q_low, 1)
                        high, low = k_parts[s % 2]
                        dve.wait_ge(k_copied, t + 2)
                        for c in range(KT):
                            nc.vector.scalar_tensor_tensor(low[:, c, 0:CTX], ps_k[:, c, 0:CTX], b_k[:, c:c + 1],
                                                           high[:, c, 0:CTX], ALU.add, ALU.subtract
                                                           ).then_inc(k_low if c == KT - 1 else dve_acc, 1)
                        for g in range(GROUPS):
                            if g == 2 and not (isinstance(t, int) and t in (0, BATCH - 1)):
                                split_ctx(t + 1, s + 1)
                            dve.wait_ge(scored, t * GROUPS + (2 * GROUPS + g + 1))
                            nc.vector.tensor_reduce(r[:, 0, g:g + 1], ps_s[g % 2][:, 0:CTX], AX.X, ALU.max, negate=True
                                                    ).then_inc(negated, 1)

                    def back(t, i, s):
                        r = row[s % 2]
                        dve.wait_ge(exps, t * GROUPS + (GROUPS + 2))
                        nc.vector.reciprocal(r[:, 2, :], r[:, 1, :]).then_inc(summed, 1)
                        dve.wait_ge(summed, t + 1)
                        dve.wait_ge(attended, t + 3)
                        for h in range(HPG):
                            rows = slice(h * SEQ, (h + 1) * SEQ)
                            out = attended_rows[s * SEQ:(s + 1) * SEQ, bass.ds(i, 1), :].rearrange(
                                "p o (g h d) -> p (o g) h d", g=GROUPS, h=HPG)[:, :, h, :]
                            nc.vector.tensor_tensor(
                                out, ps_o[rows, 0:D].rearrange("p (g h d) -> p g h d", g=GROUPS, h=HPG)[:, :, h, :],
                                r[rows, 2, :].rearrange("p (g o) -> p g o", o=1).to_broadcast([SEQ, GROUPS, HD]),
                                ALU.mult).then_inc(extracted if h == HPG - 1 else dve_acc, 1)

                    pipelined(dve, BATCH, front, back, BPT)

        project_rows(nc, "cross0_out", X, attended_rows, ident, A["L0_xattn_Wo"], A["L0_xattn_b_v"], A["L0_xattn_b_o"])


SUBLAYERS[0] = cross_attention_0


def latent_rows(nc, A, X, LT, ident, tail, ahead, ahead_loaded):
    SLOTS = TILES + 1
    with Space(nc, "latents") as sp:
        affine = sp.sb("affine", [P, 4, D])
        rows = sp.sb("rows", [P, SLOTS, D])
        final = sp.sb("final", [P, SLOTS, D])
        stats = [sp.sb(f"stats{k}", [P, n, 6]) for k, n in ((0, TILES), (1, SLOTS))]
        tmp = [sp.sb(f"tmp{k}", [P, 7, n]) for k, n in ((0, TILES), (1, SLOTS))]
        mean = [sp.sb(f"mean{k}", [P, n]) for k, n in ((0, TILES), (1, SLOTS))]
        rstd = [sp.sb(f"rstd{k}", [P, n]) for k, n in ((0, TILES), (1, SLOTS))]
        turned = [sp.ps(f"turned{k}", [P, BANK]) for k in range(2)]
        step, loaded, zeroed, stats_ready, var_ready, root_ready, rows_normed, final_ready, turned_made, copied, stored, centred, gained = (
            sp.sem(n) for n in ("step", "loaded", "zeroed", "stats_ready", "var_ready", "root_ready", "rows_normed",
                                "final_ready", "turned_made", "copied", "stored", "centred", "gained"))
        with sp.block() as block:

            @block.sync
            def _(sync):
                sync.dma_start(affine[:, :, :], A["affine"]).then_inc(loaded, 16)
                sync.wait_ge(zeroed, 1)
                sync.dma_start(rows[0:BATCH, TILES, :], A["ctx"][:, CTX - 1, :]).then_inc(loaded, 16)
                for t in range(TILES):
                    sync.wait_ge(final_ready, t + 1)
                    sync.dma_start(tail[t * BPT:(t + 1) * BPT, 0:SEQ, :], final[:, t, :]).then_inc(stored, 16)
                sync.wait_ge(final_ready, SLOTS)
                sync.dma_start(tail[:, SEQ, :], final[0:BATCH, TILES, :]).then_inc(stored, 16)
                sync.wait_ge(stored, 16 * SLOTS)

            @block.gpsimd
            def _(pool):
                nc.gpsimd.memset(rows[:, TILES, :], 0.0).then_inc(zeroed, 1)

            @block.scalar
            def _(act):
                for to, source in ahead:
                    act.dma_start(to, source).then_inc(ahead_loaded, 16)
                for k in range(2):
                    act.wait_ge(var_ready, k + 1)
                    nc.scalar.activation(tmp[k][:, 6, :], tmp[k][:, 5, :], ACT.Sqrt).then_inc(root_ready, 1)
                for t in range(0, TILES, 2):
                    act.wait_ge(turned_made, t // 2 + 1)
                    nc.scalar.copy(LT[:, :, t * P:(t + 2) * P],
                                   turned[t // 2 % 2][:, :].rearrange("p (c n) -> p c n", c=KT)).then_inc(copied, 1)

            @block.vector
            def _(dve):
                chain = Chain(dve, step)
                v = nc.vector
                for t in range(TILES):
                    v.bn_stats(stats[0][:, t, :], X[:, t, :]).then_inc(stats_ready, 1)
                dve.wait_ge(stats_ready, TILES)
                norm_moments(dve, stats[0], tmp[0], mean[0][:, :], chain, var_ready)
                dve.wait_ge(root_ready, 1)
                chain.link(v.reciprocal(rstd[0][:, :], tmp[0][:, 6, :]))
                for t in range(TILES):
                    v.tensor_scalar(rows[:, t, :], X[:, t, :], mean[0][:, t:t + 1], rstd[0][:, t:t + 1],
                                    ALU.subtract, ALU.mult).then_inc(rows_normed, 1)
                dve.wait_ge(rows_normed, TILES)
                dve.wait_ge(loaded, 32)
                for t in range(SLOTS):
                    v.bn_stats(stats[1][:, t, :], rows[:, t, :]).then_inc(stats_ready, 1)
                dve.wait_ge(stats_ready, TILES + SLOTS)
                norm_moments(dve, stats[1], tmp[1], mean[1][:, :], chain, var_ready)
                dve.wait_ge(root_ready, 2)
                chain.link(v.reciprocal(rstd[1][:, :], tmp[1][:, 6, :]))
                for t in range(SLOTS + 2):
                    if t < SLOTS:
                        v.tensor_scalar(rows[:, t, :], rows[:, t, :], mean[1][:, t:t + 1], rstd[1][:, t:t + 1],
                                        ALU.subtract, ALU.mult).then_inc(centred, 1)
                    if 1 <= t <= SLOTS:
                        gain = 0 if t - 1 < TILES else 2
                        dve.wait_ge(centred, t)
                        v.tensor_tensor(rows[:, t - 1, :], rows[:, t - 1, :], affine[:, gain, :], ALU.mult).then_inc(gained, 1)
                    if t >= 2:
                        gain = 0 if t - 2 < TILES else 2
                        dve.wait_ge(gained, t - 1)
                        v.tensor_tensor(final[:, t - 2, :], rows[:, t - 2, :], affine[:, gain + 1, :], ALU.add
                                        ).then_inc(final_ready, 1)

            @block.tensor
            def _(pe):
                for t in range(0, TILES, 2):
                    pe.wait_ge(final_ready, t + 2)
                    if t >= 4:
                        pe.wait_ge(copied, t // 2 - 1)
                    for n in range(2):
                        for c in range(KT):
                            last = nc.tensor.transpose(turned[t // 2 % 2][:, (2 * c + n) * P:(2 * c + n + 1) * P],
                                                       final[:, t + n, c * P:(c + 1) * P], ident[:, :])
                    last.then_inc(turned_made, 1)


def cross_attention_1(nc, A, X, LT, ident):
    HD = 64
    INNER = HEADS * HD
    CH = INNER // P
    TAIL = SEQ + 1
    FULL = CTX // P
    KEYS = FULL * P + TAIL
    NT = FULL + 1
    COLS = KEYS + KEYS % 2
    tail = nc.dram_tensor("tail_rows", (BATCH, TAIL, D), F32, kind="Internal").ap()
    with Space(nc, "cross1") as sp:
        wq = sp.sb("wq", [P, KT, INNER])
        wk_t = sp.sb("wk_t", [P, CH, D])
        wv = sp.sb("wv", [P, KT, INNER])
        wo = sp.sb("wo", [P, CH, D])
        affine = sp.sb("affine", [P, 2, KT * D])
        loaded = sp.sem("loaded")
        latent_rows(nc, A, X, LT, ident, tail,
                    [(wq[:, :, :], A["L1_xattn_Wq"]), (wk_t[:, :, :], A["L1_xattn_WkT"]), (wv[:, :, :], A["L1_xattn_Wv"]),
                     (wo[:, :, :], A["L1_xattn_Wo"]), (affine[:, :, :].rearrange("p a (n d) -> p a n d", n=KT), A["ctx_affine"])],
                    loaded)
        minus_half = sp.sb("minus_half", [P, FULL])
        raw = [sp.sb(f"raw{s}", [P, NT, D]) for s in range(4)]
        kv = [sp.sb(f"kv{s}", [P, FULL, D]) for s in range(2)]
        kv_parts = [[sp.sb(f"kv{s}_{a}", [P, NT, D], F32R) for a in range(2)] for s in range(2)]
        kv_t = [[sp.sb(f"kv_t{s}_{a}", [P, KT, COLS], F32R) for a in range(2)] for s in range(2)]
        stats = sp.sb("stats", [P, FULL, 6])
        tmp = [sp.sb(f"tmp{s}", [P, 7, FULL]) for s in range(2)]
        mean = [sp.sb(f"mean{s}", [P, FULL]) for s in range(2)]
        q_t = sp.sb("q_t", [P, CH, P])
        q_keys = [sp.sb(f"q_keys{a}", [P, KT, BPT, HEADS * SEQ], F32R) for a in range(2)]
        probs = [sp.sb(f"probs{s}", [P, GROUPS, NT * P]) for s in range(2)]
        probs_t = [sp.sb(f"probs_t{a}", [P, NT, GROUPS * P], F32R) for a in range(2)]
        row = [sp.sb(f"row{s}", [P, 3, GROUPS]) for s in range(2)]
        z_t = sp.sb("z_t", [P, KT, HEADS, BPT, SEQ])
        out_t = sp.sb("out_t", [P, CH, P])
        ps_x = sp.ps("ps_x", [P, 2, BANK])
        ps_s = [sp.ps(f"ps_s{s}", [P, BANK]) for s in range(2)]
        ps_t = [sp.ps(f"ps_t{s}", [P, GROUPS * P]) for s in range(2)]
        ps_z = sp.ps("ps_z", [P, 2, BANK])
        names = ("half_ready", "var_ready", "roots", "normed", "gained", "scaled", "kv_turned", "kv_copied",
                 "scored", "negated", "exps", "summed", "p_scaled", "p_ready", "turned", "t_copied", "z_made", "half_made", "z_copied", "z_copied_1",
                 "q_made", "q_copied", "qk_made", "qk_act", "qk_dve", "o_made", "o_copied", "y_made", "y_added", "step",
                 "stats_ready", "norm_acc", "zeroed", "kv_low", "rows_high", "rows_low", "t_low")
        S = {n: sp.sem(n) for n in names}
        raw_loaded = [sp.sem(f"raw_loaded{s}") for s in range(4)]
        tail_loaded = [sp.sem(f"tail_loaded{s}") for s in range(4)]

        def schedule(engine, prologue, norm, front_back, tile_front, tile_back, norm_inside=False):
            def call(f, *a):
                if f:
                    f(*a)

            call(norm, 0, 0, 0)
            call(norm, 1, 0, 1)
            call(tile_front, 0)
            call(prologue)

            def turn(i, last):
                for k in range(BPT):
                    more = not (last and k >= BPT - 2)
                    if more and not norm_inside:
                        call(norm, i * BPT + (k + 2), i + (k + 2) // BPT, (k + 2) % BPT)
                    call(front_back, i * BPT + k, i, k, not (last and k == BPT - 1), more, not (last and k >= BPT - 3))
                    if k == BPT - 2 and not last:
                        call(tile_front, i + 1)
                call(tile_back, i)

            with engine.Fori(0, TILES - 1) as i:
                turn(i, False)
            turn(TILES - 1, True)

        def qk_views(ps, r):
            for odd in range(2):
                for c in range(KT):
                    src = ps[:, odd, 2 * c * P:(2 * c + 2) * P].rearrange("p (j b q) -> p j b q", j=2, q=SEQ)
                    yield (src, *(part[:, c, :, :].rearrange("p b (r j o q) -> p r o j b q", r=4, j=2, o=2)[:, r, odd, :, :, :]
                                  for part in q_keys))

        QK = 2 * KT

        with sp.block() as block:

            @block.sync
            def _(sync):
                def load(t, s):
                    sync.dma_start(raw[s][:, 0:FULL, :], A["ctx"][t, 0:FULL * P, :].rearrange("(n p) d -> p n d", p=P)
                                   ).then_inc(raw_loaded[s], 16)
                    sync.dma_start(raw[s][0:TAIL, FULL, :], tail[t]).then_inc(tail_loaded[s], 16)

                for s in range(4):
                    load(s, s)
                with sync.Fori(0, BATCH // 4 - 1) as i:
                    for s in range(4):
                        sync.wait_ge(S["z_made"], i * 4 + (s + 1 + 4))
                        load(i * 4 + (s + 4), s)

            @block.gpsimd
            def _(pool):
                for s in range(2):
                    nc.gpsimd.memset(probs[s][:, :, KEYS:], 0.0).then_inc(S["zeroed"], 1)
                    for a in range(2):
                        nc.gpsimd.memset(kv_t[s][a][:, :, KEYS:].bitcast(F32), 0.0).then_inc(S["zeroed"], 1)
                nc.gpsimd.memset(minus_half[:, :], -0.5).then_inc(S["half_ready"], 1)
                pool.wait_ge(S["half_ready"], 1)
                pool.wait_ge(loaded, 16 * 5)

                def root(t, s):
                    pool.wait_ge(S["var_ready"], t + 1)
                    nc.gpsimd.tensor_tensor(tmp[s % 2][:, 6, :], tmp[s % 2][:, 5, :], minus_half[:, :], ALU.pow).then_inc(S["roots"], 1)

                def norm(t, i, s):
                    root(t, s)
                    affine_rows(t, s)

                def affine_rows(t, s):
                    pool.wait_ge(S["normed"], t + 1)
                    rows = kv[s % 2][:, :, :].rearrange("p n d -> p (n d)")
                    nc.gpsimd.tensor_tensor(rows, rows, affine[:, 0, :], ALU.mult).then_inc(S["gained"], 1)
                    pool.wait_ge(S["gained"], t + 1)
                    nc.gpsimd.tensor_tensor(rows, rows, affine[:, 1, :], ALU.add).then_inc(S["scaled"], 1)

                def low(t, s2, s4):
                    whole, (high, rest) = kv[s2], kv_parts[s2]
                    pool.wait_ge(S["rows_high"], t * 2 + 2)
                    nc.gpsimd.tensor_tensor(rest[:, 0:FULL, :], whole[:, :, :], high[:, 0:FULL, :], ALU.subtract
                                            ).then_inc(S["rows_low"], 1)
                    nc.gpsimd.tensor_tensor(rest[0:TAIL, FULL, :], raw[s4][0:TAIL, FULL, :], high[0:TAIL, FULL, :], ALU.subtract
                                            ).then_inc(S["rows_low"], 1)

                def prologue():
                    root(2, 2)
                    low(0, 0, 0)

                def front_back(t, i, k, ahead, more, most):
                    if ahead:
                        low(i * BPT + (k + 1), (k + 1) % 2, (k + 1) % 4)
                    if more:
                        affine_rows(i * BPT + (k + 2), (k + 2) % BPT)
                    if most:
                        root(i * BPT + (k + 3), (k + 3) % BPT)

                schedule(pool, prologue, norm, front_back, None, None, norm_inside=True)

            @block.tensor
            def _(pe):
                pe.wait_ge(loaded, 16 * 5)
                pe.wait_ge(S["zeroed"], 6)
                pe.sem_inc(S["scored"], 2 * GROUPS)
                pe.sem_inc(S["z_made"], 4)

                def turn_kv(t, i, s4):
                    pe.wait_ge(S["scaled"], t + 1)
                    pe.wait_ge(tail_loaded[s4], i * 16 + 16)
                    pe.wait_ge(S["kv_low"], t + 1)
                    pe.wait_ge(S["qk_dve"], i * (4 * QK) + 4 * QK)
                    if s4 != 0:
                        pe.wait_ge(S["o_copied"], i * 2 + 2)
                    for c in range(KT):
                        for n in range(NT):
                            k = P if n < FULL else TAIL
                            rows = kv[s4 % 2] if n < FULL else raw[s4]
                            last = nc.tensor.transpose(ps_x[:, c, n * P:n * P + k], rows[0:k, n, c * P:(c + 1) * P],
                                                       ident[0:k, 0:k])
                    last.then_inc(S["kv_turned"], 1)

                def score(t, s2, s4, groups):
                    for g in groups:
                        if g == 0:
                            pe.wait_ge(S["kv_copied"], t + 2)
                        pe.wait_ge(S["exps"], t * GROUPS + (g + 1))
                        for a, b in ((0, 0), (1, 0), (0, 1)):
                            if g == 0 and b == 1:
                                pe.wait_ge(S["kv_low"], t + 2)
                            for c in range(KT):
                                last = nc.tensor.matmul(ps_s[g % 2][:, 0:COLS], q_keys[a][:, c, s4, g * P:(g + 1) * P],
                                                        kv_t[s2][b][:, c, :], start=(c == 0 and a + b == 0),
                                                        stop=(c == KT - 1 and b == 1))
                        last.then_inc(S["scored"], 1)

                def turn_probs(t, s2, tiles):
                    for n in tiles:
                        if n == 0:
                            pe.wait_ge(S["p_ready"], t + 1)
                            pe.wait_ge(S["t_low"], t * NT + NT)
                        if n == 2:
                            pe.wait_ge(S["t_low"], t * NT + (NT + 1))
                        for g in range(GROUPS):
                            last = nc.tensor.transpose(ps_t[n % 2][:, g * P:(g + 1) * P],
                                                       probs[s2][:, g, n * P:(n + 1) * P], ident[:, :])
                        last.then_inc(S["turned"], 1)

                def attend(t, i, s4, c, tiles):
                    if 0 in tiles:
                        pe.wait_ge(S["z_copied_1" if c else "z_copied"], t + 1)
                    if c == 0 and 0 in tiles:
                        pe.wait_ge(S["y_added"], i + 1)
                        pe.wait_ge(S["rows_low"], t * 2 + 2)
                    for n in tiles:
                        k = P if n < FULL else TAIL
                        if c == 0:
                            pe.wait_ge(S["t_copied"], t * NT + (NT + n + 1))
                        for a, b in ((0, 0), (1, 0), (0, 1)):
                            if c == 0 and b == 1:
                                pe.wait_ge(S["t_low"], t * NT + (NT + n + 1))
                            last = nc.tensor.matmul(ps_z[:, c, :], kv_parts[s4 % 2][a][0:k, n, c * P:(c + 1) * P],
                                                    probs_t[b][0:k, n, :], start=(n == 0 and a + b == 0),
                                                    stop=(n == NT - 1 and b == 1))
                    if NT - 1 in tiles:
                        last.then_inc(S["z_made" if c == KT - 1 else "half_made"], 1)

                def prologue():
                    turn_kv(0, 0, 0)
                    score(0, 0, 0, range(GROUPS))

                def front_back(t, i, k, ahead, more, most):
                    s2, n2, n4, ni = k % 2, (k + 1) % 2, (k + 1) % 4, i + (k + 1) // 4
                    nt = t + 1 if isinstance(t, int) else i * BPT + (k + 1)
                    if ahead:
                        turn_kv(nt, ni, n4)
                    turn_probs(t, s2, range(FULL))
                    if ahead:
                        score(nt, n2, n4, (0, 1))
                    turn_probs(t, s2, (FULL,))
                    attend(t, i, k, 0, (0,))
                    if ahead:
                        score(nt, n2, n4, (2, 3))
                    attend(t, i, k, 0, range(1, NT))
                    attend(t, i, k, 1, range(NT))

                def tile_front(i):
                    first = isinstance(i, int) and i == 0
                    if not first:
                        pe.wait_ge(S["kv_low"], i * BPT + 1)
                    for m in range(CH):
                        for c in range(KT):
                            last = nc.tensor.matmul(ps_x[:, m // 4, (m % 4) * P:(m % 4 + 1) * P], wq[:, c, m * P:(m + 1) * P],
                                                    LT[:, c, bass.ds(i * P, P)], start=(c == 0), stop=(c == KT - 1))
                        if m % 4 == 3:
                            last.then_inc(S["q_made"], 1)
                    for r in range(4):
                        ps = ps_x if r % 2 else ps_z
                        pe.wait_ge(S["q_copied"], i * 2 + (1 if r == 0 else 2))
                        if r == 0 and not first:
                            pe.wait_ge(S["z_copied_1"], i * BPT)
                            pe.wait_ge(S["z_copied"], i * BPT)
                        if r >= 2:
                            pe.wait_ge(S["qk_dve"], i * (4 * QK) + QK * (r - 1))
                        for j in range(2):
                            for c in range(KT):
                                for odd in range(2):
                                    half = slice(64 * odd, 64 * odd + 64)
                                    last = nc.tensor.matmul(ps[:, odd, (2 * c + j) * P:(2 * c + j + 1) * P],
                                                            wk_t[half, 2 * r + j, c * P:(c + 1) * P], q_t[half, 2 * r + j, :],
                                                            start=True, stop=True)
                        last.then_inc(S["qk_made"], 1)

                def tile_back(i):
                    pe.wait_ge(S["z_copied"], i * BPT + (BPT + 1))
                    pe.wait_ge(S["z_copied_1"], i * BPT + (BPT + 1))
                    if not (isinstance(i, int) and i == TILES - 1):
                        pe.wait_ge(S["kv_low"], i * BPT + (BPT + 2))
                    for h in range(HEADS):
                        half = slice(64 * (h % 2), 64 * (h % 2) + 64)
                        for c in range(KT):
                            last = nc.tensor.matmul(ps_x[half, h // 8, (h // 2 % 4) * P:(h // 2 % 4 + 1) * P],
                                                    wv[:, c, h * HD:(h + 1) * HD],
                                                    z_t[:, c, h, :, :].rearrange("p b q -> p (b q)"),
                                                    start=(c == 0), stop=(c == KT - 1))
                        if h % 8 == 7:
                            last.then_inc(S["o_made"], 1)
                    for m in range(CH):
                        if m % 4 == 0:
                            pe.wait_ge(S["o_copied"], i * 2 + (m // 4 + 3))
                        last = nc.tensor.matmul(ps_z[:, 0, 0:D], out_t[:, m, :], wo[:, m, :], start=(m == 0), stop=(m == CH - 1))
                    last.then_inc(S["y_made"], 1)

                schedule(pe, prologue, None, front_back, tile_front, tile_back)

            @block.scalar
            def _(act):
                act.sem_inc(S["kv_copied"], 1)
                act.sem_inc(S["t_copied"], NT)
                act.sem_inc(S["exps"], 2)
                act.sem_inc(S["o_copied"], 2)
                act.sem_inc(S["z_copied_1"], 1)

                def take_kv(t, s2):
                    act.wait_ge(S["kv_turned"], t + 1)
                    act.wait_ge(S["scored"], t * GROUPS + GROUPS)
                    nc.scalar.copy(kv_t[s2][0][:, :, 0:KEYS], ps_x[:, :, 0:KEYS]).then_inc(S["kv_copied"], 1)

                def rows_high(t, ti, s2, s4):
                    act.wait_ge(S["scaled"], t + 1)
                    act.wait_ge(tail_loaded[s4], ti * 16 + 16)
                    act.wait_ge(S["z_made"], t + 3)
                    nc.scalar.copy(kv_parts[s2][0][:, 0:FULL, :], kv[s2][:, :, :]).then_inc(S["rows_high"], 1)
                    nc.scalar.copy(kv_parts[s2][0][0:TAIL, FULL, :], raw[s4][0:TAIL, FULL, :]).then_inc(S["rows_high"], 1)

                def scale(t, s2, half):
                    act.wait_ge(S["summed"], t * 2 + (half + 1))
                    for g in (2 * half, 2 * half + 1):
                        nc.scalar.activation(probs[s2][:, g, 0:KEYS], probs[s2][:, g, 0:KEYS], ACT.Copy,
                                             scale=row[s2][:, 2, g:g + 1]).then_inc(S["p_ready" if g == GROUPS - 1 else "p_scaled"], 1)

                def exp(t, s2, groups):
                    for g in groups:
                        act.wait_ge(S["negated"], t * GROUPS + (g + 1))
                        nc.scalar.activation(probs[s2][:, g, 0:KEYS], ps_s[g % 2][:, 0:KEYS], ACT.Exp, bias=row[s2][:, 0, g:g + 1],
                                             accum_out=row[s2][:, 1, g:g + 1]).then_inc(S["exps"], 1)

                def take_turned(t, n):
                    act.wait_ge(S["turned"], t * NT + (n + 1))
                    if n == 0:
                        act.wait_ge(S["z_made"], t + 4)
                    k = P if n < FULL else TAIL
                    nc.scalar.copy(probs_t[0][0:k, n, :], ps_t[n % 2][0:k, :]).then_inc(S["t_copied"], 1)

                def prologue():
                    take_kv(0, 0)
                    rows_high(0, 0, 0, 0)
                    exp(0, 0, range(GROUPS))
                    scale(0, 0, 0)
                    scale(0, 0, 1)

                def front_back(t, i, k, ahead, more, most):
                    s2, n2 = k % 2, (k + 1) % 2
                    nt = i * BPT + (k + 1)
                    if ahead:
                        take_kv(nt, n2)
                    take_turned(t, 0)
                    take_turned(t, 1)
                    if ahead:
                        rows_high(nt, i + (k + 1) // BPT, n2, (k + 1) % 4)
                        exp(nt, n2, (0,))
                    take_turned(t, 2)
                    if ahead:
                        exp(nt, n2, (1, 2))
                        scale(nt, n2, 0)
                        exp(nt, n2, (3,))
                        scale(nt, n2, 1)
                    act.wait_ge(S["z_made"], t + 5)
                    nc.scalar.copy(z_t[:, 1, :, k, :], ps_z[:, 1, :].rearrange("p (h q) -> p h q", q=SEQ)
                                   ).then_inc(S["z_copied_1"], 1)

                def tile_front(i):
                    for a in range(2):
                        act.wait_ge(S["q_made"], i * 2 + (a + 1))
                        nc.scalar.activation(q_t[:, 4 * a:4 * a + 4, :].rearrange("p m n -> p (m n)"), ps_x[:, a, :], ACT.Copy,
                                             scale=HD ** -0.5).then_inc(S["q_copied"], 1)
                    for r in range(4):
                        ps = ps_x if r % 2 else ps_z
                        act.wait_ge(S["qk_made"], i * 4 + (r + 1))
                        for src, high, low in qk_views(ps, r):
                            nc.scalar.copy(high, src).then_inc(S["qk_act"], 1)

                def tile_back(i):
                    for a in range(2):
                        act.wait_ge(S["o_made"], i * 2 + (a + 1))
                        nc.scalar.copy(out_t[:, 4 * a:4 * a + 4, :].rearrange("p m n -> p (m n)"), ps_x[:, a, :]
                                       ).then_inc(S["o_copied"], 1)

                schedule(act, prologue, None, front_back, tile_front, tile_back)

            @block.vector
            def _(dve):
                dve.wait_ge(loaded, 16 * 5)
                dve.sem_inc(S["z_copied"], 1)
                dve.sem_inc(S["y_added"], 1)
                dve.sem_inc(S["kv_low"], 1)
                dve.sem_inc(S["t_low"], NT)
                v = nc.vector

                def measure(t, i, s):
                    dve.wait_ge(raw_loaded[s], i * 16 + 16)
                    for n in range(FULL):
                        last = v.bn_stats(stats[:, n, :], raw[s][:, n, :]).then_inc(S["stats_ready"], 1)
                    dve.wait_ge(S["stats_ready"], t * FULL + FULL)
                    norm_moments(dve, stats, tmp[s % 2], mean[s % 2][:, :], Chain(dve, S["step"], t * MOMENT_LINKS), S["var_ready"])

                def apply(t, i, s):
                    dve.wait_ge(S["roots"], t + 1)
                    if not (isinstance(t, int) and t < 2):
                        dve.wait_ge(S["kv_turned"], t - 1)
                        dve.wait_ge(S["rows_low"], t * 2 - 2)
                    for n in range(FULL):
                        v.tensor_scalar(kv[s % 2][:, n, :], raw[s][:, n, :], mean[s % 2][:, n:n + 1], tmp[s % 2][:, 6, n:n + 1],
                                        ALU.subtract, ALU.mult).then_inc(S["normed"] if n == FULL - 1 else S["norm_acc"], 1)

                def norm(t, i, s):
                    measure(t, i, s)
                    apply(t, i, s)

                def take_kv(t, s2):
                    dve.wait_ge(S["kv_copied"], t + 2)
                    v.tensor_tensor(kv_t[s2][1][:, :, 0:KEYS], ps_x[:, :, 0:KEYS], kv_t[s2][0][:, :, 0:KEYS], ALU.subtract
                                    ).then_inc(S["kv_low"], 1)

                def take_turned(t, n):
                    dve.wait_ge(S["t_copied"], t * NT + (NT + n + 1))
                    k = P if n < FULL else TAIL
                    v.tensor_tensor(probs_t[1][0:k, n, :], ps_t[n % 2][0:k, :], probs_t[0][0:k, n, :], ALU.subtract
                                    ).then_inc(S["t_low"], 1)

                def maxima(t, s2, groups):
                    for g in groups:
                        dve.wait_ge(S["scored"], t * GROUPS + (2 * GROUPS + g + 1))
                        v.tensor_reduce(row[s2][:, 0, g:g + 1], ps_s[g % 2][:, 0:KEYS], AX.X, ALU.max, negate=True
                                        ).then_inc(S["negated"], 1)

                def invert(t, s2, half):
                    dve.wait_ge(S["exps"], t * GROUPS + (2 * half + 4))
                    v.reciprocal(row[s2][:, 2, 2 * half:2 * half + 2], row[s2][:, 1, 2 * half:2 * half + 2]).then_inc(S["summed"], 1)

                def prologue():
                    measure(2, 0, 2)
                    take_kv(0, 0)
                    maxima(0, 0, range(GROUPS))
                    invert(0, 0, 0)
                    invert(0, 0, 1)

                def front_back(t, i, k, ahead, more, most):
                    nt, n2 = i * BPT + (k + 1), (k + 1) % 2
                    if ahead:
                        take_kv(nt, n2)
                    take_turned(t, 0)
                    take_turned(t, 1)
                    if ahead:
                        maxima(nt, n2, (0,))
                    if more:
                        apply(i * BPT + (k + 2), i + (k + 2) // BPT, (k + 2) % BPT)
                    if ahead:
                        maxima(nt, n2, (1,))
                    take_turned(t, 2)
                    if ahead:
                        maxima(nt, n2, (2,))
                        invert(nt, n2, 0)
                        maxima(nt, n2, (3,))
                        invert(nt, n2, 1)
                    dve.wait_ge(S["half_made"], t + 1)
                    v.tensor_copy(z_t[:, 0, :, k, :], ps_z[:, 0, :].rearrange("p (h q) -> p h q", q=SEQ)
                                  ).then_inc(S["z_copied"], 1)
                    if most:
                        measure(i * BPT + (k + 3), i + (k + 3) // BPT, (k + 3) % BPT)

                def tile_front(i):
                    for r in range(4):
                        ps = ps_x if r % 2 else ps_z
                        for n, (src, high, low) in enumerate(qk_views(ps, r)):
                            if n % KT == 0:
                                dve.wait_ge(S["qk_act"], i * (4 * QK) + (r * QK + n + KT))
                            v.tensor_tensor(low, src, high, ALU.subtract).then_inc(S["qk_dve"], 1)

                def tile_back(i):
                    dve.wait_ge(S["y_made"], i + 1)
                    v.tensor_tensor(X[:, bass.ds(i, 1), :].rearrange("p o d -> p (o d)"),
                                    X[:, bass.ds(i, 1), :].rearrange("p o d -> p (o d)"), ps_z[:, 0, 0:D],
                                    ALU.add).then_inc(S["y_added"], 1)

                schedule(dve, prologue, norm, front_back, tile_front, tile_back, norm_inside=True)


SUBLAYERS[3] = cross_attention_1


def mamba(nc, A, X, XT, ident):
    INNER, STATE, CONV, RANK = 2 * D, 16, 4, 16
    CH = INNER // P
    N = TOKENS // 2
    NQ = N // 2
    DBL = RANK + 2 * STATE
    with Space(nc, "mamba") as top:
        H = top.sb("H", [P, KT, TOKENS])
        w_in = top.sb("w_in", [P, KT, 2 * INNER])
        w_x = top.sb("w_x", [P, CH, DBL])
        w_dt = top.sb("w_dt", [RANK, INNER])
        taps = top.sb("taps", [P, CH, CONV])
        cols = top.sb("cols", [P, 2, CH])
        a_log = top.sb("a_log", [P, CH, STATE])
        d = top.sb("d", [P, CH])
        decay = top.sb("decay", [P, CH, STATE])
        diag = top.sb("diag", [P, CH, P])
        w_out = top.sb("w_out", [P, CH, D])
        w_fc2 = top.sb("w_fc2", [P, KT, D])
        b_fc2 = top.sb("b_fc2", [1, D])
        ones = top.sb("ones", [1, P])
        loads = [(a_log[:, :, :], "L1_attn_A_log"), (d[:, :], "L1_attn_D"), (w_in[:, :, :], "L1_attn_in_proj_w"),
                 (w_x[:, :, :], "L1_attn_x_proj_w"), (w_dt[:, :], "L1_attn_dt_proj_w"), (taps[:, :, :], "L1_attn_conv_w"),
                 (cols[:, :, :], "mamba_cols"), (w_out[:, :, :], "L1_attn_out_proj_w"), (w_fc2[:, :, :], "L1_attn_fc2_w"),
                 (b_fc2[:, :], "L1_attn_fc2_b")]
        loaded = top.sem("loaded")
        with top.block() as block:

            @block.scalar
            def _(act):
                for to, name in loads:
                    act.dma_start(to, A[name]).then_inc(loaded, 16)

        project_queries(nc, A, XT, H, "mamba_fc1", A["L1_attn_fc1_w"], A["L1_attn_fc1_b"])
        with Space(nc, "mamba_set") as sp:
            exped, ones_set, done = (sp.sem(n) for n in ("exped", "ones_set", "done"))
            with sp.block() as block:

                @block.sync
                def _(sync):
                    sync.wait_ge(loaded, 16 * len(loads))

                @block.gpsimd
                def _(pool):
                    nc.gpsimd.memset(ones[:, :], 1.0).then_inc(ones_set, 1)

                @block.scalar
                def _(act):
                    act.wait_ge(loaded, 16 * len(loads))
                    nc.scalar.activation(a_log[:, :, :], a_log[:, :, :], ACT.Exp).then_inc(exped, 1)

                @block.vector
                def _(dve):
                    dve.wait_ge(loaded, 16 * len(loads))
                    for c in range(CH):
                        nc.vector.tensor_scalar(diag[:, c, :], ident[:, :], d[:, c:c + 1], None, ALU.mult).then_inc(done, 1)
                    dve.wait_ge(exped, 1)
                    nc.vector.tensor_scalar(decay[:, :, :], a_log[:, :, :], -1.0, None, ALU.mult).then_inc(done, 1)

        for half in range(2):
            with Space(nc, f"mamba{half}") as sp:
                u = sp.sb("u", [P, CH, N])
                dt = sp.sb("dt", [P, CH, N])
                dtu = sp.sb("dtu", [P, CH, N])
                gate = sp.sb("gate", [P, CH, N])
                x_dbl = sp.sb("x_dbl", [DBL, N])
                x_parts = sp.sb("x_parts", [DBL, 2, N], F32R)
                mamba_inputs(nc, (w_in, w_x, w_dt, taps, cols), H, half, u, dt, dtu, gate, x_dbl, x_parts, INNER, CONV, RANK, DBL, CH, N)
                mamba_scan(nc, half, ident, decay, diag, u, dt, dtu, gate, x_parts, STATE, RANK, DBL, CH, N, NQ)
                mamba_output(nc, half, X, gate, w_out, w_fc2, b_fc2, ones, CH, N)


def mamba_inputs(nc, weights, H, half, u, dt, dtu, gate, x_dbl, x_parts, INNER, CONV, RANK, DBL, CH, N):
    BS = 512
    with Space(nc, f"mamba{half}_in") as sp:
        w_in, w_x, w_dt, taps, cols = weights
        one = sp.sb("one", [P, 1])
        xc = sp.sb("xc", [P, CH, N])
        e = sp.sb("e", [P, CH, N])
        conv = e
        lg = sp.sb("lg", [P, CH, N])
        ps = [sp.ps(f"ps{k}", [P, N]) for k in range(4)]
        one_set, made, taken, tap_step, conv_ready, u_ready, exp_ready, log_ready, acc, step, x_high, dt_ready, acc_pool, rest_ready, rest_added = (
            sp.sem(n) for n in ("one_set", "made", "taken", "tap_step", "conv_ready", "u_ready", "exp_ready",
                                "log_ready", "acc", "step", "x_high", "dt_ready", "acc_pool", "rest_ready", "rest_added"))
        with sp.block() as block:

            @block.gpsimd
            def _(pool):
                nc.gpsimd.memset(one[:, :], 1.0).then_inc(one_set, 1)
                pool.wait_ge(x_high, 1)
                nc.gpsimd.tensor_tensor(x_parts[:, 1, :], x_dbl[:, :], x_parts[:, 0, :], ALU.subtract).then_inc(acc_pool, 1)
                for c in range(CH):
                    pool.wait_ge(rest_ready, c + 1)
                    nc.gpsimd.tensor_tensor(xc[:, c, :], dt[:, c, :], xc[:, c, :], ALU.add).then_inc(rest_added, 1)

            @block.tensor
            def _(pe):
                for g in range(3 * CH + 1):
                    if g >= 4:
                        pe.wait_ge(taken, g - 3)
                    if g == 2 * CH:
                        pe.wait_ge(u_ready, CH)
                    if g == 2 * CH + 1:
                        pe.wait_ge(taken, 2 * CH + 1)
                    for n in range(N // BS):
                        cut = slice(n * BS, (n + 1) * BS)
                        if g < 2 * CH:
                            for c in range(KT):
                                last = nc.tensor.matmul(ps[g % 4][:, cut], w_in[:, c, g * P:(g + 1) * P],
                                                        H[:, c, half * N + n * BS:half * N + (n + 1) * BS],
                                                        start=(c == 0), stop=(c == KT - 1))
                        elif g == 2 * CH:
                            for c in range(CH):
                                last = nc.tensor.matmul(ps[g % 4][0:DBL, cut], w_x[:, c, :], u[:, c, cut],
                                                        start=(c == 0), stop=(c == CH - 1))
                        else:
                            m = g - 2 * CH - 1
                            last = nc.tensor.matmul(ps[g % 4][:, cut], w_dt[:, m * P:(m + 1) * P], x_dbl[0:RANK, cut],
                                                    start=True, stop=True)
                    last.then_inc(made, 1)

            @block.scalar
            def _(act):
                act.wait_ge(one_set, 1)
                for g in range(CH):
                    act.wait_ge(made, g + 1)
                    nc.scalar.copy(xc[:, g, :], ps[g % 4][:, :]).then_inc(taken, 1)
                for g in range(CH, 2 * CH):
                    act.wait_ge(made, g + 1)
                    nc.scalar.activation(gate[:, g - CH, :], ps[g % 4][:, :], ACT.Silu).then_inc(taken, 1)
                    c = g - CH
                    act.wait_ge(conv_ready, c + 1)
                    nc.scalar.activation(u[:, c, :], conv[:, c, :], ACT.Silu, bias=cols[:, 0, c:c + 1]).then_inc(u_ready, 1)
                act.wait_ge(made, 2 * CH + 1)
                nc.scalar.copy(x_dbl[:, :], ps[2 * CH % 4][0:DBL, :]).then_inc(taken, 1)
                act.wait_ge(taken, 2 * CH + 1)
                nc.scalar.copy(x_parts[:, 0, :], x_dbl[:, :]).then_inc(x_high, 1)
                for c in range(CH):
                    g = 2 * CH + 1 + c
                    act.wait_ge(made, g + 1)
                    nc.scalar.activation(lg[:, c, :], ps[g % 4][:, :], ACT.Abs, bias=cols[:, 1, c:c + 1]).then_inc(acc, 1)
                    nc.scalar.activation(dt[:, c, :], ps[g % 4][:, :], ACT.Relu, bias=cols[:, 1, c:c + 1]).then_inc(taken, 1)
                for c in range(CH):
                    act.wait_ge(acc, c + 1)
                    nc.scalar.activation(e[:, c, :], lg[:, c, :], ACT.Exp, scale=-1.0).then_inc(exp_ready, 1)
                for c in range(CH):
                    act.wait_ge(exp_ready, c + 1)
                    nc.scalar.activation(lg[:, c, :], e[:, c, :], ACT.Ln, bias=one[:, 0:1]).then_inc(log_ready, 1)

            @block.vector
            def _(dve):
                chain = Chain(dve, tap_step)
                v = nc.vector
                seqs = lambda a: a.rearrange("p (b s) -> p b s", s=SEQ)
                for c in range(CH):
                    dve.wait_ge(taken, c + 1)
                    x, y = seqs(xc[:, c, :]), seqs(conv[:, c, :])
                    chain.link(v.tensor_scalar(y, x, taps[:, c, CONV - 1:CONV], None, ALU.mult))
                    for back in range(1, CONV):
                        last = v.scalar_tensor_tensor(y[:, :, back:], x[:, :, 0:SEQ - back], taps[:, c, CONV - 1 - back:CONV - back],
                                                      y[:, :, back:], ALU.mult, ALU.add)
                        if back < CONV - 1:
                            chain.link(last)
                    last.then_inc(conv_ready, 1)
                fix = Chain(dve, step)
                for c in range(CH):
                    dve.wait_ge(exp_ready, c + 1)
                    fix.link(v.tensor_scalar(xc[:, c, :], e[:, c, :], 1.0, 1.0, ALU.add, ALU.subtract))
                    dve.wait_ge(taken, 2 * CH + 2 + c)
                    v.tensor_tensor(xc[:, c, :], e[:, c, :], xc[:, c, :], ALU.subtract).then_inc(rest_ready, 1)
                for c in range(CH):
                    dve.wait_ge(log_ready, c + 1)
                    dve.wait_ge(rest_added, c + 1)
                    v.tensor_tensor(dt[:, c, :], lg[:, c, :], xc[:, c, :], ALU.add).then_inc(dt_ready, 1)
                for c in range(CH):
                    dve.wait_ge(dt_ready, c + 1)
                    v.tensor_tensor(dtu[:, c, :], dt[:, c, :], u[:, c, :], ALU.mult).then_inc(dt_ready, 1)


def mamba_scan(nc, half, ident, decay, diag, u, dt, dtu, gate, x_parts, STATE, RANK, DBL, CH, N, NQ):
    UN = 2 * CH
    with Space(nc, f"mamba{half}_scan") as sp:
        pick = [[sp.sb(f"pick{k}{s}", [DBL, P], F32R) for s in range(2)] for k in range(2)]
        b_all = [sp.sb(f"b_all{s}", [P, NQ]) for s in range(2)]
        dec = [sp.sb(f"dec{s}", [P, NQ]) for s in range(CH)]
        inp = [sp.sb(f"inp{s}", [P, NQ]) for s in range(CH)]
        h = [sp.sb(f"h{s}", [P, NQ]) for s in range(CH)]
        hc = [sp.sb(f"hc{s}", [P, NQ]) for s in range(CH)]
        ps_b = [sp.ps(f"ps_b{s}", [P, NQ]) for s in range(2)]
        ps_c = [sp.ps(f"ps_c{s}", [P, NQ]) for s in range(2)]
        ps_y = sp.ps("ps_y", [P, CH, NQ])
        picked, spread = ([sp.sem(f"{name}_{k}") for k in "bc"] for name in ("picked", "spread"))
        zeroed, b_copied, decayed, fed, scanned, weighed, summed, gated = (
            sp.sem(n) for n in ("zeroed", "b_copied", "decayed", "fed", "scanned", "weighed", "summed", "gated"))
        with sp.block() as block:

            @block.gpsimd
            def _(pool):
                for s in range(CH):
                    nc.gpsimd.memset(dec[s][:, :], 0.0).then_inc(zeroed, 1)
                pool.sem_inc(fed, 2 * CH)
                for q in range(2):
                    def front(n, i, s):
                        n = n + q * STATE
                        pool.wait_ge(b_copied, n + 3)
                        for c in range(CH):
                            pool.wait_ge(scanned, n * CH + (c + 1))
                            nc.gpsimd.tensor_tensor(inp[c][:, :], dtu[:, c, q * NQ:(q + 1) * NQ], b_all[s][:, :],
                                                    ALU.mult).then_inc(fed, 1)

                    pipelined(pool, STATE, front, nothing)

            @block.scalar
            def _(act):
                act.wait_ge(zeroed, CH)
                act.sem_inc(b_copied, 2)
                for q in range(2):
                    def copy_b(n, s):
                        g = n + q * STATE
                        act.wait_ge(spread[0], g + 3)
                        act.wait_ge(fed, g * CH + CH)
                        nc.scalar.copy(b_all[s][:, :], ps_b[s][:, :]).then_inc(b_copied, 1)

                    def choose(k, n, s):
                        act.wait_ge(spread[k], n + (q * STATE + 1))
                        nc.scalar.copy(pick[k][s][:, :], ident[0:DBL, bass.ds(n + (RANK + k * STATE), 1)].to_broadcast([DBL, P])
                                       ).then_inc(picked[k], 1)

                    def front(n, i, s):
                        choose(1, n, s)
                        if not (isinstance(n, int) and n == STATE - 1):
                            choose(0, n + 1, 1 - s)

                    choose(0, 0, 0)
                    copy_b(0, 0)

                    def back(n, i, s):
                        g = n + q * STATE
                        for c in range(CH):
                            if c == 2 and not (isinstance(n, int) and n == STATE - 1):
                                copy_b(i * 2 + (s + 1), (s + 1) % 2)
                            act.wait_ge(scanned, g * CH + (c + 1))
                            rows = dt[:, c, q * NQ:(q + 1) * NQ].rearrange("p (b s) -> p b s", s=SEQ)
                            nc.scalar.activation(dec[c][:, :].rearrange("p (b s) -> p b s", s=SEQ)[:, :, 1:], rows[:, :, 1:],
                                                 ACT.Exp, scale=decay[:, c, bass.ds(n, 1)]).then_inc(decayed, 1)

                    pipelined(act, STATE, front, back)

            @block.tensor
            def _(pe):
                for k in range(2):
                    pe.sem_inc(spread[k], 2)
                pe.sem_inc(summed, CH)
                for q in range(2):
                    def spread_row(k, n, s):
                        g = n + q * STATE
                        pe.wait_ge(picked[k], g + 1)
                        if k == 0:
                            pe.wait_ge(b_copied, g + 1)
                        else:
                            pe.wait_ge(weighed, g * CH + CH)
                        for part in range(2):
                            last = nc.tensor.matmul((ps_b, ps_c)[k][s][:, :], pick[k][s][:, :], x_parts[:, part, q * NQ:(q + 1) * NQ],
                                                    start=(part == 0), stop=(part == 1))
                        last.then_inc(spread[k], 1)

                    def front(n, i, s):
                        spread_row(1, n, s)
                        if not (isinstance(n, int) and n == STATE - 1):
                            spread_row(0, n + 1, 1 - s)

                    spread_row(0, 0, 0)
                    if q:
                        pe.wait_ge(gated, q * CH)
                    for c in range(CH):
                        nc.tensor.matmul(ps_y[:, c, :], diag[:, c, :], u[:, c, q * NQ:(q + 1) * NQ], start=True, stop=False,
                                         skip_group_check=True)

                    def back(n, i, s):
                        n = n + q * STATE
                        for c in range(CH):
                            pe.wait_ge(weighed, n * CH + (c + 1 + 2 * CH))
                            nc.tensor.matmul(ps_y[:, c, :], ident[:, :], hc[c][:, :], start=False, stop=False,
                                             skip_group_check=True).then_inc(summed, 1)

                    pipelined(pe, STATE, front, back)

            @block.vector
            def _(dve):
                dve.sem_inc(scanned, CH)
                dve.sem_inc(weighed, 2 * CH)
                for q in range(2):
                    def scan(t, i, k):
                        g = t + q * STATE * CH
                        dve.wait_ge(decayed, g + 1)
                        dve.wait_ge(fed, g + (1 + 2 * CH))
                        dve.wait_ge(weighed, g + (1 + CH))
                        nc.vector.tensor_tensor_scan(h[k % CH][:, :], dec[k % CH][:, :], inp[k % CH][:, :], 0.0, ALU.mult, ALU.add
                                                     ).then_inc(scanned, 1)

                    def weigh(t, i, k):
                        g = t + q * STATE * CH
                        dve.wait_ge(scanned, g + (CH + 1))
                        if k % CH == 0:
                            dve.wait_ge(spread[1], i * 2 + (k // CH + q * STATE + 3))
                        dve.wait_ge(summed, g + 1)
                        nc.vector.tensor_tensor(hc[k % CH][:, :], h[k % CH][:, :], ps_c[k // CH][:, :], ALU.mult).then_inc(weighed, 1)

                    pipelined(dve, STATE * CH, scan, weigh, UN)
                    dve.wait_ge(summed, (q + 1) * STATE * CH + CH)
                    for c in range(CH):
                        out = gate[:, c, q * NQ:(q + 1) * NQ]
                        nc.vector.tensor_tensor(out, out, ps_y[:, c, :], ALU.mult).then_inc(gated, 1)


def mamba_output(nc, half, X, gated, w_out, w_fc2, b_fc2, ones, CH, N):
    BS = 512
    with Space(nc, f"mamba{half}_out") as sp:
        mid = sp.sb("mid", [P, KT, N])
        ps_m = [sp.ps(f"ps_m{s}", [P, KT, BS]) for s in range(2)]
        ps_y = [sp.ps(f"ps_y{s}", [P, BANK]) for s in range(2)]
        made, copied, y_made, added = (sp.sem(n) for n in ("made", "copied", "y_made", "added"))
        with sp.block() as block:

            @block.tensor
            def _(pe):
                for n in range(N // BS):
                    for m in range(KT):
                        for c in range(CH):
                            last = nc.tensor.matmul(ps_m[n][:, m, :], w_out[:, c, m * P:(m + 1) * P],
                                                    gated[:, c, n * BS:(n + 1) * BS], start=(c == 0), stop=(c == CH - 1))
                    last.then_inc(made, 1)
                for t in range(N // P):
                    pe.wait_ge(copied, t * P // BS + 1)
                    if t >= 2:
                        pe.wait_ge(added, t - 1)
                    nc.tensor.matmul(ps_y[t % 2][:, 0:D], ones[:, :], b_fc2[:, :], start=True, stop=False)
                    for c in range(KT):
                        last = nc.tensor.matmul(ps_y[t % 2][:, 0:D], mid[:, c, t * P:(t + 1) * P], w_fc2[:, c, :],
                                                start=False, stop=(c == KT - 1))
                    last.then_inc(y_made, 1)

            @block.scalar
            def _(act):
                for n in range(N // BS):
                    act.wait_ge(made, n + 1)
                    nc.scalar.copy(mid[:, :, n * BS:(n + 1) * BS], ps_m[n][:, :, :]).then_inc(copied, 1)

            @block.vector
            def _(dve):
                for t in range(N // P):
                    tile = half * (N // P) + t
                    dve.wait_ge(y_made, t + 1)
                    nc.vector.tensor_tensor(X[:, tile, :], X[:, tile, :], ps_y[t % 2][:, 0:D], ALU.add).then_inc(added, 1)


SUBLAYERS[4] = mamba


def _by_partition(w):
    return w.reshape(-1, 128, w.shape[-1]).transpose(1, 0, 2)


def _expert_layout(w_gate, w_up, w_down, fp):
    e, f, d = w_gate.shape
    gu = np.concatenate([w_gate, w_up], axis=1).transpose(0, 2, 1).reshape(e, d // 128, 128, 2 * f).transpose(0, 2, 1, 3)
    dn = w_down.transpose(0, 2, 1).reshape(e, f // fp, fp, d).transpose(0, 2, 1, 3)
    return gu, dn


def _alibi():
    head = np.arange(HPG)[:, None, None, None] + HPG * np.arange(GROUPS)[None, None, :, None]
    query, key = np.arange(SEQ)[None, :, None, None], np.arange(SEQ)[None, None, None, :]
    slope = (1.0 / (2.0 ** 8) ** ((head + 1) / HEADS)).astype(np.float32)
    bias = np.where(key <= query, slope * (key - query).astype(np.float32), np.float32(NEG))
    return bias.astype(np.float32).reshape(P, GROUPS, SEQ)


def _own(width, value):
    return (np.arange(P)[:, None] // width == np.arange(P // width)).astype(np.float32) * np.float32(value)


def _lay_out(v):
    a = {"x": v["x"]}
    a["alibi"] = _alibi()
    a["own16"] = _own(16, 1 / 16)
    a["own4"] = _own(16, 1 / 4)
    ctx_t = v["ctx_1024"].transpose(0, 2, 1).reshape(BATCH, KT, P, CTX).transpose(0, 2, 1, 3)
    a["ctx_t"], a["ctx_ends"] = ctx_t, ctx_t[:, :, :, -1].transpose(1, 2, 0)
    for n in ("Wq", "Wo"):
        a[f"L0_xattn_{n}"] = _by_partition(v[f"L0_xattn_{n}"])
    a["L0_xattn_Wkv"] = _by_partition(np.concatenate([v["L0_xattn_Wk"], v["L0_xattn_Wv"]], axis=1))
    for n in ("b_q", "b_k", "b_v"):
        a[f"L0_xattn_{n}"] = v[f"L0_xattn_{n}"].reshape(KT, P).T
    a["L0_xattn_b_o"] = v["L0_xattn_b_o"].reshape(1, D)
    a["ctx"] = v["ctx_1024"]
    latent, context = (np.stack([v[f"L1_xattn_{n}_g"], v[f"L1_xattn_{n}_b"]]) for n in ("ln2", "ln1"))
    a["affine"] = np.broadcast_to(np.concatenate([latent, context]), (P, 4, D))
    a["ctx_affine"] = np.broadcast_to(context[:, None, :], (P, 2, 2, D))
    a["L1_xattn_Wq"], a["L1_xattn_Wo"] = _by_partition(v["L1_xattn_Wq"]), _by_partition(v["L1_xattn_Wo"])
    a["L1_xattn_WkT"] = _by_partition(v["L1_xattn_Wkv"][:, :1024].T)
    a["L1_xattn_Wv"] = _by_partition(v["L1_xattn_Wkv"][:, 1024:])
    for n in ("fc1", "in_proj", "x_proj", "out_proj", "fc2"):
        a[f"L1_attn_{n}_w"] = _by_partition(v[f"L1_attn_{n}_w"].T)
    a["L1_attn_dt_proj_w"] = v["L1_attn_dt_proj_w"].T
    a["L1_attn_fc1_b"], a["L1_attn_D"] = v["L1_attn_fc1_b"].reshape(-1, P).T, v["L1_attn_D"].reshape(-1, P).T
    a["L1_attn_fc2_b"] = v["L1_attn_fc2_b"].reshape(1, D)
    a["L1_attn_A_log"], a["L1_attn_conv_w"] = _by_partition(v["L1_attn_A_log"]), _by_partition(v["L1_attn_conv_w"])
    a["mamba_cols"] = np.stack([v["L1_attn_conv_b"].reshape(-1, P).T, v["L1_attn_dt_proj_b"].reshape(-1, P).T], axis=1)
    slot = np.arange(P, dtype=np.float32)
    a["codes"] = np.broadcast_to(HALF - np.arange(HALF, dtype=np.float32), (P, HALF))
    ends = [np.full(P, HALF), np.full(P, 2 * HALF), np.where(slot < REST, HALF, 2 * HALF)]
    a["slot_base"] = np.stack([e - TOKENS - slot for e in ends] + [TOKENS + slot], axis=1).astype(np.float32)
    a["L0_attn_w"] = _by_partition(v["L0_attn_W_kqv"].T)
    a["L0_ffn_gate_w"] = _by_partition(v["L0_ffn_gate_w"].T)
    a["L0_ffn_up"], a["L0_ffn_down"] = _expert_layout(v["L0_ffn_w_gate"], v["L0_ffn_w_up"], v["L0_ffn_w_down"], 96)
    a["L1_ffn_gate_w"] = _by_partition(v["L1_ffn_gate_w"].T)
    a["L1_ffn_up"], a["L1_ffn_down"] = _expert_layout(
        np.concatenate([v["L1_ffn_w1"], v["L1_ffn_sw1"][None]]), np.concatenate([v["L1_ffn_w3"], v["L1_ffn_sw3"][None]]),
        np.concatenate([v["L1_ffn_w2"], v["L1_ffn_sw2"][None]]), 128)
    return a


def kernel(**inputs):
    import concourse.bacc as bacc
    from concourse.bass_utils import run_bass_kernel_spmd

    arrays = {n: np.ascontiguousarray(a) for n, a in _lay_out({n: np.asarray(a) for n, a in inputs.items()}).items()}
    nc = bacc.Bacc("TRN2", target_bir_lowering=False, num_devices=1)
    aps = {n: nc.dram_tensor(f"in_{n}", a.shape, mybir.dt.from_np(a.dtype), kind="ExternalInput").ap() for n, a in arrays.items()}
    out = nc.dram_tensor("out", (BATCH, SEQ, D), F32, kind="ExternalOutput").ap()
    build_program(nc, aps, out)
    result = run_bass_kernel_spmd(nc, [{f"in_{n}": a for n, a in arrays.items()}], core_ids=[0])
    return result.results[0]["out"]
```
